# Optimizing a Trainium2 kernel written in Bass

```python
import numpy as np
import jax
import jax.numpy as jnp

def _softmax(x, axis=-1):
    return jax.nn.softmax(x, axis=axis)

def _gelu(x):
    return jax.nn.gelu(x, approximate=True)

def _silu(x):
    return jax.nn.silu(x)

def _sigmoid(x):
    return jax.nn.sigmoid(x)

def _layernorm(x, axis=-1, eps=1e-05):
    m = jnp.mean(x, axis=axis, keepdims=True)
    v = jnp.var(x, axis=axis, keepdims=True)
    return (x - m) / jnp.sqrt(v + eps)

def _scatter_add(tgt, idx, src, axis=0):
    return tgt.at[idx].add(src)

def _segment_sum(src, seg, n):
    return jax.ops.segment_sum(src, seg, n)
kernel_name = 'mk_sandwich_d1_jaxref_r8_fc14f4'

def setup_inputs(seed: int=0):
    np.random.seed(seed)
    _w = jnp.asarray

    def _L0_attn_setup():
        import jax, jax.numpy as jnp
        import numpy as np
        D_MODEL = 512
        D_XB = 128
        D_INNER = 512
        HEADDIM = 128
        DSTATE = 128
        NHEADS = D_INNER // HEADDIM
        DCONV = 4
        INTER = 1792
        EPS = 1e-05
        CHUNK = 128

        def rmsnorm(x, w):
            return x * jax.lax.rsqrt(jnp.mean(x * x, axis=-1, keepdims=True) + EPS) * w

        def silu(x):
            return x * jax.nn.sigmoid(x)

        def mamba2(x, w_in, conv_w, conv_b, A_log, D, dt_bias, w_out):
            B, L, _ = x.shape
            H, P, N = (NHEADS, HEADDIM, DSTATE)
            G = D_XB // P
            rep = H // G
            zxbcdt = x @ w_in.T
            z, xs, Bs, Cs, dt = jnp.split(zxbcdt, [D_INNER, D_INNER + D_XB, D_INNER + 2 * D_XB, 2 * D_INNER + 2 * D_XB], axis=-1)
            xBC = jnp.concatenate([xs, Bs, Cs], axis=-1)
            conv = jax.lax.conv_general_dilated(xBC.transpose(0, 2, 1), conv_w[:, None, :], (1,), [(DCONV - 1, 0)], feature_group_count=conv_w.shape[0])
            xBC = silu(conv.transpose(0, 2, 1) + conv_b)
            xs, Bs, Cs = jnp.split(xBC, [D_XB, 2 * D_XB], axis=-1)
            dt = jax.nn.softplus(dt + dt_bias)
            A = -jnp.exp(A_log)
            xh = jnp.repeat(xs.reshape(B, L, G, P), rep, axis=2)
            Bh = jnp.repeat(Bs.reshape(B, L, G, N), rep, axis=2)
            Ch = Cs.reshape(B, L, H, N)
            c, Q = (L // CHUNK, CHUNK)
            a = (dt * A).reshape(B, c, Q, H).transpose(0, 1, 3, 2)
            dtc = dt.reshape(B, c, Q, H).transpose(0, 1, 3, 2)
            Xc = xh.reshape(B, c, Q, H, P).transpose(0, 1, 3, 2, 4)
            Bc = Bh.reshape(B, c, Q, H, N).transpose(0, 1, 3, 2, 4)
            Cc = Ch.reshape(B, c, Q, H, N).transpose(0, 1, 3, 2, 4)
            cs = jnp.cumsum(a, axis=-1)
            tri = jnp.tril(jnp.ones((Q, Q), bool))
            Ldec = jnp.where(tri, jnp.exp(cs[..., :, None] - cs[..., None, :]), 0.0)
            Xdt = Xc * dtc[..., None]
            att = jnp.einsum('bchqn,bchkn->bchqk', Cc, Bc) * Ldec
            Yd = jnp.einsum('bchqk,bchkp->bchqp', att, Xdt)
            dec_end = jnp.exp(cs[..., -1:] - cs)
            states = jnp.einsum('bchq,bchqn,bchqp->bchpn', dec_end, Bc, Xdt)
            g = jnp.exp(cs[..., -1])

            def step(S, inp):
                gk, st = inp
                return (gk[:, :, None, None] * S + st, S)
            S0 = jnp.zeros((B, H, P, N), x.dtype)
            _, prev = jax.lax.scan(step, S0, (g.transpose(1, 0, 2), states.transpose(1, 0, 2, 3, 4)))
            prev = prev.transpose(1, 0, 2, 3, 4)
            Yo = jnp.einsum('bchqn,bchpn,bchq->bchqp', Cc, prev, jnp.exp(cs))
            Y = (Yd + Yo).transpose(0, 1, 3, 2, 4).reshape(B, L, H, P)
            Y = Y + D[:, None] * xh
            y = Y.reshape(B, L, D_INNER) * silu(z)
            return y @ w_out.T
        key = jax.random.key(seed)
        ks = jax.random.split(key, 10)
        B, L = (2, 256)
        proj_out = 2 * D_INNER + 2 * D_XB + NHEADS
        conv_dim = 2 * D_XB + D_INNER
        return {'hidden_states': jax.random.normal(ks[0], (B, L, D_MODEL), jnp.float32), 'w_in': jax.random.normal(ks[1], (proj_out, D_MODEL), jnp.float32) * 0.02, 'conv_w': jax.random.normal(ks[2], (conv_dim, DCONV), jnp.float32) * 0.1, 'conv_b': jnp.zeros((conv_dim,), jnp.float32), 'A_log': jnp.log(jnp.arange(1, NHEADS + 1, dtype=jnp.float32)), 'D': jnp.ones((NHEADS,), jnp.float32), 'dt_bias': jax.random.normal(ks[3], (NHEADS,), jnp.float32) * 0.1, 'w_out': jax.random.normal(ks[4], (D_MODEL, D_INNER), jnp.float32) * 0.02, 'ln1_w': jnp.ones((D_MODEL,), jnp.float32), 'ln2_w': jnp.ones((D_MODEL,), jnp.float32), 'gate_w': jax.random.normal(ks[5], (INTER, D_MODEL), jnp.float32) * 0.02, 'up_w': jax.random.normal(ks[6], (INTER, D_MODEL), jnp.float32) * 0.02, 'down_w': jax.random.normal(ks[7], (D_MODEL, INTER), jnp.float32) * 0.02}
    _L0_attn_in = _L0_attn_setup()

    def _L0_ffn_setup():
        import jax, jax.numpy as jnp
        import numpy as np
        N_STREAMS = 4
        DIM = 128
        SINKHORN_ITERS = 50
        SINKHORN_TAU = 0.1
        RMS_EPS = 1.1920929e-07

        def sinkhorn_log(logits, num_iters=SINKHORN_ITERS, tau=SINKHORN_TAU):
            Z = logits / tau
            u0 = jnp.zeros(Z.shape[:-1], Z.dtype)
            v0 = jnp.zeros_like(u0)

            def step(carry, _):
                u, v = carry
                u = -jax.nn.logsumexp(Z + v[..., None, :], axis=-1)
                v = -jax.nn.logsumexp(Z + u[..., :, None], axis=-2)
                return ((u, v), None)
            (u, v), _ = jax.lax.scan(step, (u0, v0), None, length=num_iters)
            return jnp.exp(Z + u[..., :, None] + v[..., None, :])
        key = jax.random.key(seed)
        ks = jax.random.split(key, 6)
        B, T = (4, 256)
        n, C = (N_STREAMS, DIM)
        wd = n * C
        x = jax.random.normal(ks[0], (B, T, wd), dtype=jnp.float32)
        W_res = 0.01 * jax.random.normal(ks[1], (n * n, wd), dtype=jnp.float32)
        W_pre = 0.01 * jax.random.normal(ks[2], (n, wd), dtype=jnp.float32)
        W_post = 0.01 * jax.random.normal(ks[3], (n, wd), dtype=jnp.float32)
        H_res_base = jnp.full((n, n), -0.5, dtype=jnp.float32)
        H_res_base = H_res_base.at[jnp.arange(n), jnp.arange(n)].set(0.0)
        H_pre_base = jnp.zeros((n,), dtype=jnp.float32).at[0].set(1.0)
        H_post_base = jnp.zeros((n,), dtype=jnp.float32)
        gate = jnp.array([5.0], dtype=jnp.float32)
        W_branch = 1.0 / np.sqrt(C) * jax.random.normal(ks[4], (C, C), dtype=jnp.float32)
        return {'x': x, 'W_res': W_res, 'W_pre': W_pre, 'W_post': W_post, 'H_res_base': H_res_base, 'H_pre_base': H_pre_base, 'H_post_base': H_post_base, 'gate': gate, 'W_branch': W_branch}
    _L0_ffn_in = _L0_ffn_setup()
    _d = {'L0_attn_hidden_states': _L0_attn_in['hidden_states'], 'L0_attn_w_in': _L0_attn_in['w_in'], 'L0_attn_conv_w': _L0_attn_in['conv_w'], 'L0_attn_conv_b': _L0_attn_in['conv_b'], 'L0_attn_A_log': _L0_attn_in['A_log'], 'L0_attn_D': _L0_attn_in['D'], 'L0_attn_dt_bias': _L0_attn_in['dt_bias'], 'L0_attn_w_out': _L0_attn_in['w_out'], 'L0_attn_ln1_w': _L0_attn_in['ln1_w'], 'L0_attn_ln2_w': _L0_attn_in['ln2_w'], 'L0_attn_gate_w': _L0_attn_in['gate_w'], 'L0_attn_up_w': _L0_attn_in['up_w'], 'L0_attn_down_w': _L0_attn_in['down_w'], 'L0_ffn_W_res': _L0_ffn_in['W_res'], 'L0_ffn_W_pre': _L0_ffn_in['W_pre'], 'L0_ffn_W_post': _L0_ffn_in['W_post'], 'L0_ffn_H_res_base': _L0_ffn_in['H_res_base'], 'L0_ffn_H_pre_base': _L0_ffn_in['H_pre_base'], 'L0_ffn_H_post_base': _L0_ffn_in['H_post_base'], 'L0_ffn_gate': _L0_ffn_in['gate'], 'L0_ffn_W_branch': _L0_ffn_in['W_branch']}
    _x0 = _d['L0_attn_hidden_states']
    _d['L0_attn_hidden_states'] = jax.random.normal(jax.random.fold_in(jax.random.key(seed), 1), (2, 1024, 512), dtype=_x0.dtype)
    del _x0
    return _d

def reference(L0_attn_hidden_states, L0_attn_w_in, L0_attn_conv_w, L0_attn_conv_b, L0_attn_A_log, L0_attn_D, L0_attn_dt_bias, L0_attn_w_out, L0_attn_ln1_w, L0_attn_ln2_w, L0_attn_gate_w, L0_attn_up_w, L0_attn_down_w, L0_ffn_W_res, L0_ffn_W_pre, L0_ffn_W_post, L0_ffn_H_res_base, L0_ffn_H_pre_base, L0_ffn_H_post_base, L0_ffn_gate, L0_ffn_W_branch):

    def _L0_attn_ref(hidden_states, w_in, conv_w, conv_b, A_log, D, dt_bias, w_out, ln1_w, ln2_w, gate_w, up_w, down_w):
        import jax, jax.numpy as jnp
        import numpy as np
        D_MODEL = 512
        D_XB = 128
        D_INNER = 512
        HEADDIM = 128
        DSTATE = 128
        NHEADS = D_INNER // HEADDIM
        DCONV = 4
        INTER = 1792
        EPS = 1e-05
        CHUNK = 128

        def rmsnorm(x, w):
            return x * jax.lax.rsqrt(jnp.mean(x * x, axis=-1, keepdims=True) + EPS) * w

        def silu(x):
            return x * jax.nn.sigmoid(x)

        def mamba2(x, w_in, conv_w, conv_b, A_log, D, dt_bias, w_out):
            B, L, _ = x.shape
            H, P, N = (NHEADS, HEADDIM, DSTATE)
            G = D_XB // P
            rep = H // G
            zxbcdt = x @ w_in.T
            z, xs, Bs, Cs, dt = jnp.split(zxbcdt, [D_INNER, D_INNER + D_XB, D_INNER + 2 * D_XB, 2 * D_INNER + 2 * D_XB], axis=-1)
            xBC = jnp.concatenate([xs, Bs, Cs], axis=-1)
            conv = jax.lax.conv_general_dilated(xBC.transpose(0, 2, 1), conv_w[:, None, :], (1,), [(DCONV - 1, 0)], feature_group_count=conv_w.shape[0])
            xBC = silu(conv.transpose(0, 2, 1) + conv_b)
            xs, Bs, Cs = jnp.split(xBC, [D_XB, 2 * D_XB], axis=-1)
            dt = jax.nn.softplus(dt + dt_bias)
            A = -jnp.exp(A_log)
            xh = jnp.repeat(xs.reshape(B, L, G, P), rep, axis=2)
            Bh = jnp.repeat(Bs.reshape(B, L, G, N), rep, axis=2)
            Ch = Cs.reshape(B, L, H, N)
            c, Q = (L // CHUNK, CHUNK)
            a = (dt * A).reshape(B, c, Q, H).transpose(0, 1, 3, 2)
            dtc = dt.reshape(B, c, Q, H).transpose(0, 1, 3, 2)
            Xc = xh.reshape(B, c, Q, H, P).transpose(0, 1, 3, 2, 4)
            Bc = Bh.reshape(B, c, Q, H, N).transpose(0, 1, 3, 2, 4)
            Cc = Ch.reshape(B, c, Q, H, N).transpose(0, 1, 3, 2, 4)
            cs = jnp.cumsum(a, axis=-1)
            tri = jnp.tril(jnp.ones((Q, Q), bool))
            Ldec = jnp.where(tri, jnp.exp(cs[..., :, None] - cs[..., None, :]), 0.0)
            Xdt = Xc * dtc[..., None]
            att = jnp.einsum('bchqn,bchkn->bchqk', Cc, Bc) * Ldec
            Yd = jnp.einsum('bchqk,bchkp->bchqp', att, Xdt)
            dec_end = jnp.exp(cs[..., -1:] - cs)
            states = jnp.einsum('bchq,bchqn,bchqp->bchpn', dec_end, Bc, Xdt)
            g = jnp.exp(cs[..., -1])

            def step(S, inp):
                gk, st = inp
                return (gk[:, :, None, None] * S + st, S)
            S0 = jnp.zeros((B, H, P, N), x.dtype)
            _, prev = jax.lax.scan(step, S0, (g.transpose(1, 0, 2), states.transpose(1, 0, 2, 3, 4)))
            prev = prev.transpose(1, 0, 2, 3, 4)
            Yo = jnp.einsum('bchqn,bchpn,bchq->bchqp', Cc, prev, jnp.exp(cs))
            Y = (Yd + Yo).transpose(0, 1, 3, 2, 4).reshape(B, L, H, P)
            Y = Y + D[:, None] * xh
            y = Y.reshape(B, L, D_INNER) * silu(z)
            return y @ w_out.T
        res = hidden_states
        h = rmsnorm(hidden_states, ln1_w)
        h = res + mamba2(h, w_in, conv_w, conv_b, A_log, D, dt_bias, w_out)
        res = h
        h2 = rmsnorm(h, ln2_w)
        mlp = silu(h2 @ gate_w.T) * (h2 @ up_w.T) @ down_w.T
        return res + mlp

    def _L0_ffn_ref(x, W_res, W_pre, W_post, H_res_base, H_pre_base, H_post_base, gate, W_branch):
        import jax, jax.numpy as jnp
        import numpy as np
        N_STREAMS = 4
        DIM = 128
        SINKHORN_ITERS = 50
        SINKHORN_TAU = 0.1
        RMS_EPS = 1.1920929e-07

        def sinkhorn_log(logits, num_iters=SINKHORN_ITERS, tau=SINKHORN_TAU):
            Z = logits / tau
            u0 = jnp.zeros(Z.shape[:-1], Z.dtype)
            v0 = jnp.zeros_like(u0)

            def step(carry, _):
                u, v = carry
                u = -jax.nn.logsumexp(Z + v[..., None, :], axis=-1)
                v = -jax.nn.logsumexp(Z + u[..., :, None], axis=-2)
                return ((u, v), None)
            (u, v), _ = jax.lax.scan(step, (u0, v0), None, length=num_iters)
            return jnp.exp(Z + u[..., :, None] + v[..., None, :])
        B, T, nC = x.shape
        n = N_STREAMS
        C = nC // n
        x_norm = x * jax.lax.rsqrt(jnp.mean(x * x, axis=-1, keepdims=True) + RMS_EPS)
        H_res_logits = (x_norm @ W_res.T).reshape(B, T, n, n) + H_res_base
        H_pre_logits = x_norm @ W_pre.T + H_pre_base
        H_post_logits = x_norm @ W_post.T + H_post_base
        H_res = sinkhorn_log(H_res_logits)
        H_pre = jax.nn.softmax(H_pre_logits, axis=-1)
        H_post = jax.nn.softmax(H_post_logits, axis=-1)
        g = jax.nn.sigmoid(gate)[0]
        I = jnp.eye(n, dtype=H_res.dtype)
        H_res = (1.0 - g) * I + g * H_res
        x_streams = x.reshape(B, T, n, C)
        x_pre = jnp.einsum('btnc,btn->btc', x_streams, H_pre)
        y = x_pre @ W_branch
        x_mixed = jnp.einsum('btij,btjc->btic', H_res, x_streams)
        y_distributed = jnp.einsum('btc,btn->btnc', y, H_post)
        return (x_mixed + y_distributed).reshape(B, T, nC)
    x = L0_attn_hidden_states
    x = x + _layernorm(_L0_attn_ref(_layernorm(x, axis=-1), L0_attn_w_in, L0_attn_conv_w, L0_attn_conv_b, L0_attn_A_log, L0_attn_D, L0_attn_dt_bias, L0_attn_w_out, L0_attn_ln1_w, L0_attn_ln2_w, L0_attn_gate_w, L0_attn_up_w, L0_attn_down_w), axis=-1)
    x = x + _layernorm(_L0_ffn_ref(_layernorm(x, axis=-1), L0_ffn_W_res, L0_ffn_W_pre, L0_ffn_W_post, L0_ffn_H_res_base, L0_ffn_H_pre_base, L0_ffn_H_post_base, L0_ffn_gate, L0_ffn_W_branch), axis=-1)
    return x

_drawn_inputs = setup_inputs


def setup_inputs(seed=0):
    import zlib

    import numpy as np

    out = dict(_drawn_inputs(seed))
    spreads = {'L0_attn_conv_b': (0.0, 0.8),
     'L0_attn_D': (1.0, 0.6),
     'L0_attn_ln1_w': (1.0, 0.6),
     'L0_attn_ln2_w': (1.0, 0.6),
     'L0_ffn_H_post_base': (0.0, 0.8)}
    factors = {'L0_attn_w_in': 8.0,
     'L0_attn_conv_w': 8.0,
     'L0_attn_A_log': 8.0,
     'L0_attn_dt_bias': 8.0,
     'L0_attn_w_out': 8.0,
     'L0_ffn_W_pre': 6.084,
     'L0_ffn_W_post': 5.684,
     'L0_attn_gate_w': 64.0,
     'L0_attn_up_w': 64.0,
     'L0_attn_down_w': 64.0}
    for name, (base, spread) in spreads.items():
        noise = np.random.default_rng([zlib.crc32(name.encode()), seed]).standard_normal(out[name].shape)
        drawn = base * np.exp(spread * noise) if base else spread * noise
        out[name] = jnp.asarray(drawn.astype(out[name].dtype))
    for name, factor in factors.items():
        out[name] = (out[name] * factor).astype(out[name].dtype)
    return out
```

```python
from contextlib import ExitStack

import concourse.bass as bass
from concourse import mybir

F32 = mybir.dt.float32
F32R = mybir.dt.float32r
ACT = mybir.ActivationFunctionType
ALU = mybir.AluOpType
AX = mybir.AxisListType

P = 128
D = 512
KD = D // P
H = 4
INTER = 1792
NJ = INTER // P
TOK = 2048
BATCHES = 2
TA = 256
CA = TA // P
NA = TOK // TA
TB = 512
CB = TB // P
NB = TOK // TB
NXBC = 6
TAPS = 4
HALO = TAPS - 1
NPAIR = 5
NLOG = 24
SINK = 50
EPS = 1e-5
EPS_MHC = 1.1920929e-07
MASKED = -1.0e30
SHIFT = 80.0
SCALE_UP = 5.5406223843935098e34
LN1P_TERMS = 8


SU_G = 14
SU_V = 4
CSTEPS = 2 * CB + (2 * CB + 4) + 6 + 3 * (2 * SINK - 1) + 1 + CB * (3 + 16 + 4 + 1)


def at_tile(ap, m):
    if isinstance(m, int):
        return ap[m]
    names = " ".join("bcde"[:len(ap.shape) - 2])
    return ap[bass.ds(m, 1)].rearrange(f"a p {names} -> (a p) {names}") if len(ap.shape) == 3 else \
        ap[bass.ds(m, 1)].squeeze(0)


class Steps:

    def __init__(self, eng, sem, per_tile):
        self.eng, self.sem, self.per_tile, self.k, self.m = eng, sem, per_tile, 0, 0

    def begin(self, m):
        self.m, self.k = m, 0

    def done(self, ins):
        ins.then_inc(self.sem, 1)
        self.k += 1

    def wait(self, back=0):
        self.eng.wait_ge(self.sem, self.m * self.per_tile + (self.k - back))

    def end(self):
        assert self.k == self.per_tile, (self.k, self.per_tile)


def heads(ap):
    return ap.rearrange("p (h q) -> p h q", h=H)


def mamba_mlp_mhc(nc, x, w_in, w_dt, conv_w, conv_b, w_out, gate_w, up_w, down_w, ln_w,
                  rows, w_logit, w_branch, out):
    DT = 18
    h_scr = nc.dram_tensor("h_scr", (NA, P, CA, D), F32, kind="Internal").ap()
    h2t_scr = nc.dram_tensor("h2t_scr", (NA, P, KD, TA), F32, kind="Internal").ap()
    x_a = x.rearrange("(m t p) d -> m p t d", t=CA, p=P)
    x_b = x.rearrange("(m t p) d -> m p t d", t=CB, p=P)
    out_b = out.rearrange("(m t p) d -> m p t d", t=CB, p=P)
    h_scr_b = h_scr.rearrange("(m u) p t d -> m u p t d", u=2)
    h2t_scr_b = h2t_scr.rearrange("(m u) p k q -> m u p k q", u=2)

    with ExitStack() as whole:
        def sem(name):
            return whole.enter_context(nc.semaphore(name))

        def sb(stack, name, shape, dt=F32):
            return stack.enter_context(nc.sbuf_tensor(name, shape, dt))

        ident = sb(whole, "ident", [P, P])
        rows_sb = sb(whole, "rows_sb", [P, 64])
        NR = rows.shape[1]
        ln_sb = sb(whole, "ln_sb", [P, 2 * KD])
        halfc = sb(whole, "halfc", [P, CB])
        idle = sb(whole, "idle", [P, 1])
        epsc = sb(whole, "epsc", [P, CB])
        epsm = sb(whole, "epsm", [P, CB])
        gate_hi = sb(whole, "gate_hi", [P, NJ, KD * P], F32R)
        gate_lo = sb(whole, "gate_lo", [P, NJ, KD * P], F32R)
        banks = [whole.enter_context(nc.psum_tensor(f"bank{i}", [P, 512], F32)) for i in range(8)]

        with ExitStack() as st:
            tri = sb(st, "tri", [P, P])
            negmask = sb(st, "negmask", [P, P])
            ones = sb(st, "ones", [P, P])
            keep = sb(st, "keep", [P, NA + 1])
            w_raw = sb(st, "w_raw", [P, 2, 4 * P])
            win_hi = sb(st, "win_hi", [P, KD, 2 * NPAIR * P], F32R)
            win_lo = sb(st, "win_lo", [P, KD, 2 * NPAIR * P], F32R)
            wdt_raw = sb(st, "wdt_raw", [P, KD, H])
            wdt_hi = sb(st, "wdt_hi", [P, KD, H], F32R)
            wdt_lo = sb(st, "wdt_lo", [P, KD, H], F32R)
            wout_sb = sb(st, "wout_sb", [P, H, D])
            convw_sb = sb(st, "convw_sb", [P, NXBC, TAPS])
            convb_sb = sb(st, "convb_sb", [P, NXBC])
            a_rate = sb(st, "a_rate", [P, 2 * H])
            x_t = sb(st, "x_t", [P, 2, CA, D])
            h0 = sb(st, "h0", [P, 2, CA, D])
            u = sb(st, "u", [P, CA, D])
            u_hi = sb(st, "u_hi", [P, KD, TA], F32R)
            u_lo = sb(st, "u_lo", [P, KD, TA], F32R)
            xraw = sb(st, "xraw", [P, NXBC, HALO + TA])
            xbc = sb(st, "xbc", [P, 2, NXBC, TA])
            xbc_tanh = sb(st, "xbc_tanh", [P, NXBC * TA])
            z_tanh = sb(st, "z_tanh", [P, 2, 2 * TA])
            zs = sb(st, "zs", [P, 2, H, TA])
            decay = sb(st, "decay", [P, 512])
            ecs = sb(st, "ecs", [P, 512])
            c_dec = sb(st, "c_dec", [P, 512])
            xw = sb(st, "xw", [P, 512])
            xb_tok = sb(st, "xb_tok", [P, 2 * P + H])
            state = sb(st, "state", [P, 512])
            atri = sb(st, "atri", [P, 512])
            y = sb(st, "y", [P, 512])
            h = sb(st, "h", [P, CA, D])
            h2 = sb(st, "h2", [P, CA, D])
            h2t = sb(st, "h2t", [P, KD, TA])
            st6 = sb(st, "st6", [P, CA, 6])
            mom = sb(st, "mom", [P, CA, 2])
            ve = sb(st, "ve", [P, CA])
            rstd = sb(st, "rstd", [P, CA])
            qv = sb(st, "qv", [P, CA])
            rr = sb(st, "rr", [P, CA])
            ss = sb(st, "ss", [P, CA])
            msq = sb(st, "msq", [P, CA])
            rh = sb(st, "rh", [P, CA])
            pre = sb(st, "pre", [P, 2 * H])
            nabs = sb(st, "nabs", [P, 2 * H])
            e1 = sb(st, "e1", [P, 2 * H])
            s1 = sb(st, "s1", [P, 2 * H])
            s2 = sb(st, "s2", [P, 2 * H])
            acc = sb(st, "acc", [P, 2 * H])
            relu = sb(st, "relu", [P, 2 * H])
            dtv = sb(st, "dtv", [P, 2, 2 * H])
            av = sb(st, "av", [P, 2, 2 * H])
            wt = sb(st, "wt", [P, H])
            wk = sb(st, "wk", [P, H])

            b_tp, b_ip = banks[0:2], banks[2:4]
            b_cs, b_g, b_y, b_misc = banks[4], banks[5], banks[6], banks[7]
            DT0 = 264

            c_in = sem("constants_loaded")
            wraw_in = [sem("raw_weight_loaded_0"), sem("raw_weight_loaded_1")]
            whi = sem("weight_hi_ready")
            wlo = sem("weight_lo_ready")
            su_v = sem("setup_vector_steps")
            su_g = sem("setup_gpsimd_steps")
            su_a = sem("setup_scalar_steps")
            x_in = [sem("x_loaded_even"), sem("x_loaded_odd")]
            stats = sem("ln_stats_done")
            moments = sem("ln_moments_done")
            scales = sem("ln_scale_steps")
            h0_ready = sem("h0_ready")
            u_ready = sem("u_ready")
            ut_done = sem("u_transposed")
            uh_ready = sem("u_hi_ready")
            ul_ready = sem("u_lo_ready")
            ip_done = sem("in_projection_pair_done")
            xraw_ready = sem("conv_input_ready")
            halo_ready = sem("conv_halo_ready")
            conv_step = sem("conv_steps")
            xtanh = sem("xbc_tanh_ready")
            xbc_ready = sem("xbc_ready")
            ztanh = sem("z_tanh_ready")
            zs_ready = sem("z_silu_ready")
            dtp_done = sem("dt_projected")
            dt_step = sem("dt_steps")
            dt_exp = sem("dt_exp_ready")
            atri_ready = sem("atri_ready")
            misc_done = sem("token_major_done")
            xb_ready = sem("token_major_copied")
            csbc_done = sem("cumsum_done")
            ecs_ready = sem("exp_cumsum_ready")
            diff_done = sem("cumsum_differences_ready")
            e_ready = sem("decay_exps_ready")
            wk_ready = sem("state_weights_ready")
            g_done = sem("scores_done")
            m_ready = sem("decayed_scores_ready")
            cd_ready = sem("c_decayed_ready")
            xw_ready = sem("x_weighted_ready")
            y_done = sem("y_done")
            st_done = sem("chunk_state_done")
            yd_ready = sem("y_plus_dx_ready")
            yg_ready = sem("y_gated_ready")
            s_upd = sem("state_updated")
            state_raw = sem("state_before_reset")
            o_done = sem("out_projection_done")
            h_ready = sem("h_ready")
            ss_ready = sem("h_mean_square_ready")
            rms_step = sem("h_rms_steps")
            h2_ready = sem("h2_ready")
            h2t_done = sem("h2_transposed")
            h2t_ready = sem("h2t_copied")
            a_out = sem("block_a_stored")

            PIN = 2 * NPAIR * P // 512 * KD + (KD if (2 * NPAIR * P) % 512 else 0)
            pieces = []
            for k in range(KD):
                for c0 in range(0, 2 * NPAIR * P, 512):
                    pieces.append(("in", k, c0, min(512, 2 * NPAIR * P - c0)))
            for j in range(NJ):
                pieces.append(("gate", j, 0, KD * P))
            assert len(pieces) - NJ == PIN

            with nc.Block() as block:

                @block.sync
                def _(sp):
                    sp.dma_start(ln_sb[:, :], ln_w).then_inc(c_in, 16)
                    sp.dma_start(rows_sb[:, 0:NR], rows.broadcast_to([P, NR])).then_inc(c_in, 16)
                    sp.dma_start(convw_sb[:, :, :], conv_w).then_inc(c_in, 16)
                    sp.dma_start(convb_sb[:, :], conv_b).then_inc(c_in, 16)
                    sp.dma_start(wdt_raw[:, :, :], w_dt).then_inc(c_in, 16)
                    sp.dma_start(wout_sb[:, :, :], w_out).then_inc(c_in, 16)
                    for m in range(2):
                        sp.dma_start(x_t[:, m, :, :], x_a[m]).then_inc(x_in[m], 16)
                    for n, (kind, a, c0, w) in enumerate(pieces):
                        if n >= 2:
                            sp.wait_ge(wlo, n - 1)
                        src = w_in[:, a, c0:c0 + w] if kind == "in" else gate_w[:, a, :]
                        sp.dma_start(w_raw[:, n % 2, 0:w], src).then_inc(wraw_in[n % 2], 16)

                    def load_x(m, q):
                        sp.wait_ge(u_ready, (m - 2) * CA + CA)
                        sp.dma_start(x_t[:, q, :, :], at_tile(x_a, m)).then_inc(x_in[q], 16)

                    def store(m):
                        sp.wait_ge(h2_ready, m * CA + CA)
                        sp.dma_start(at_tile(h_scr, m), h[:, :, :]).then_inc(a_out, 16)
                        sp.wait_ge(h2t_ready, m * 2 + 2)
                        sp.dma_start(at_tile(h2t_scr, m), h2t[:, :, :]).then_inc(a_out, 16)

                    with sp.Fori(0, NA // 2 - 1) as b:
                        load_x(b * 2 + 2, 0)
                        store(b * 2)
                        load_x(b * 2 + 3, 1)
                        store(b * 2 + 1)
                    store(NA - 2)
                    store(NA - 1)
                    sp.wait_ge(a_out, 32 * NA)

                @block.gpsimd
                def _(pool):
                    g = nc.gpsimd
                    n = 0

                    def after(ins):
                        nonlocal n
                        n += 1
                        ins.then_inc(su_g, 1)
                        pool.wait_ge(su_g, n)

                    after(g.memset(ident[:, :], 0.0))
                    after(g.affine_select(out=ident[:, :], in_=ident[:, :], compare_op=ALU.not_equal,
                                          fill=1.0, base=0, pattern=[[-1, P]], channel_multiplier=1))
                    after(g.memset(ones[:, :], 1.0))
                    after(g.memset(negmask[:, :], 0.0))
                    after(g.affine_select(out=tri[:, :], in_=ones[:, :], compare_op=ALU.is_ge,
                                          fill=0.0, base=0, pattern=[[1, P]], channel_multiplier=-1))
                    after(g.affine_select(out=negmask[:, :], in_=negmask[:, :], compare_op=ALU.is_ge,
                                          fill=MASKED, base=0, pattern=[[1, P]], channel_multiplier=-1))
                    after(g.memset(halfc[:, :], -0.5))
                    after(g.memset(epsc[:, :], EPS))
                    after(g.memset(epsm[:, :], EPS_MHC))
                    after(g.memset(keep[:, :], 1.0))
                    for b in range(0, BATCHES + 1):
                        i = b * NA // BATCHES
                        after(g.memset(keep[:, i:i + 1], 0.0))
                    after(g.memset(state[:, :], 0.0))
                    assert n == SU_G, n
                    g.memset(xraw[:, :, 0:HALO], 0.0).then_inc(halo_ready, 1)

                    def ln_scales(m):
                        s = Steps(pool, scales, 7)
                        s.begin(m)
                        pool.wait_ge(moments, m * CA + CA)
                        pool.wait_ge(u_ready, m * CA)
                        s.done(g.tensor_tensor(ve[:, :], mom[:, :, 1], epsc[:, 0:CA], ALU.add))
                        s.wait()
                        s.done(g.tensor_tensor(rstd[:, :], ve[:, :], halfc[:, 0:CA], ALU.pow))
                        s.wait()
                        s.done(g.tensor_tensor(qv[:, :], rstd[:, :], rstd[:, :], ALU.mult))
                        s.wait()
                        s.done(g.tensor_tensor(qv[:, :], qv[:, :], mom[:, :, 1], ALU.mult))
                        s.wait()
                        s.done(g.tensor_tensor(qv[:, :], qv[:, :], epsc[:, 0:CA], ALU.add))
                        s.wait()
                        s.done(g.tensor_tensor(rr[:, :], qv[:, :], halfc[:, 0:CA], ALU.pow))
                        s.wait()
                        s.done(g.tensor_tensor(rr[:, :], rr[:, :], rstd[:, :], ALU.mult))
                        s.end()

                    def halo(m):
                        pool.wait_ge(conv_step, m * 24)
                        kp = keep[:, bass.ds(m, 1)].rearrange("p (a o) -> p a o", o=1)
                        g.tensor_tensor(xraw[:, :, 0:HALO], xraw[:, :, TA:TA + HALO],
                                        kp.broadcast_to([P, NXBC, HALO]), ALU.mult)\
                            .then_inc(halo_ready, 1)

                    def a_tri(m, q, c):
                        pool.wait_ge(dt_step, m * DT + DT)
                        pool.wait_ge(csbc_done, m * CA + c)
                        a4 = av[:, q, c * H:c * H + H].rearrange("p (h o) -> p h o", o=1)
                        t4 = tri[:, :].rearrange("p (o q) -> p o q", o=1)
                        g.tensor_tensor(heads(atri[:, :]), t4.broadcast_to([P, H, P]),
                                        a4.broadcast_to([P, H, P]), ALU.mult).then_inc(atri_ready, 1)

                    def c_decayed(m, q, c):
                        pool.wait_ge(ecs_ready, m * CA + c + 1)
                        pool.wait_ge(xbc_ready, m + 1)
                        pool.wait_ge(y_done, m * CA + c)
                        g.tensor_tensor(heads(c_dec[:, :]), xbc[:, q, 2:6, c * P:c * P + P],
                                        heads(ecs[:, :]), ALU.mult).then_inc(cd_ready, 1)

                    def x_weighted(m, c):
                        pool.wait_ge(wk_ready, m * CA + c + 1)
                        pool.wait_ge(xb_ready, m * CA + c + 1)
                        pool.wait_ge(st_done, m * CA + c)
                        x4 = xb_tok[:, 0:P].rearrange("p (o q) -> p o q", o=1)
                        w4 = wk[:, :].rearrange("p (h o) -> p h o", o=1)
                        g.tensor_tensor(heads(xw[:, :]), x4.broadcast_to([P, H, P]),
                                        w4.broadcast_to([P, H, P]), ALU.mult).then_inc(xw_ready, 1)

                    def h_rms(m):
                        pool.wait_ge(ss_ready, m * CA + CA)
                        pool.wait_ge(h2_ready, m * CA)
                        g.tensor_tensor(msq[:, :], ss[:, :], epsc[:, 0:CA], ALU.add)\
                            .then_inc(rms_step, 1)
                        pool.wait_ge(rms_step, m * 2 + 1)
                        g.tensor_tensor(rh[:, :], msq[:, :], halfc[:, 0:CA], ALU.pow).then_inc(rms_step, 1)

                    def scan(m, q, nxt):
                        if nxt:
                            halo(m + 1)
                        for c in range(CA):
                            a_tri(m, q, c)
                            c_decayed(m, q, c)
                            x_weighted(m, c)
                        h_rms(m)

                    ln_scales(0)
                    ln_scales(1)
                    with pool.Fori(0, NA // 2 - 1) as b:
                        for q in range(2):
                            m = b * 2 + q
                            scan(m, q, True)
                            ln_scales(m + 2)
                    scan(NA - 2, 0, True)
                    scan(NA - 1, 1, False)

                @block.scalar
                def _(act):
                    a = nc.scalar
                    act.wait_ge(c_in, 96)
                    a.activation(a_rate[:, 0:H], rows_sb[:, 0:H], ACT.Exp).then_inc(su_a, 1)
                    a.activation(a_rate[:, H:2 * H], rows_sb[:, 0:H], ACT.Exp).then_inc(su_a, 1)

                    def u_high(m):
                        for i in range(2):
                            act.wait_ge(ut_done, m * 2 + i + 1)
                            act.wait_ge(dtp_done, m) if not isinstance(m, int) or m > 0 else None
                            a.copy(u_hi[:, 2 * i:2 * i + 2, :],
                                   b_tp[i][:, :].rearrange("p (k q) -> p k q", k=2)).then_inc(uh_ready, 1)

                    def conv_in(m, g):
                        act.wait_ge(ip_done, m * NPAIR + g + 1)
                        act.wait_ge(halo_ready, m + 1)
                        a.copy(xraw[:, 2 * g:2 * g + 2, HALO:HALO + TA],
                               b_ip[(QOF[0] + g) % 2][:, :].rearrange("p (k q) -> p k q", k=2))\
                            .then_inc(xraw_ready, 1)

                    def z_th(m, q, i):
                        act.wait_ge(ip_done, m * NPAIR + 3 + i + 1)
                        act.wait_ge(zs_ready, m * 2 + i - 1) if not (isinstance(m, int) and m == 0 and i < 1 + 1) else None
                        a.activation(z_tanh[:, i, :], b_ip[(q + 3 + i) % 2][:, :], ACT.Tanh, scale=0.5)\
                            .then_inc(ztanh, 1)

                    def dt_e(m):
                        act.wait_ge(dt_step, m * DT + 2)
                        a.activation(e1[:, :], nabs[:, :], ACT.Exp).then_inc(dt_exp, 1)

                    def xbc_th(m, q):
                        act.wait_ge(conv_step, m * 24 + 24)
                        if not (isinstance(m, int) and m == 0):
                            act.wait_ge(xbc_ready, m)
                        a.activation(xbc_tanh[:, :], xbc[:, q, :, :].rearrange("p c q -> p (c q)"),
                                     ACT.Tanh).then_inc(xtanh, 1)

                    def tok_major(m, c):
                        act.wait_ge(misc_done, m * CA + c + 1)
                        if not (isinstance(m, int) and m * CA + c == 0):
                            act.wait_ge(st_done, m * CA + c)
                        a.copy(xb_tok[:, :], b_misc[:, 0:2 * P + H]).then_inc(xb_ready, 1)

                    def exp_cs(m, c):
                        act.wait_ge(csbc_done, m * CA + c + 1)
                        if not (isinstance(m, int) and m * CA + c == 0):
                            act.wait_ge(cd_ready, m * CA + c)
                            act.wait_ge(s_upd, m * CA + c)
                        a.activation(ecs[:, :], b_cs[:, :], ACT.Exp).then_inc(ecs_ready, 1)

                    def decays(m, c):
                        act.wait_ge(diff_done, m * CA + c + 1)
                        a.activation(wt[:, :], wt[:, :], ACT.Exp).then_inc(e_ready, 1)
                        a.activation(decay[:, :], decay[:, :], ACT.Exp).then_inc(e_ready, 1)

                    def square_sum(m, c):
                        act.wait_ge(h_ready, m * CA + c + 1)
                        if not (isinstance(m, int) and m == 0):
                            act.wait_ge(h2t_done, m * 2)
                            act.wait_ge(rms_step, m * 2)
                        a.activation(h2[:, c, :], h[:, c, :], ACT.Square, scale=float(D) ** -0.5,
                                     accum_out=ss[:, c:c + 1])\
                            .then_inc(ss_ready, 1)

                    def h2t_copy(m):
                        for i in range(2):
                            act.wait_ge(h2t_done, m * 2 + i + 1)
                            if not (isinstance(m, int) and m == 0):
                                act.wait_ge(a_out, m * 32)
                            a.copy(h2t[:, 2 * i:2 * i + 2, :],
                                   b_tp[i][:, :].rearrange("p (k q) -> p k q", k=2)).then_inc(h2t_ready, 1)

                    QOF = [0]
                    for n_, (kind, r, c0, w) in enumerate(pieces):
                        act.wait_ge(wraw_in[n_ % 2], 16 * (n_ // 2 + 1))
                        if kind == "in":
                            a.activation(win_hi[:, r, c0:c0 + w], w_raw[:, n_ % 2, 0:w], ACT.Copy,
                                         scale=ln_sb[:, r:r + 1]).then_inc(whi, 1)
                        else:
                            for k in range(KD):
                                ins = a.activation(gate_hi[:, r, k * P:k * P + P],
                                                   w_raw[:, n_ % 2, k * P:k * P + P], ACT.Copy,
                                                   scale=ln_sb[:, KD + k:KD + k + 1])
                            ins.then_inc(whi, 1)
                        if n_ == PIN - 1:
                            for k in range(KD):
                                ins = a.activation(wdt_hi[:, k, :], wdt_raw[:, k, :], ACT.Copy,
                                                   scale=ln_sb[:, k:k + 1])
                            ins.then_inc(su_a, 1)

                    def front(m, q):
                        QOF[0] = q
                        for g in range(3):
                            conv_in(m, g)
                        for i in range(2):
                            z_th(m, q, i)
                        dt_e(m)
                        xbc_th(m, q)

                    u_high(0)
                    front(0, 0)

                    def body(m, q, nxt):
                        QOF[0] = 1 - q
                        if nxt:
                            u_high(m + 1)
                        tok_major(m, 0)
                        exp_cs(m, 0)
                        decays(m, 0)
                        if nxt:
                            conv_in(m + 1, 0)
                            conv_in(m + 1, 1)
                            conv_in(m + 1, 2)
                        tok_major(m, 1)
                        exp_cs(m, 1)
                        if nxt:
                            z_th(m + 1, 1 - q, 0)
                        decays(m, 1)
                        square_sum(m, 0)
                        if nxt:
                            z_th(m + 1, 1 - q, 1)
                            dt_e(m + 1)
                            xbc_th(m + 1, 1 - q)
                        square_sum(m, 1)
                        h2t_copy(m)

                    with act.Fori(0, NA // 2 - 1) as b:
                        for q in range(2):
                            body(b * 2 + q, q, True)
                    body(NA - 2, 0, True)
                    body(NA - 1, 1, False)

                @block.vector
                def _(dve):
                    v = nc.vector
                    dve.wait_ge(c_in, 96)
                    dve.wait_ge(su_a, 2)
                    n = 0

                    def after(ins):
                        nonlocal n
                        n += 1
                        ins.then_inc(su_v, 1)
                        dve.wait_ge(su_v, n)

                    after(v.tensor_scalar(a_rate[:, :], a_rate[:, :], -1.0, None, ALU.mult))
                    after(v.tensor_scalar(convw_sb[:, :, :].rearrange("p c t -> p (c t)"),
                                          convw_sb[:, :, :].rearrange("p c t -> p (c t)"), 0.5, None, ALU.mult))
                    after(v.tensor_scalar(convb_sb[:, :], convb_sb[:, :], 0.5, None, ALU.mult))
                    after(v.tensor_scalar(wout_sb[:, :, :].rearrange("p h d -> p (h d)"),
                                          wout_sb[:, :, :].rearrange("p h d -> p (h d)"), 0.5, None, ALU.mult))
                    assert n == SU_V

                    def ln_stats(m, q):
                        dve.wait_ge(x_in[q], (m - q) * 8 + 16)
                        for t in range(CA):
                            v.bn_stats(st6[:, t, :], x_t[:, q, t, :]).then_inc(stats, 1)
                        dve.wait_ge(stats, m * CA + CA)
                        v.memset(idle[:, :], 0.0)
                        for t in range(CA):
                            v.bn_aggr(mom[:, t, :], st6[:, t, :]).then_inc(moments, 1)

                    def normalize(m, q):
                        dve.wait_ge(scales, m * 7 + 7)
                        if not (isinstance(m, int) and m == 0):
                            dve.wait_ge(ut_done, m * 2)
                        for t in range(CA):
                            v.tensor_scalar(h0[:, q, t, :], x_t[:, q, t, :], mom[:, t, 0:1], rstd[:, t:t + 1],
                                            ALU.subtract, ALU.mult).then_inc(h0_ready, 1)
                        for t in range(CA):
                            v.tensor_scalar(u[:, t, :], x_t[:, q, t, :], mom[:, t, 0:1], rr[:, t:t + 1],
                                            ALU.subtract, ALU.mult).then_inc(u_ready, 1)

                    def u_low(m):
                        for i in range(2):
                            dve.wait_ge(uh_ready, m * 2 + i + 1)
                            v.tensor_tensor(u_lo[:, 2 * i:2 * i + 2, :],
                                            b_tp[i][:, :].rearrange("p (k q) -> p k q", k=2),
                                            u_hi[:, 2 * i:2 * i + 2, :].bitcast(F32), ALU.subtract)\
                                .then_inc(ul_ready, 1)

                    def conv(m, q, g):
                        dve.wait_ge(xraw_ready, m * 3 + g + 1)
                        dve.wait_ge(halo_ready, m + 1)
                        s = Steps(dve, conv_step, 24)
                        s.begin(m)
                        s.k = 8 * g
                        for tap in range(TAPS - 1, -1, -1):
                            for ch in (2 * g, 2 * g + 1):
                                src = xraw[:, ch, tap:tap + TA]
                                if tap == TAPS - 1:
                                    s.done(v.tensor_scalar(xbc[:, q, ch, :], src, convw_sb[:, ch, tap:tap + 1],
                                                           convb_sb[:, ch:ch + 1], ALU.mult, ALU.add))
                                else:
                                    s.wait(1)
                                    s.done(v.scalar_tensor_tensor(xbc[:, q, ch, :], src,
                                                                  convw_sb[:, ch, tap:tap + 1],
                                                                  xbc[:, q, ch, :], ALU.mult, ALU.add))

                    def xbc_silu(m, q):
                        dve.wait_ge(xtanh, m + 1)
                        flat = xbc[:, q, :, :].rearrange("p c q -> p (c q)")
                        v.scalar_tensor_tensor(flat, xbc_tanh[:, :], 1.0, flat, ALU.add, ALU.mult)\
                            .then_inc(xbc_ready, 1)

                    def z_silu(m, q, i):
                        dve.wait_ge(ztanh, m * 2 + i + 1)
                        v.scalar_tensor_tensor(zs[:, q, 2 * i:2 * i + 2, :].rearrange("p c q -> p (c q)"),
                                               z_tanh[:, i, :], 1.0, b_ip[(q + 3 + i) % 2][:, :],
                                               ALU.add, ALU.mult).then_inc(zs_ready, 1)

                    def dt_chain(m, q):
                        s = Steps(dve, dt_step, DT)
                        s.begin(m)
                        dve.wait_ge(dtp_done, m + 1)
                        b2 = rows_sb[:, H:3 * H]
                        s.done(v.tensor_tensor(pre[:, :], b_misc[:, DT0:DT0 + 2 * H], b2, ALU.add))
                        s.wait()
                        s.done(v.scalar_tensor_tensor(nabs[:, :], pre[:, :], -1.0, pre[:, :], ALU.mult, ALU.min))
                        dve.wait_ge(dt_exp, m + 1)
                        s.done(v.tensor_scalar(s1[:, :], e1[:, :], 2.0, None, ALU.add))
                        s.wait()
                        s.done(v.reciprocal(s1[:, :], s1[:, :]))
                        s.wait()
                        s.done(v.tensor_tensor(s1[:, :], s1[:, :], e1[:, :], ALU.mult))
                        s.wait()
                        s.done(v.tensor_tensor(s2[:, :], s1[:, :], s1[:, :], ALU.mult))
                        s.wait()
                        s.done(v.tensor_scalar(acc[:, :], s2[:, :], 1.0 / (2 * LN1P_TERMS + 1), None, ALU.mult))
                        for k in range(LN1P_TERMS - 1, 0, -1):
                            s.wait()
                            s.done(v.scalar_tensor_tensor(acc[:, :], acc[:, :], 1.0 / (2 * k + 1), s2[:, :],
                                                          ALU.add, ALU.mult))
                        s.wait()
                        s.done(v.scalar_tensor_tensor(acc[:, :], acc[:, :], 1.0, s1[:, :], ALU.add, ALU.mult))
                        s.done(v.tensor_scalar(relu[:, :], pre[:, :], 0.0, None, ALU.max))
                        s.wait()
                        s.done(v.scalar_tensor_tensor(dtv[:, q, :], acc[:, :], 2.0, relu[:, :], ALU.mult, ALU.add))
                        s.wait()
                        s.done(v.tensor_tensor(av[:, q, :], dtv[:, q, :], a_rate[:, :], ALU.mult))
                        s.end()

                    def differences(m, c):
                        dve.wait_ge(ecs_ready, m * CA + c + 1)
                        dve.wait_ge(xb_ready, m * CA + c + 1)
                        if not (isinstance(m, int) and m * CA + c == 0):
                            dve.wait_ge(y_done, m * CA + c)
                        for hh in range(H):
                            v.scalar_tensor_tensor(decay[:, hh * P:hh * P + P], b_cs[:, hh * P:hh * P + P],
                                                   xb_tok[:, 2 * P + hh:2 * P + hh + 1], negmask[:, :],
                                                   ALU.subtract, ALU.add)
                        v.tensor_tensor(wt[:, :], heads(b_cs[:, :])[:, :, P - 1], xb_tok[:, 2 * P:2 * P + H],
                                        ALU.subtract).then_inc(diff_done, 1)

                    def decay_scores(m, q, c):
                        dve.wait_ge(e_ready, (m * CA + c) * 2 + 1)
                        if not (isinstance(m, int) and m * CA + c == 0):
                            dve.wait_ge(xw_ready, m * CA + c)
                        v.tensor_tensor(wk[:, :], wt[:, :], dtv[:, q, c * H:c * H + H], ALU.mult)\
                            .then_inc(wk_ready, 1)
                        dve.wait_ge(e_ready, (m * CA + c) * 2 + 2)
                        dve.wait_ge(g_done, m * CA + c + 1)
                        for hh in range(H):
                            ins = v.scalar_tensor_tensor(decay[:, hh * P:hh * P + P], b_g[:, hh * P:hh * P + P],
                                                         dtv[:, q, c * H + hh:c * H + hh + 1],
                                                         decay[:, hh * P:hh * P + P], ALU.mult, ALU.mult)
                        ins.then_inc(m_ready, 1)

                    def y_gate(m, q, c):
                        dve.wait_ge(y_done, m * CA + c + 1)
                        if not (isinstance(m, int) and m * CA + c == 0):
                            dve.wait_ge(o_done, m * CA + c)
                        for hh in range(H):
                            ins = v.scalar_tensor_tensor(y[:, hh * P:hh * P + P], xbc[:, q, 0, c * P:c * P + P],
                                                         rows_sb[:, 3 * H + hh:3 * H + hh + 1],
                                                         b_y[:, hh * P:hh * P + P], ALU.mult, ALU.add)
                        ins.then_inc(yd_ready, 1)
                        dve.wait_ge(yd_ready, m * CA + c + 1)
                        v.tensor_tensor(heads(y[:, :]), heads(y[:, :]), zs[:, q, :, c * P:c * P + P], ALU.mult)\
                            .then_inc(yg_ready, 1)

                    def state_update(m, q, c):
                        dve.wait_ge(st_done, m * CA + c + 1)
                        dve.wait_ge(cd_ready, m * CA + c + 1)
                        last = q == 1 and c == CA - 1
                        for hh in range(H):
                            ins = v.scalar_tensor_tensor(state[:, hh * P:hh * P + P], state[:, hh * P:hh * P + P],
                                                         ecs[:, hh * P + P - 1:hh * P + P],
                                                         b_cs[:, hh * P:hh * P + P], ALU.mult, ALU.add)
                        if last:
                            ins.then_inc(state_raw, 1)
                            dve.wait_ge(state_raw, (m + 1) // 2 if isinstance(m, int) else QH[0] + 1)
                            ins = v.tensor_scalar(state[:, :], state[:, :], keep[:, bass.ds(m + 1, 1)], None,
                                                  ALU.mult)
                        ins.then_inc(s_upd, 1)

                    def residual(m, q, c):
                        dve.wait_ge(o_done, m * CA + c + 1)
                        if not (isinstance(m, int) and m == 0):
                            dve.wait_ge(a_out, m * 32)
                        v.tensor_tensor(h[:, c, :], b_g[:, :], h0[:, q, c, :], ALU.add).then_inc(h_ready, 1)

                    def h2_norm(m):
                        dve.wait_ge(rms_step, m * 2 + 2)
                        for t in range(CA):
                            v.tensor_scalar(h2[:, t, :], h[:, t, :], rh[:, t:t + 1], None, ALU.mult)\
                                .then_inc(h2_ready, 1)

                    QH = [0]
                    ln_stats(0, 0)
                    normalize(0, 0)
                    for n_, (kind, r, c0, w) in enumerate(pieces):
                        dve.wait_ge(whi, n_ + 1)
                        raw = w_raw[:, n_ % 2, :]
                        if kind == "in":
                            v.scalar_tensor_tensor(win_lo[:, r, c0:c0 + w], raw[:, 0:w], ln_sb[:, r:r + 1],
                                                   win_hi[:, r, c0:c0 + w].bitcast(F32),
                                                   ALU.mult, ALU.subtract).then_inc(wlo, 1)
                        else:
                            for k in range(KD):
                                ins = v.scalar_tensor_tensor(gate_lo[:, r, k * P:k * P + P],
                                                             raw[:, k * P:k * P + P],
                                                             ln_sb[:, KD + k:KD + k + 1],
                                                             gate_hi[:, r, k * P:k * P + P].bitcast(F32),
                                                             ALU.mult, ALU.subtract)
                            ins.then_inc(wlo, 1)
                        if n_ == PIN - 1:
                            dve.wait_ge(su_a, 3)
                            for k in range(KD):
                                ins = v.scalar_tensor_tensor(wdt_lo[:, k, :], wdt_raw[:, k, :],
                                                             ln_sb[:, k:k + 1], wdt_hi[:, k, :].bitcast(F32),
                                                             ALU.mult, ALU.subtract)
                            ins.then_inc(su_v, 1)
                    ln_stats(1, 1)
                    u_low(0)
                    normalize(1, 1)
                    for g in range(3):
                        conv(0, 0, g)
                    z_silu(0, 0, 0)
                    z_silu(0, 0, 1)
                    dt_chain(0, 0)
                    xbc_silu(0, 0)

                    def body(m, q, nxt, nxt2):
                        if nxt:
                            u_low(m + 1)
                        differences(m, 0)
                        decay_scores(m, q, 0)
                        if nxt:
                            conv(m + 1, 1 - q, 0)
                        y_gate(m, q, 0)
                        state_update(m, q, 0)
                        if nxt:
                            conv(m + 1, 1 - q, 1)
                        residual(m, q, 0)
                        differences(m, 1)
                        decay_scores(m, q, 1)
                        if nxt:
                            conv(m + 1, 1 - q, 2)
                            z_silu(m + 1, 1 - q, 0)
                        y_gate(m, q, 1)
                        state_update(m, q, 1)
                        if nxt:
                            z_silu(m + 1, 1 - q, 1)
                            dt_chain(m + 1, 1 - q)
                            xbc_silu(m + 1, 1 - q)
                        residual(m, q, 1)
                        if nxt2:
                            ln_stats(m + 2, q)
                        h2_norm(m)
                        if nxt2:
                            normalize(m + 2, q)

                    with dve.Fori(0, NA // 2 - 1) as b:
                        QH[0] = b
                        for q in range(2):
                            body(b * 2 + q, q, True, True)
                    body(NA - 2, 0, True, False)
                    body(NA - 1, 1, False, False)

                @block.tensor
                def _(pe):
                    t_ = nc.tensor

                    def u_transpose(m):
                        pe.wait_ge(u_ready, m * CA + CA)
                        if not (isinstance(m, int) and m == 0):
                            pe.wait_ge(ul_ready, m * 2)
                            if not (isinstance(m, int) and m == 1):
                                pe.wait_ge(h2t_ready, (m - 1) * 2)
                        for i in range(2):
                            for k in range(2):
                                for t in range(CA):
                                    ins = t_.transpose(b_tp[i][:, k * TA + t * P:k * TA + t * P + P],
                                                       u[:, t, (2 * i + k) * P:(2 * i + k + 1) * P], ident[:, :])
                            ins.then_inc(ut_done, 1)

                    def in_proj(m, q, g):
                        if g == 0:
                            pe.wait_ge(ul_ready, m * 2 + 2)
                        if g < 2:
                            if not (isinstance(m, int) and m == 0):
                                pe.wait_ge(zs_ready, m * 2 - 1 + g)
                        else:
                            pe.wait_ge(xraw_ready, m * 3 + g - 1)
                        bank = b_ip[(q + g) % 2]
                        for c in range(2):
                            col = (2 * g + c) * P
                            n = 0
                            for k in range(KD):
                                for wv, uv in ((win_hi, u_hi), (win_lo, u_hi), (win_hi, u_lo)):
                                    ins = t_.matmul(bank[:, c * TA:c * TA + TA], wv[:, k, col:col + P], uv[:, k, :],
                                                    start=(n == 0), stop=(n == 3 * KD - 1))
                                    n += 1
                        ins.then_inc(ip_done, 1)

                    def dt_proj(m):
                        if not (isinstance(m, int) and m == 0):
                            pe.wait_ge(xb_ready, m * CA)
                        for t in range(CA):
                            n = 0
                            for k in range(KD):
                                for wv, uv in ((wdt_hi, u_hi), (wdt_lo, u_hi), (wdt_hi, u_lo)):
                                    ins = t_.matmul(b_misc[:, DT0 + t * H:DT0 + t * H + H],
                                                    uv[:, k, t * P:t * P + P], wv[:, k, :],
                                                    start=(n == 0), stop=(n == 3 * KD - 1))
                                    n += 1
                        ins.then_inc(dtp_done, 1)

                    def scan_in(m, q, c):
                        pe.wait_ge(dt_step, m * DT + DT)
                        pe.wait_ge(xbc_ready, m + 1)
                        if not (isinstance(m, int) and m * CA + c == 0):
                            pe.wait_ge(xb_ready, m * CA + c)
                            pe.wait_ge(s_upd, m * CA + c)
                        tok = slice(c * P, c * P + P)
                        t_.transpose(b_misc[:, 0:P], xbc[:, q, 0, tok], ident[:, :])
                        t_.transpose(b_misc[:, P:2 * P], xbc[:, q, 1, tok], ident[:, :])
                        t_.matmul(b_misc[:, 2 * P:2 * P + H], tri[:, :], av[:, q, c * H:c * H + H],
                                  start=True, stop=True).then_inc(misc_done, 1)
                        pe.wait_ge(atri_ready, m * CA + c + 1)
                        t_.matmul(b_cs[:, :], ones[:, :], atri[:, :], start=True, stop=True).then_inc(csbc_done, 1)
                        if not (isinstance(m, int) and m * CA + c == 0):
                            pe.wait_ge(h_ready, m * CA + c)
                        t_.matmul(b_g[:, :], xbc[:, q, 1, tok], xbc[:, q, 2:6, tok],
                                  start=True, stop=True).then_inc(g_done, 1)

                    def scan_out(m, c):
                        pe.wait_ge(xw_ready, m * CA + c + 1)
                        pe.wait_ge(diff_done, m * CA + c + 1)
                        pe.wait_ge(m_ready, m * CA + c + 1)
                        pe.wait_ge(cd_ready, m * CA + c + 1)
                        if not (isinstance(m, int) and m * CA + c == 0):
                            pe.wait_ge(yd_ready, m * CA + c)
                            pe.wait_ge(s_upd, m * CA + c)
                        t_.matmul(b_y[:, :], xb_tok[:, 0:P], decay[:, :], start=True, stop=False)
                        for hh in range(H):
                            ins = t_.matmul(b_y[:, hh * P:hh * P + P], state[:, hh * P:hh * P + P],
                                            c_dec[:, hh * P:hh * P + P], start=False, stop=(hh == H - 1))
                        ins.then_inc(y_done, 1)
                        t_.matmul(b_cs[:, :], xb_tok[:, P:2 * P], xw[:, :], start=True, stop=True)\
                            .then_inc(st_done, 1)

                    def out_proj(m, c):
                        pe.wait_ge(yg_ready, m * CA + c + 1)
                        for hh in range(H):
                            ins = t_.matmul(b_g[:, :], y[:, hh * P:hh * P + P], wout_sb[:, hh, :],
                                            start=(hh == 0), stop=(hh == H - 1))
                        ins.then_inc(o_done, 1)

                    def h2_transpose(m):
                        pe.wait_ge(h2_ready, m * CA + CA)
                        for i in range(2):
                            for k in range(2):
                                for t in range(CA):
                                    ins = t_.transpose(b_tp[i][:, k * TA + t * P:k * TA + t * P + P],
                                                       h2[:, t, (2 * i + k) * P:(2 * i + k + 1) * P], ident[:, :])
                            ins.then_inc(h2t_done, 1)

                    pe.wait_ge(su_g, SU_G)
                    u_transpose(0)
                    pe.wait_ge(wlo, PIN)
                    pe.wait_ge(su_v, SU_V + 1)
                    for g in range(NPAIR):
                        in_proj(0, 0, g)
                    dt_proj(0)

                    def body(m, q, nxt):
                        if nxt:
                            u_transpose(m + 1)
                        scan_in(m, q, 0)
                        if nxt:
                            in_proj(m + 1, 1 - q, 0)
                            in_proj(m + 1, 1 - q, 1)
                        scan_out(m, 0)
                        if nxt:
                            in_proj(m + 1, 1 - q, 2)
                        out_proj(m, 0)
                        scan_in(m, q, 1)
                        if nxt:
                            in_proj(m + 1, 1 - q, 3)
                        scan_out(m, 1)
                        if nxt:
                            in_proj(m + 1, 1 - q, 4)
                            dt_proj(m + 1)
                        out_proj(m, 1)
                        h2_transpose(m)

                    with pe.Fori(0, NA // 2 - 1) as b:
                        for q in range(2):
                            body(b * 2 + q, q, True)
                    body(NA - 2, 0, True)
                    body(NA - 1, 1, False)

        with ExitStack() as st:
            up_hi = sb(st, "up_hi", [P, NJ, KD * P], F32R)
            up_lo = sb(st, "up_lo", [P, NJ, KD * P], F32R)
            down_sb = sb(st, "down_sb", [P, NJ, D])
            h2_raw = sb(st, "h2_raw", [P, KD, TB])
            h2_hi = sb(st, "h2_hi", [P, KD, TB], F32R)
            h2_lo = sb(st, "h2_lo", [P, KD, TB], F32R)
            hm = sb(st, "hm", [P, CB, D])
            x1 = sb(st, "x1", [P, CB, D])
            xn = sb(st, "xn", [P, CB, D])
            th = sb(st, "th", [P, TB])
            glu = sb(st, "glu", [P, 2, TB])
            tr = sb(st, "tr", [P, D])
            mix = sb(st, "mix", [P, 2, D])
            up_raw = mix
            wlog = sb(st, "wlog", [P, KD, NLOG])
            wbr = sb(st, "wbr", [P, P])
            xpre = sb(st, "xpre", [P, P])
            sg = sb(st, "sg", [P, 4])
            eye = sb(st, "eye", [P, 4, CB, 4])
            b6 = sb(st, "b6", [P, CB, 6])
            bm = sb(st, "bm", [P, CB, 2])
            bv = sb(st, "bv", [P, CB])
            br = sb(st, "br", [P, CB])
            bq = sb(st, "bq", [P, CB])
            bx = sb(st, "bx", [P, CB])
            f6 = sb(st, "f6", [P, 2, 6])
            fm = sb(st, "fm", [P, 2, 2])
            fv = sb(st, "fv", [P, 2])
            fr = sb(st, "fr", [P, 2])
            lg = sb(st, "lg", [P, CB, NLOG])
            sm = sb(st, "sm", [P, CB, 8])
            smx = sb(st, "smx", [P, CB, 2])
            zl = sb(st, "zl", [P, 4, CB, 4])
            ze = sb(st, "ze", [P, 4, CB, 4])
            pm = sb(st, "pm", [P, 4, CB, 4])
            rowv = sb(st, "rowv", [P, 4, CB])
            colv = sb(st, "colv", [P, CB, 4])

            b_gate, b_up = banks[0], banks[1]
            b_down = banks[2:6]
            b_tr, b_lg = banks[6], banks[7]

            k_in = sem("b_constants_loaded")
            ur_in = [sem("up_raw_loaded_0"), sem("up_raw_loaded_1")]
            up_h = sem("up_hi_ready")
            up_l = sem("up_lo_ready")
            b_su = sem("b_setup_steps")
            h2_in = sem("h2t_loaded")
            hm_in = sem("h_loaded")
            xb_in = sem("x_again_loaded")
            hh_ready = sem("h2_hi_ready")
            hl_ready = sem("h2_lo_ready")
            gate_done = sem("gate_product_done")
            up_done = sem("up_product_done")
            th_ready = sem("gate_tanh_ready")
            s1_ready = sem("gate_silu_ready")
            glu_ready = sem("glu_ready")
            down_done = sem("down_product_done")
            mo_ready = sem("mlp_output_ready")
            c_step = sem("mhc_vector_steps")
            mom_b = sem("mlp_output_moments_ready")
            lnb = sem("mlp_output_scale_ready")
            nb_ready = sem("mlp_output_normalized")
            x1_ready = sem("x1_ready")
            mom_x = sem("x1_moments_ready")
            lnx = sem("x1_scale_steps")
            xn_ready = sem("streams_ready")
            xt_done = sem("streams_transposed")
            xt_ready = sem("streams_transpose_copied")
            lg_done = sem("logits_done")
            sm_in = sem("softmax_inputs_ready")
            sm_exp = sem("softmax_exps_ready")
            z_in = sem("sinkhorn_inputs_ready")
            z_exp = sem("sinkhorn_exps_ready")
            xp_ready = sem("x_pre_ready")
            xpt_done = sem("x_pre_transposed")
            xpt_ready = sem("x_pre_transpose_copied")
            br_done = sem("branch_product_done")
            mom_f = sem("mix_moments_ready")
            lnf = sem("mix_scale_ready")
            fin_n = sem("mix_normalized")
            fin = sem("tile_output_ready")
            b_out = [sem("even_outputs_stored"), sem("odd_outputs_stored")]

            with nc.Block() as block:

                @block.sync
                def _(sp):
                    def load_h2(m):
                        if not (isinstance(m, int) and m == 0):
                            sp.wait_ge(hl_ready, m * KD)
                        for uu in range(2):
                            sp.dma_start(h2_raw[:, :, uu * TA:uu * TA + TA],
                                         at_tile(h2t_scr_b[:, uu], m)).then_inc(h2_in, 16)

                    def load_hm(m):
                        if not (isinstance(m, int) and m == 0):
                            sp.wait_ge(x1_ready, m * CB)
                        for uu in range(2):
                            sp.dma_start(hm[:, 2 * uu:2 * uu + 2, :], at_tile(h_scr_b[:, uu], m))\
                                .then_inc(hm_in, 16)

                    def load_x(m):
                        if not (isinstance(m, int) and m == 0):
                            sp.wait_ge(fin, m * CB)
                        sp.dma_start(x1[:, :, :], at_tile(x_b, m)).then_inc(xb_in, 16)

                    def store(m):
                        for t in range(CB):
                            sp.wait_ge(fin, m * CB + t + 1)
                            sp.dma_start(at_tile(out_b[:, :, t], m), mix[:, t % 2, :]).then_inc(b_out[t % 2], 16)

                    load_h2(0)
                    sp.dma_start(wlog[:, :, :], w_logit).then_inc(k_in, 16)
                    sp.dma_start(wbr[:, :], w_branch).then_inc(k_in, 16)
                    for j in range(NJ):
                        if j >= 2:
                            sp.wait_ge(up_l, j - 1)
                        sp.dma_start(up_raw[:, j % 2, :], up_w[:, j, :]).then_inc(ur_in[j % 2], 16)
                        sp.dma_start(down_sb[:, j, :], down_w[:, j, :]).then_inc(k_in, 16)
                    load_hm(0)
                    load_x(0)
                    with sp.Fori(1, NB) as m:
                        load_h2(m)
                        load_hm(m)
                        store(m - 1)
                        load_x(m)
                    store(NB - 1)
                    for half in b_out:
                        sp.wait_ge(half, 16 * TOK // P // 2)

                @block.gpsimd
                def _(pool):
                    g = nc.gpsimd

                    def out_scale(m):
                        pool.wait_ge(mom_b, m * CB + CB)
                        g.tensor_tensor(bv[:, :], bm[:, :, 1], epsc[:, :], ALU.add).then_inc(lnb, 1)
                        pool.wait_ge(lnb, m * 2 + 1)
                        g.tensor_tensor(br[:, :], bv[:, :], halfc[:, :], ALU.pow).then_inc(lnb, 1)

                    def x1_add(m):
                        pool.wait_ge(xb_in, m * 16 + 16)
                        for t in range(CB):
                            pool.wait_ge(nb_ready, m * CB + t + 1)
                            g.tensor_tensor(x1[:, t, :], x1[:, t, :], hm[:, t, :], ALU.add).then_inc(x1_ready, 1)

                    def x1_scales(m):
                        s = Steps(pool, lnx, 6)
                        s.begin(m)
                        pool.wait_ge(mom_x, m * CB + CB)
                        s.done(g.tensor_tensor(bv[:, :], bm[:, :, 1], epsc[:, :], ALU.add))
                        s.wait()
                        s.done(g.tensor_tensor(br[:, :], bv[:, :], halfc[:, :], ALU.pow))
                        s.wait()
                        s.done(g.tensor_tensor(bq[:, :], br[:, :], br[:, :], ALU.mult))
                        s.wait()
                        s.done(g.tensor_tensor(bq[:, :], bq[:, :], bm[:, :, 1], ALU.mult))
                        s.wait()
                        s.done(g.tensor_tensor(bq[:, :], bq[:, :], epsm[:, :], ALU.add))
                        s.wait()
                        s.done(g.tensor_tensor(bx[:, :], bq[:, :], halfc[:, :], ALU.pow))
                        s.end()

                    def mix_scale(m, t):
                        i = m * CB + t
                        pool.wait_ge(mom_f, i + 1)
                        g.tensor_tensor(fv[:, t % 2:t % 2 + 1], fm[:, t % 2, 1:2], epsc[:, 0:1], ALU.add)\
                            .then_inc(lnf, 1)
                        pool.wait_ge(lnf, i * 2 + 1)
                        g.tensor_tensor(fr[:, t % 2:t % 2 + 1], fv[:, t % 2:t % 2 + 1], halfc[:, 0:1], ALU.pow)\
                            .then_inc(lnf, 1)

                    def final_add(m, t):
                        pool.wait_ge(fin_n, m * CB + t + 1)
                        g.tensor_tensor(mix[:, t % 2, :], mix[:, t % 2, :], x1[:, t, :], ALU.add)\
                            .then_inc(fin, 1)

                    def mhc(m):
                        out_scale(m)
                        x1_add(m)
                        x1_scales(m)
                        for t in range(CB):
                            mix_scale(m, t)
                            final_add(m, t)

                    with pool.Fori(0, NB) as m:
                        mhc(m)

                @block.scalar
                def _(act):
                    a = nc.scalar
                    for j in range(NJ):
                        act.wait_ge(ur_in[j % 2], 16 * (j // 2 + 1))
                        for k in range(KD):
                            ins = a.activation(up_hi[:, j, k * P:k * P + P], up_raw[:, j % 2, k * P:k * P + P],
                                               ACT.Copy, scale=ln_sb[:, KD + k:KD + k + 1])
                        ins.then_inc(up_h, 1)
                        if j == 0:
                            a.activation(sg[:, 0:1], rows_sb[:, 16:17], ACT.Exp, scale=-1.0).then_inc(b_su, 1)
                            act.wait_ge(h2_in, 32)
                            for k in range(KD):
                                a.copy(h2_hi[:, k, :], h2_raw[:, k, :]).then_inc(hh_ready, 1)

                    def h2_high(m):
                        act.wait_ge(h2_in, m * 32 + 32)
                        act.wait_ge(up_done, m * NJ)
                        for k in range(KD):
                            a.copy(h2_hi[:, k, :], h2_raw[:, k, :]).then_inc(hh_ready, 1)

                    def gate_tanh(m, j):
                        act.wait_ge(gate_done, m * NJ + j + 1)
                        if not (isinstance(m, int) and m * NJ + j == 0):
                            act.wait_ge(glu_ready, m * NJ + j)
                        a.activation(th[:, :], b_gate[:, :], ACT.Tanh, scale=0.5).then_inc(th_ready, 1)

                    def tr_copy(m, t):
                        i = m * CB + t
                        act.wait_ge(xt_done, i + 1)
                        if not (isinstance(m, int) and i == 0):
                            act.wait_ge(lg_done, i)
                        a.copy(tr[:, :], b_tr[:, :]).then_inc(xt_ready, 1)

                    def softmax_exp(m):
                        act.wait_ge(sm_in, m + 1)
                        a.activation(sm[:, :, :], sm[:, :, :], ACT.Exp).then_inc(sm_exp, 1)

                    def sink_exp(m):
                        act.wait_ge(z_in, m + 1)
                        a.activation(ze[:, :, :, :], zl[:, :, :, :], ACT.Exp).then_inc(z_exp, 1)
                        act.wait_ge(z_in, m + 1)
                        a.activation(pm[:, :, :, :], pm[:, :, :, :], ACT.Exp).then_inc(z_exp, 1)

                    def xpre_copy(m, t):
                        i = m * CB + t
                        act.wait_ge(xpt_done, i + 1)
                        if t > 0:
                            act.wait_ge(br_done, i)
                        else:
                            act.wait_ge(lg_done, i + CB)
                        a.copy(tr[:, 0:P], b_lg[:, 0:P]).then_inc(xpt_ready, 1)

                    def body(m, mlp, mhc, c):
                        for j in range(NJ):
                            if mlp:
                                gate_tanh(m, j)
                            if mhc:
                                if j == 2:
                                    for t in range(CB):
                                        tr_copy(c, t)
                                if j == 3:
                                    softmax_exp(c)
                                    sink_exp(c)
                                if j >= 10:
                                    xpre_copy(c, j - 10)
                    body(0, True, False, 0)
                    with act.Fori(1, NB) as m:
                        h2_high(m)
                        body(m, True, True, m - 1)
                    body(0, False, True, NB - 1)

                @block.vector
                def _(dve):
                    v = nc.vector
                    PER = CSTEPS

                    for j in range(NJ):
                        dve.wait_ge(up_h, j + 1)
                        for k in range(KD):
                            ins = v.scalar_tensor_tensor(up_lo[:, j, k * P:k * P + P],
                                                         up_raw[:, j % 2, k * P:k * P + P],
                                                         ln_sb[:, KD + k:KD + k + 1],
                                                         up_hi[:, j, k * P:k * P + P].bitcast(F32),
                                                         ALU.mult, ALU.subtract)
                        ins.then_inc(up_l, 1)
                        if j == 0:
                            for k in range(KD):
                                dve.wait_ge(hh_ready, k + 1)
                                v.tensor_tensor(h2_lo[:, k, :], h2_raw[:, k, :], h2_hi[:, k, :].bitcast(F32),
                                                ALU.subtract).then_inc(hl_ready, 1)
                    n = 1

                    def after(ins):
                        nonlocal n
                        n += 1
                        ins.then_inc(b_su, 1)
                        dve.wait_ge(b_su, n)

                    dve.wait_ge(b_su, 1)
                    after(v.tensor_scalar(sg[:, 1:2], sg[:, 0:1], 1.0, None, ALU.add))
                    after(v.reciprocal(sg[:, 2:3], sg[:, 1:2]))
                    after(v.tensor_scalar(sg[:, 3:4], sg[:, 2:3], -1.0, 1.0, ALU.mult, ALU.add))
                    after(v.memset(eye[:, :, :, :], 0.0))
                    for i in range(4):
                        after(v.tensor_scalar(eye[:, i, :, i], eye[:, i, :, i], sg[:, 3:4], None, ALU.add))

                    def h2_low(m):
                        for k in range(KD):
                            dve.wait_ge(hh_ready, m * KD + k + 1)
                            v.tensor_tensor(h2_lo[:, k, :], h2_raw[:, k, :], h2_hi[:, k, :].bitcast(F32),
                                            ALU.subtract).then_inc(hl_ready, 1)

                    def gate_silu(m, j):
                        dve.wait_ge(th_ready, m * NJ + j + 1)
                        v.scalar_tensor_tensor(th[:, :], th[:, :], 1.0, b_gate[:, :], ALU.add, ALU.mult)\
                            .then_inc(s1_ready, 1)

                    def gate_up(m, j):
                        i = m * NJ + j
                        dve.wait_ge(up_done, i + 1)
                        dve.wait_ge(s1_ready, i + 1)
                        if not (isinstance(m, int) and i < 2):
                            dve.wait_ge(down_done, i - 1)
                        v.scalar_tensor_tensor(glu[:, j % 2, :], th[:, :], 0.5, b_up[:, :], ALU.mult, ALU.mult)\
                            .then_inc(glu_ready, 1)

                    def mlp_out(m):
                        dve.wait_ge(down_done, m * NJ + NJ)
                        dve.wait_ge(hm_in, m * 32 + 32)
                        for t in range(CB):
                            v.tensor_tensor(hm[:, t, :], b_down[t][:, :], hm[:, t, :], ALU.add)\
                                .then_inc(mo_ready, 1)

                    s = Steps(dve, c_step, PER)

                    def step(ins, wait=True):
                        s.done(ins)
                        if wait:
                            s.wait()

                    def norm_out(m):
                        for t in range(CB):
                            dve.wait_ge(mo_ready, m * CB + t + 1)
                            step(v.bn_stats(b6[:, t, :], hm[:, t, :]), wait=False)
                        s.wait()
                        v.memset(idle[:, :], 0.0)
                        for t in range(CB):
                            v.bn_aggr(bm[:, t, :], b6[:, t, :]).then_inc(mom_b, 1)
                        dve.wait_ge(lnb, m * 2 + 2)
                        for t in range(CB):
                            v.tensor_scalar(hm[:, t, :], hm[:, t, :], bm[:, t, 0:1], br[:, t:t + 1],
                                            ALU.subtract, ALU.mult).then_inc(nb_ready, 1)

                    def streams(m):
                        for t in range(CB):
                            dve.wait_ge(x1_ready, m * CB + t + 1)
                            step(v.bn_stats(b6[:, t, :], x1[:, t, :]), wait=False)
                        s.wait()
                        v.memset(idle[:, :], 0.0)
                        for t in range(CB):
                            v.bn_aggr(bm[:, t, :], b6[:, t, :]).then_inc(mom_x, 1)
                        dve.wait_ge(lnx, m * 6 + 2)
                        for t in range(CB):
                            v.tensor_scalar(xn[:, t, :], x1[:, t, :], bm[:, t, 0:1], br[:, t:t + 1],
                                            ALU.subtract, ALU.mult).then_inc(xn_ready, 1)

                    def logits(m):
                        dve.wait_ge(lnx, m * 6 + 6)
                        dve.wait_ge(lg_done, m * CB + CB)
                        for t in range(CB):
                            step(v.scalar_tensor_tensor(lg[:, t, :], b_lg[:, t * NLOG:(t + 1) * NLOG],
                                                        bx[:, t:t + 1], rows_sb[:, 17:17 + NLOG],
                                                        ALU.mult, ALU.add), wait=(t == CB - 1))
                        pp = lg[:, :, 16:24].rearrange("p t (s j) -> p t s j", s=2)
                        sm4 = sm[:, :, :].rearrange("p t (s j) -> p t s j", s=2)
                        mx = smx[:, :, :].rearrange("p t (s o) -> p t s o", o=1)
                        step(v.tensor_reduce(smx[:, :, :], pp, AX.X, ALU.max))
                        v.tensor_tensor(sm4, pp, mx.broadcast_to([P, CB, 2, 4]), ALU.subtract).then_inc(sm_in, 1)
                        for t in range(CB):
                            step(v.tensor_scalar(zl[:, :, t, :], lg[:, t, 0:16].rearrange("p (i j) -> p i j", i=4),
                                                 10.0, None, ALU.mult), wait=(t == CB - 1))
                        step(v.tensor_reduce(rowv[:, :, :], zl[:, :, :, :], AX.X, ALU.max))
                        step(v.tensor_tensor(zl[:, :, :, :], zl[:, :, :, :],
                                             rowv[:, :, :].rearrange("p i (t o) -> p i t o", o=1)
                                             .broadcast_to([P, 4, CB, 4]), ALU.subtract))
                        step(v.tensor_reduce(colv[:, :, :], zl[:, :, :, :].rearrange("p i t j -> p t j i"),
                                             AX.X, ALU.max))
                        cb = colv[:, :, :].rearrange("p (o t) j -> p o (t j)", o=1).broadcast_to([P, 4, 4 * CB])
                        v.scalar_tensor_tensor(pm[:, :, :, :].rearrange("p i t j -> p i (t j)"),
                                               zl[:, :, :, :].rearrange("p i t j -> p i (t j)"), SHIFT, cb,
                                               ALU.add, ALU.subtract).then_inc(z_in, 1)

                    pit = pm[:, :, :, :].rearrange("p i t j -> p (i t) j")
                    pij = pm[:, :, :, :].rearrange("p i t j -> p i (t j)")
                    row_b = rowv[:, :, :].rearrange("p i (t o) -> p (i t) o", o=1).broadcast_to([P, 4 * CB, 4])
                    col_b = colv[:, :, :].rearrange("p (o t) j -> p o (t j)", o=1).broadcast_to([P, 4, 4 * CB])

                    def softmax_finish(m):
                        sm4 = sm[:, :, :].rearrange("p t (s j) -> p t s j", s=2)
                        mx = smx[:, :, :].rearrange("p t (s o) -> p t s o", o=1)
                        dve.wait_ge(sm_exp, m + 1)
                        step(v.tensor_reduce(smx[:, :, :], sm4, AX.X, ALU.add))
                        step(v.reciprocal(smx[:, :, :], smx[:, :, :]))
                        step(v.tensor_tensor(sm4, sm4, mx.broadcast_to([P, CB, 2, 4]), ALU.mult))

                    def sink_first(m):
                        dve.wait_ge(z_exp, m * 2 + 1)
                        step(v.tensor_reduce(rowv[:, :, :], ze[:, :, :, :], AX.X, ALU.add))
                        step(v.reciprocal(rowv[:, :, :], rowv[:, :, :]))
                        dve.wait_ge(z_exp, m * 2 + 2)
                        step(v.tensor_tensor(pit, pit, row_b, ALU.mult))

                    def sink_row():
                        step(v.tensor_reduce(rowv[:, :, :], pm[:, :, :, :], AX.X, ALU.add))
                        step(v.reciprocal(rowv[:, :, :], rowv[:, :, :]))
                        step(v.scalar_tensor_tensor(pit, row_b, SCALE_UP, pit, ALU.mult, ALU.mult))

                    def sink_col(last=False):
                        step(v.tensor_reduce(colv[:, :, :], pm[:, :, :, :].rearrange("p i t j -> p t j i"),
                                             AX.X, ALU.add))
                        step(v.reciprocal(colv[:, :, :], colv[:, :, :]))
                        step(v.scalar_tensor_tensor(pij, col_b, 1.0 if last else SCALE_UP, pij,
                                                    ALU.mult, ALU.mult))

                    def sink_end():
                        flat = pm[:, :, :, :].rearrange("p i t j -> p (i t j)")
                        step(v.scalar_tensor_tensor(flat, flat, sg[:, 2:3],
                                                    eye[:, :, :, :].rearrange("p i t j -> p (i t j)"),
                                                    ALU.mult, ALU.add))

                    def x_pre(m, t):
                        i = m * CB + t
                        if not (isinstance(m, int) and i == 0):
                            dve.wait_ge(xpt_done, i)
                        for n4 in range(4):
                            src, wgt = xn[:, t, n4 * P:n4 * P + P], sm[:, t, n4:n4 + 1]
                            if n4 == 0:
                                step(v.tensor_scalar(xpre[:, :], src, wgt, None, ALU.mult))
                            elif n4 < 3:
                                step(v.scalar_tensor_tensor(xpre[:, :], src, wgt, xpre[:, :], ALU.mult, ALU.add))
                            else:
                                v.scalar_tensor_tensor(xpre[:, :], src, wgt, xpre[:, :], ALU.mult, ALU.add)\
                                    .then_inc(xp_ready, 1)

                    def mixing(m, t):
                        i = m * CB + t
                        dve.wait_ge(b_out[t % 2], (m * 2 + t // 2) * 16)
                        for jj in range(4):
                            for ii in range(4):
                                dst = mix[:, t % 2, ii * P:ii * P + P]
                                src, wgt = xn[:, t, jj * P:jj * P + P], pm[:, ii, t, jj:jj + 1]
                                if jj == 0:
                                    step(v.tensor_scalar(dst, src, wgt, None, ALU.mult), wait=False)
                                else:
                                    s.wait(3)
                                    step(v.scalar_tensor_tensor(dst, src, wgt, dst, ALU.mult, ALU.add), wait=False)
                        dve.wait_ge(br_done, i + 1)
                        for ii in range(4):
                            dst = mix[:, t % 2, ii * P:ii * P + P]
                            s.wait(3)
                            step(v.scalar_tensor_tensor(dst, b_lg[:, P:2 * P], sm[:, t, 4 + ii:5 + ii], dst,
                                                        ALU.mult, ALU.add), wait=(ii == 3))
                        step(v.bn_stats(f6[:, t % 2, :], mix[:, t % 2, :]), wait=False)
                        s.wait()
                        v.memset(idle[:, :], 0.0)
                        v.bn_aggr(fm[:, t % 2, :], f6[:, t % 2, :]).then_inc(mom_f, 1)

                    def mix_norm(m, t):
                        i = m * CB + t
                        dve.wait_ge(lnf, i * 2 + 2)
                        v.tensor_scalar(mix[:, t % 2, :], mix[:, t % 2, :], fm[:, t % 2, 0:1],
                                        fr[:, t % 2:t % 2 + 1], ALU.subtract, ALU.mult).then_inc(fin_n, 1)

                    halves = [0]

                    def sinkhorn(upto):
                        while halves[0] < min(upto, 2 * SINK):
                            k = halves[0]
                            if k % 2 == 0:
                                sink_row()
                            else:
                                sink_col(last=(k == 2 * SINK - 1))
                            halves[0] += 1

                    def body(m, mlp, mhc, c):
                        s.begin(c)
                        for j in range(NJ):
                            if mlp:
                                gate_silu(m, j)
                            if mhc:
                                if j == 0:
                                    norm_out(c)
                                if j == 1:
                                    streams(c)
                                if j == 3:
                                    logits(c)
                                if j == 4:
                                    softmax_finish(c)
                                    sink_first(c)
                                    halves[0] = 1
                                if 4 <= j <= 10:
                                    sinkhorn(1 + 14 * (j - 4) + 7)
                            if mlp:
                                gate_up(m, j)
                            if mhc:
                                if 4 <= j <= 10:
                                    sinkhorn(1 + 14 * (j - 4) + 14)
                                if j == 10:
                                    sinkhorn(2 * SINK)
                                    sink_end()
                                if j >= 10:
                                    x_pre(c, j - 10)
                                    mixing(c, j - 10)
                                    mix_norm(c, j - 10)
                        if mhc:
                            s.end()
                        if mlp:
                            mlp_out(m)

                    body(0, True, False, 0)
                    with dve.Fori(1, NB) as m:
                        h2_low(m)
                        body(m, True, True, m - 1)
                    body(0, False, True, NB - 1)

                @block.tensor
                def _(pe):
                    t_ = nc.tensor

                    def product(m, j, bank, w_hi, w_lo, signal):
                        n = 0
                        for k in range(KD):
                            for wv, hv in ((w_hi, h2_hi), (w_lo, h2_hi), (w_hi, h2_lo)):
                                ins = t_.matmul(bank[:, :], wv[:, j, k * P:k * P + P], hv[:, k, :],
                                                start=(n == 0), stop=(n == 3 * KD - 1))
                                n += 1
                        ins.then_inc(signal, 1)

                    def gate(m, j):
                        i = m * NJ + j
                        if j == 0:
                            pe.wait_ge(hl_ready, m * KD + KD)
                        if not (isinstance(m, int) and i == 0):
                            pe.wait_ge(s1_ready, i)
                        product(m, j, b_gate, gate_hi, gate_lo, gate_done)

                    def up(m, j, first):
                        i = m * NJ + j
                        if first:
                            pe.wait_ge(up_l, j + 1)
                        if not (isinstance(m, int) and i == 0):
                            pe.wait_ge(glu_ready, i)
                        product(m, j, b_up, up_hi, up_lo, up_done)

                    def down(m, j):
                        i = m * NJ + j
                        pe.wait_ge(glu_ready, i + 1)
                        if j == 0:
                            if isinstance(m, int) and m == 0:
                                pe.wait_ge(k_in, 16 * (2 + NJ))
                            else:
                                pe.wait_ge(mo_ready, m * CB)
                        for t in range(CB):
                            ins = t_.matmul(b_down[t][:, :], glu[:, j % 2, t * P:t * P + P], down_sb[:, j, :],
                                            start=(j == 0), stop=(j == NJ - 1))
                        ins.then_inc(down_done, 1)

                    def stream_logits(c):
                        for t in range(CB):
                            i = c * CB + t
                            pe.wait_ge(xn_ready, i + 1)
                            if t > 0:
                                pe.wait_ge(xt_ready, i)
                            elif not (isinstance(c, int) and c == 0):
                                pe.wait_ge(fin_n, i)
                            for k in range(KD):
                                ins = t_.transpose(b_tr[:, k * P:k * P + P], xn[:, t, k * P:k * P + P], ident[:, :])
                            ins.then_inc(xt_done, 1)
                            pe.wait_ge(xt_ready, i + 1)
                            for k in range(KD):
                                ins = t_.matmul(b_lg[:, t * NLOG:(t + 1) * NLOG], tr[:, k * P:k * P + P],
                                                wlog[:, k, :], start=(k == 0), stop=(k == KD - 1))
                            ins.then_inc(lg_done, 1)

                    def branch(c, t):
                        i = c * CB + t
                        pe.wait_ge(xp_ready, i + 1)
                        pe.wait_ge(fin_n, i) if t > 0 else None
                        t_.transpose(b_lg[:, 0:P], xpre[:, :], ident[:, :]).then_inc(xpt_done, 1)
                        pe.wait_ge(xpt_ready, i + 1)
                        t_.matmul(b_lg[:, P:2 * P], tr[:, 0:P], wbr[:, :], start=True, stop=True)\
                            .then_inc(br_done, 1)

                    def body(m, mlp, mhc, c, first):
                        for j in range(NJ):
                            if mlp:
                                gate(m, j)
                                up(m, j, first)
                                if j > 0:
                                    down(m, j - 1)
                            if mhc and j == 2:
                                stream_logits(c)
                            if mhc and j >= 10:
                                branch(c, j - 10)
                        if mlp:
                            down(m, NJ - 1)

                    body(0, True, False, 0, True)
                    with pe.Fori(1, NB) as m:
                        body(m, True, True, m - 1, False)
                    body(0, False, True, NB - 1, False)


def kernel(**inputs):
    import numpy as _np
    import concourse.bacc as _bacc
    from concourse import mybir as _mybir
    from concourse.bass_utils import run_bass_kernel_spmd as _run

    i = {k: _np.asarray(a) for k, a in inputs.items()}

    def by_chunk(w):
        return w.reshape(-1, P, w.shape[1]).transpose(1, 0, 2)

    w_in = i["L0_attn_w_in"].T
    z, xb, dt = w_in[:, :D], w_in[:, D:D + 6 * P], w_in[:, D + 6 * P:]

    def by_hidden(w):
        return w.reshape(NJ, P, KD, P).transpose(3, 0, 2, 1).reshape(P, NJ, KD * P)

    feeds = {
        "x": i["L0_attn_hidden_states"].reshape(TOK, D),
        "w_in": by_chunk(_np.concatenate([xb, z], axis=1)),
        "w_dt": by_chunk(dt),
        "conv_w": i["L0_attn_conv_w"].reshape(NXBC, P, TAPS).transpose(1, 0, 2),
        "conv_b": i["L0_attn_conv_b"].reshape(NXBC, P).T,
        "w_out": by_chunk(i["L0_attn_w_out"].T),
        "gate_w": by_hidden(i["L0_attn_gate_w"]),
        "up_w": by_hidden(i["L0_attn_up_w"]),
        "down_w": by_chunk(i["L0_attn_down_w"].T),
        "ln_w": _np.concatenate([i["L0_attn_ln1_w"].reshape(KD, P).T, i["L0_attn_ln2_w"].reshape(KD, P).T], axis=1),
        "rows": _np.concatenate([i["L0_attn_A_log"], i["L0_attn_dt_bias"], i["L0_attn_dt_bias"], i["L0_attn_D"],
                                 i["L0_ffn_gate"], i["L0_ffn_H_res_base"].reshape(-1), i["L0_ffn_H_pre_base"],
                                 i["L0_ffn_H_post_base"]]).reshape(1, -1),
        "w_logit": by_chunk(_np.concatenate([i["L0_ffn_W_res"], i["L0_ffn_W_pre"], i["L0_ffn_W_post"]]).T),
        "w_branch": i["L0_ffn_W_branch"],
    }
    nc = _bacc.Bacc("TRN2", target_bir_lowering=False, num_devices=1)
    arrays, args = {}, []
    for name, a in feeds.items():
        a = _np.ascontiguousarray(a)
        arrays[f"in_{name}"] = a
        args.append(nc.dram_tensor(f"in_{name}", a.shape, _mybir.dt.from_np(a.dtype), kind="ExternalInput").ap())
    args.append(nc.dram_tensor("out_0", (TOK, D), F32, kind="ExternalOutput").ap())
    mamba_mlp_mhc(nc, *args)
    r = _run(nc, [arrays], core_ids=[0])
    return r.results[0]["out_0"].reshape(BATCHES, TOK // BATCHES, D)
```

```python
from contextlib import ExitStack

import concourse.bass as bass
from concourse import mybir

F32 = mybir.dt.float32
F32R = mybir.dt.float32r
ACT = mybir.ActivationFunctionType
ALU = mybir.AluOpType
AX = mybir.AxisListType

P = 128
D = 512
KD = D // P
H = 4
INTER = 1792
NJ = INTER // P
TOK = 2048
BATCHES = 2
TA = 256
CA = TA // P
NA = TOK // TA
TB = 512
CB = TB // P
NB = TOK // TB
NXBC = 6
TAPS = 4
HALO = TAPS - 1
NPAIR = 5
NLOG = 24
SINK = 50
EPS = 1e-5
EPS_MHC = 1.1920929e-07
MASKED = -1.0e30
SHIFT = 80.0
SCALE_UP = 5.5406223843935098e34
LN1P_TERMS = 8


SU_G = 15
SU_V = 5
CSTEPS = 2 * CB + (2 * CB + 7) + 3 + 6 + 6 * (2 * SINK - 1) + 3 * CB + 16 * (CB - 1) + CB


def at_tile(ap, m):
    if isinstance(m, int):
        return ap[m]
    names = " ".join("bcde"[:len(ap.shape) - 2])
    return ap[bass.ds(m, 1)].rearrange(f"a p {names} -> (a p) {names}") if len(ap.shape) == 3 else \
        ap[bass.ds(m, 1)].squeeze(0)


class Steps:

    def __init__(self, eng, sem, per_tile):
        self.eng, self.sem, self.per_tile, self.k, self.m = eng, sem, per_tile, 0, 0

    def begin(self, m):
        self.m, self.k = m, 0

    def done(self, ins):
        ins.then_inc(self.sem, 1)
        self.k += 1

    def wait(self, back=0):
        self.eng.wait_ge(self.sem, self.m * self.per_tile + (self.k - back))

    def end(self):
        assert self.k == self.per_tile, (self.k, self.per_tile)


def heads(ap):
    return ap.rearrange("p (h q) -> p h q", h=H)


def mamba_mlp_mhc(nc, x, w_in, w_dt, conv_w, conv_b, w_out, gate_w, up_w, down_w, ln_w,
                  rows, w_logit, w_branch, out):
    DT = 18
    h_scr = nc.dram_tensor("h_scr", (NA, P, CA, D), F32, kind="Internal").ap()
    h2t_scr = nc.dram_tensor("h2t_scr", (NA, P, KD, TA), F32, kind="Internal").ap()
    x_a = x.rearrange("(m t p) d -> m p t d", t=CA, p=P)
    x_b = x.rearrange("(m t p) d -> m p t d", t=CB, p=P)
    out_b = out.rearrange("(m t p) d -> m p t d", t=CB, p=P)
    h_scr_b = h_scr.rearrange("(m u) p t d -> m u p t d", u=2)
    h2t_scr_b = h2t_scr.rearrange("(m u) p k q -> m u p k q", u=2)

    with ExitStack() as whole:
        def sem(name):
            return whole.enter_context(nc.semaphore(name))

        def sb(stack, name, shape, dt=F32):
            return stack.enter_context(nc.sbuf_tensor(name, shape, dt))

        def over_raw(stack, name, shape):
            with nc.sbuf_tensor(f"{name}_raw", shape, F32) as raw:
                pass
            return sb(stack, f"{name}_lo", shape, F32R), raw

        ident = sb(whole, "ident", [P, P])
        rows_sb = sb(whole, "rows_sb", [P, 64])
        NR = rows.shape[1]
        ln_sb = sb(whole, "ln_sb", [P, 2 * KD])
        halfc = sb(whole, "halfc", [P, CB])
        idle = sb(whole, "idle", [P, 1])
        epsc = sb(whole, "epsc", [P, CB])
        epsm = sb(whole, "epsm", [P, CB])
        zeroc = sb(whole, "zeroc", [P, 1])
        gate_hi = sb(whole, "gate_hi", [P, NJ, KD * P], F32R)
        gate_lo, gate_raw = over_raw(whole, "gate", [P, NJ, KD * P])
        banks = [whole.enter_context(nc.psum_tensor(f"bank{i}", [P, 512], F32)) for i in range(8)]

        with ExitStack() as st:
            tri = sb(st, "tri", [P, P])
            negmask = sb(st, "negmask", [P, P])
            ones = sb(st, "ones", [P, P])
            keep = sb(st, "keep", [P, NA + 1])
            win_hi = sb(st, "win_hi", [P, KD, 2 * NPAIR * P], F32R)
            win_lo, win_raw = over_raw(st, "win", [P, KD, 2 * NPAIR * P])
            wdt_raw = sb(st, "wdt_raw", [P, KD, H])
            wdt_hi = sb(st, "wdt_hi", [P, KD, H], F32R)
            wdt_lo = sb(st, "wdt_lo", [P, KD, H], F32R)
            wout_sb = sb(st, "wout_sb", [P, H, D])
            convw_sb = sb(st, "convw_sb", [P, NXBC, TAPS])
            convb_sb = sb(st, "convb_sb", [P, NXBC])
            a_rate = sb(st, "a_rate", [P, 2 * H])
            x_t = sb(st, "x_t", [P, 2, CA, D])
            h0 = sb(st, "h0", [P, 2, CA, D])
            u = sb(st, "u", [P, CA, D])
            u_hi = sb(st, "u_hi", [P, KD, TA], F32R)
            u_lo = sb(st, "u_lo", [P, KD, TA], F32R)
            xraw = sb(st, "xraw", [P, NXBC, HALO + TA])
            xbc = sb(st, "xbc", [P, 2, NXBC, TA])
            xbc_tanh = sb(st, "xbc_tanh", [P, NXBC * TA])
            z_tanh = sb(st, "z_tanh", [P, 2, 2 * TA])
            zs = sb(st, "zs", [P, 2, H, TA])
            decay = sb(st, "decay", [P, 512])
            ecs = sb(st, "ecs", [P, 512])
            c_dec = sb(st, "c_dec", [P, 512])
            xw = sb(st, "xw", [P, 512])
            xb_tok = sb(st, "xb_tok", [P, 2 * P + H])
            state = sb(st, "state", [P, 512])
            atri = sb(st, "atri", [P, 512])
            y = sb(st, "y", [P, 512])
            h = sb(st, "h", [P, CA, D])
            h2 = sb(st, "h2", [P, CA, D])
            h2t = sb(st, "h2t", [P, KD, TA])
            st6 = sb(st, "st6", [P, CA, 6])
            mom = sb(st, "mom", [P, CA, 2])
            ve = sb(st, "ve", [P, CA])
            rstd = sb(st, "rstd", [P, CA])
            qv = sb(st, "qv", [P, CA])
            rr = sb(st, "rr", [P, CA])
            ss = sb(st, "ss", [P, CA])
            msq = sb(st, "msq", [P, CA])
            rh = sb(st, "rh", [P, CA])
            pre = sb(st, "pre", [P, 2 * H])
            nabs = sb(st, "nabs", [P, 2 * H])
            e1 = sb(st, "e1", [P, 2 * H])
            s1 = sb(st, "s1", [P, 2 * H])
            s2 = sb(st, "s2", [P, 2 * H])
            acc = sb(st, "acc", [P, 2 * H])
            relu = sb(st, "relu", [P, 2 * H])
            dtv = sb(st, "dtv", [P, 2, 2 * H])
            av = sb(st, "av", [P, 2, 2 * H])
            wt = sb(st, "wt", [P, H])
            wk = sb(st, "wk", [P, H])

            b_tp, b_ip = banks[0:2], banks[2:4]
            b_cs, b_g, b_y, b_misc = banks[4], banks[5], banks[6], banks[7]
            DT0 = 264

            c_in = sem("constants_loaded")
            ln_in = sem("norm_weights_loaded")
            win_in = [sem(f"w_in_chunk{k}_loaded") for k in range(KD)]
            gate_in = sem("gate_weights_loaded")
            ghi = sem("gate_hi_ready")
            glo = sem("gate_lo_ready")
            whi = sem("weight_hi_ready")
            wlo = sem("weight_lo_ready")
            su_v = sem("setup_vector_steps")
            su_g = sem("setup_gpsimd_steps")
            su_a = sem("setup_scalar_steps")
            x_in = [sem("x_loaded_even"), sem("x_loaded_odd")]
            stats = sem("ln_stats_done")
            moments = sem("ln_moments_done")
            scales = sem("ln_scale_steps")
            h0_ready = sem("h0_ready")
            u_ready = sem("u_ready")
            ut_done = sem("u_transposed")
            uh_ready = sem("u_hi_ready")
            ul_ready = sem("u_lo_ready")
            ip_done = sem("in_projection_pair_done")
            xraw_ready = sem("conv_input_ready")
            halo_ready = sem("conv_halo_ready")
            conv_step = sem("conv_steps")
            xtanh = sem("xbc_tanh_ready")
            xbc_ready = sem("xbc_ready")
            ztanh = sem("z_tanh_ready")
            zs_ready = sem("z_silu_ready")
            dtp_done = sem("dt_projected")
            dt_step = sem("dt_steps")
            dt_exp = sem("dt_exp_ready")
            atri_ready = sem("atri_ready")
            misc_done = sem("token_major_done")
            xb_ready = sem("token_major_copied")
            csbc_done = sem("cumsum_done")
            ecs_ready = sem("exp_cumsum_ready")
            diff_done = sem("cumsum_differences_ready")
            e_ready = sem("decay_exps_ready")
            wk_ready = sem("state_weights_ready")
            g_done = sem("scores_done")
            m_ready = sem("decayed_scores_ready")
            cd_ready = sem("c_decayed_ready")
            xw_ready = sem("x_weighted_ready")
            y_done = sem("y_done")
            st_done = sem("chunk_state_done")
            yd_ready = sem("y_plus_dx_ready")
            yg_ready = sem("y_gated_ready")
            s_upd = sem("state_updated")
            state_raw = sem("state_before_reset")
            o_done = sem("out_projection_done")
            h_ready = sem("h_ready")
            ss_ready = sem("h_mean_square_ready")
            rms_step = sem("h_rms_steps")
            h2_ready = sem("h2_ready")
            h2t_done = sem("h2_transposed")
            h2t_ready = sem("h2t_copied")
            a_out = sem("block_a_stored")

            with nc.Block() as block:

                @block.sync
                def _(sp):
                    sp.dma_start(ln_sb[:, :], ln_w).then_inc(ln_in, 16)
                    sp.dma_start(x_t[:, 0, :, :], x_a[0]).then_inc(x_in[0], 16)
                    for k in range(KD):
                        sp.dma_start(win_raw[:, k, :], w_in[:, k, :]).then_inc(win_in[k], 16)
                    sp.dma_start(rows_sb[:, 0:NR], rows.broadcast_to([P, NR])).then_inc(c_in, 16)
                    sp.dma_start(convw_sb[:, :, :], conv_w).then_inc(c_in, 16)
                    sp.dma_start(convb_sb[:, :], conv_b).then_inc(c_in, 16)
                    sp.dma_start(wdt_raw[:, :, :], w_dt).then_inc(c_in, 16)
                    sp.dma_start(x_t[:, 1, :, :], x_a[1]).then_inc(x_in[1], 16)
                    sp.dma_start(wout_sb[:, :, :], w_out).then_inc(c_in, 16)
                    sp.dma_start(gate_raw[:, :, :], gate_w).then_inc(gate_in, 16)

                    def load_x(m, q):
                        sp.wait_ge(u_ready, (m - 2) * CA + CA)
                        sp.dma_start(x_t[:, q, :, :], at_tile(x_a, m)).then_inc(x_in[q], 16)

                    def store(m):
                        sp.wait_ge(h2_ready, m * CA + CA)
                        sp.dma_start(at_tile(h_scr, m), h[:, :, :]).then_inc(a_out, 16)
                        sp.wait_ge(h2t_ready, m * 2 + 2)
                        sp.dma_start(at_tile(h2t_scr, m), h2t[:, :, :]).then_inc(a_out, 16)

                    with sp.Fori(0, NA // 2 - 1) as b:
                        load_x(b * 2 + 2, 0)
                        store(b * 2)
                        load_x(b * 2 + 3, 1)
                        store(b * 2 + 1)
                    store(NA - 2)
                    store(NA - 1)
                    sp.wait_ge(a_out, 32 * NA)

                @block.gpsimd
                def _(pool):
                    g = nc.gpsimd
                    n = 0

                    def after(ins):
                        nonlocal n
                        n += 1
                        ins.then_inc(su_g, 1)
                        pool.wait_ge(su_g, n)

                    after(g.memset(ident[:, :], 0.0))
                    after(g.affine_select(out=ident[:, :], in_=ident[:, :], compare_op=ALU.not_equal,
                                          fill=1.0, base=0, pattern=[[-1, P]], channel_multiplier=1))
                    after(g.memset(ones[:, :], 1.0))
                    after(g.memset(negmask[:, :], 0.0))
                    after(g.affine_select(out=tri[:, :], in_=ones[:, :], compare_op=ALU.is_ge,
                                          fill=0.0, base=0, pattern=[[1, P]], channel_multiplier=-1))
                    after(g.affine_select(out=negmask[:, :], in_=negmask[:, :], compare_op=ALU.is_ge,
                                          fill=MASKED, base=0, pattern=[[1, P]], channel_multiplier=-1))
                    after(g.memset(halfc[:, :], -0.5))
                    after(g.memset(epsc[:, :], EPS))
                    after(g.memset(epsm[:, :], EPS_MHC))
                    after(g.memset(zeroc[:, :], 0.0))
                    after(g.memset(keep[:, :], 1.0))
                    for b in range(0, BATCHES + 1):
                        i = b * NA // BATCHES
                        after(g.memset(keep[:, i:i + 1], 0.0))
                    after(g.memset(state[:, :], 0.0))
                    assert n == SU_G, n
                    g.memset(xraw[:, :, 0:HALO], 0.0).then_inc(halo_ready, 1)

                    def ln_scales(m):
                        s = Steps(pool, scales, 7)
                        s.begin(m)
                        pool.wait_ge(moments, m * CA + CA)
                        pool.wait_ge(u_ready, m * CA)
                        s.done(g.tensor_tensor(ve[:, :], mom[:, :, 1], epsc[:, 0:CA], ALU.add))
                        s.wait()
                        s.done(g.tensor_tensor(rstd[:, :], ve[:, :], halfc[:, 0:CA], ALU.pow))
                        s.wait()
                        s.done(g.tensor_tensor(qv[:, :], rstd[:, :], rstd[:, :], ALU.mult))
                        s.wait()
                        s.done(g.tensor_tensor(qv[:, :], qv[:, :], mom[:, :, 1], ALU.mult))
                        s.wait()
                        s.done(g.tensor_tensor(qv[:, :], qv[:, :], epsc[:, 0:CA], ALU.add))
                        s.wait()
                        s.done(g.tensor_tensor(rr[:, :], qv[:, :], halfc[:, 0:CA], ALU.pow))
                        s.wait()
                        s.done(g.tensor_tensor(rr[:, :], rr[:, :], rstd[:, :], ALU.mult))
                        s.end()

                    def halo(m):
                        pool.wait_ge(conv_step, m * 24)
                        kp = keep[:, bass.ds(m, 1)].rearrange("p (a o) -> p a o", o=1)
                        g.tensor_tensor(xraw[:, :, 0:HALO], xraw[:, :, TA:TA + HALO],
                                        kp.broadcast_to([P, NXBC, HALO]), ALU.mult)\
                            .then_inc(halo_ready, 1)

                    def a_tri(m, q, c):
                        pool.wait_ge(dt_step, m * DT + DT)
                        pool.wait_ge(csbc_done, m * CA + c)
                        a4 = av[:, q, c * H:c * H + H].rearrange("p (h o) -> p h o", o=1)
                        t4 = tri[:, :].rearrange("p (o q) -> p o q", o=1)
                        g.tensor_tensor(heads(atri[:, :]), t4.broadcast_to([P, H, P]),
                                        a4.broadcast_to([P, H, P]), ALU.mult).then_inc(atri_ready, 1)

                    def c_decayed(m, q, c):
                        pool.wait_ge(ecs_ready, m * CA + c + 1)
                        pool.wait_ge(xbc_ready, m + 1)
                        pool.wait_ge(y_done, m * CA + c)
                        g.tensor_tensor(heads(c_dec[:, :]), xbc[:, q, 2:6, c * P:c * P + P],
                                        heads(ecs[:, :]), ALU.mult).then_inc(cd_ready, 1)

                    def x_weighted(m, c):
                        pool.wait_ge(wk_ready, m * CA + c + 1)
                        pool.wait_ge(xb_ready, m * CA + c + 1)
                        pool.wait_ge(st_done, m * CA + c)
                        x4 = xb_tok[:, 0:P].rearrange("p (o q) -> p o q", o=1)
                        w4 = wk[:, :].rearrange("p (h o) -> p h o", o=1)
                        g.tensor_tensor(heads(xw[:, :]), x4.broadcast_to([P, H, P]),
                                        w4.broadcast_to([P, H, P]), ALU.mult).then_inc(xw_ready, 1)

                    def h_rms(m):
                        pool.wait_ge(ss_ready, m * CA + CA)
                        pool.wait_ge(h2_ready, m * CA)
                        g.tensor_tensor(msq[:, :], ss[:, :], epsc[:, 0:CA], ALU.add)\
                            .then_inc(rms_step, 1)
                        pool.wait_ge(rms_step, m * 2 + 1)
                        g.tensor_tensor(rh[:, :], msq[:, :], halfc[:, 0:CA], ALU.pow).then_inc(rms_step, 1)

                    def gate_low(m):
                        pool.wait_ge(ghi, m + 1)
                        two = slice(2 * m, 2 * m + 2) if isinstance(m, int) else bass.ds(m * 2, 2)
                        g.tensor_tensor(gate_lo[:, two, :], gate_raw[:, two, :],
                                        gate_hi[:, two, :].bitcast(F32), ALU.subtract).then_inc(glo, 1)

                    def scan(m, q, nxt):
                        if nxt:
                            halo(m + 1)
                        for c in range(CA):
                            a_tri(m, q, c)
                            c_decayed(m, q, c)
                            x_weighted(m, c)
                        h_rms(m)
                        if nxt:
                            gate_low(m)

                    ln_scales(0)
                    ln_scales(1)
                    with pool.Fori(0, NA // 2 - 1) as b:
                        for q in range(2):
                            m = b * 2 + q
                            scan(m, q, True)
                            ln_scales(m + 2)
                    scan(NA - 2, 0, True)
                    scan(NA - 1, 1, False)

                @block.scalar
                def _(act):
                    a = nc.scalar
                    act.wait_ge(ln_in, 16)
                    for k in range(KD):
                        act.wait_ge(win_in[k], 16)
                        a.activation(win_hi[:, k, :], win_raw[:, k, :], ACT.Copy,
                                     scale=ln_sb[:, k:k + 1]).then_inc(whi, 1)
                    act.wait_ge(c_in, 80)
                    for k in range(KD):
                        ins = a.activation(wdt_hi[:, k, :], wdt_raw[:, k, :], ACT.Copy,
                                           scale=ln_sb[:, k:k + 1])
                    ins.then_inc(su_a, 1)
                    a.activation(a_rate[:, 0:H], rows_sb[:, 0:H], ACT.Exp).then_inc(su_a, 1)
                    a.activation(a_rate[:, H:2 * H], rows_sb[:, 0:H], ACT.Exp).then_inc(su_a, 1)

                    def u_high(m):
                        for i in range(2):
                            act.wait_ge(ut_done, m * 2 + i + 1)
                            act.wait_ge(dtp_done, m) if not isinstance(m, int) or m > 0 else None
                            a.copy(u_hi[:, 2 * i:2 * i + 2, :],
                                   b_tp[i][:, :].rearrange("p (k q) -> p k q", k=2)).then_inc(uh_ready, 1)

                    def conv_in(m, g):
                        act.wait_ge(ip_done, m * NPAIR + g + 1)
                        act.wait_ge(halo_ready, m + 1)
                        a.copy(xraw[:, 2 * g:2 * g + 2, HALO:HALO + TA],
                               b_ip[(QOF[0] + g) % 2][:, :].rearrange("p (k q) -> p k q", k=2))\
                            .then_inc(xraw_ready, 1)

                    def z_th(m, q, i):
                        act.wait_ge(ip_done, m * NPAIR + 3 + i + 1)
                        act.wait_ge(zs_ready, m * 2 + i - 1) if not (isinstance(m, int) and m == 0 and i < 1 + 1) else None
                        a.activation(z_tanh[:, i, :], b_ip[(q + 3 + i) % 2][:, :], ACT.Tanh, scale=0.5)\
                            .then_inc(ztanh, 1)

                    def dt_e(m):
                        act.wait_ge(dt_step, m * DT + 2)
                        a.activation(e1[:, :], nabs[:, :], ACT.Exp).then_inc(dt_exp, 1)

                    def xbc_th(m, q):
                        act.wait_ge(conv_step, m * 24 + 24)
                        if not (isinstance(m, int) and m == 0):
                            act.wait_ge(xbc_ready, m)
                        a.activation(xbc_tanh[:, :], xbc[:, q, :, :].rearrange("p c q -> p (c q)"),
                                     ACT.Tanh).then_inc(xtanh, 1)

                    def tok_major(m, c):
                        act.wait_ge(misc_done, m * CA + c + 1)
                        if not (isinstance(m, int) and m * CA + c == 0):
                            act.wait_ge(st_done, m * CA + c)
                        a.copy(xb_tok[:, :], b_misc[:, 0:2 * P + H]).then_inc(xb_ready, 1)

                    def exp_cs(m, c):
                        act.wait_ge(csbc_done, m * CA + c + 1)
                        if not (isinstance(m, int) and m * CA + c == 0):
                            act.wait_ge(cd_ready, m * CA + c)
                            act.wait_ge(s_upd, m * CA + c)
                        a.activation(ecs[:, :], b_cs[:, :], ACT.Exp).then_inc(ecs_ready, 1)

                    def decays(m, c):
                        act.wait_ge(diff_done, m * CA + c + 1)
                        a.activation(wt[:, :], wt[:, :], ACT.Exp).then_inc(e_ready, 1)
                        a.activation(decay[:, :], decay[:, :], ACT.Exp).then_inc(e_ready, 1)

                    def square_sum(m, c):
                        act.wait_ge(h_ready, m * CA + c + 1)
                        if not (isinstance(m, int) and m == 0):
                            act.wait_ge(h2t_done, m * 2)
                            act.wait_ge(rms_step, m * 2)
                        a.activation(h2[:, c, :], h[:, c, :], ACT.Square, scale=float(D) ** -0.5,
                                     accum_out=ss[:, c:c + 1])\
                            .then_inc(ss_ready, 1)

                    def h2t_copy(m):
                        for i in range(2):
                            act.wait_ge(h2t_done, m * 2 + i + 1)
                            if not (isinstance(m, int) and m == 0):
                                act.wait_ge(a_out, m * 32)
                            for k in range(2):
                                ins = a.activation(h2t[:, 2 * i + k, :], b_tp[i][:, k * TA:k * TA + TA],
                                                   ACT.Copy, scale=ln_sb[:, KD + 2 * i + k:KD + 2 * i + k + 1])
                            ins.then_inc(h2t_ready, 1)

                    QOF = [0]
                    def gate_high(m):
                        act.wait_ge(gate_in, 16)
                        two = slice(2 * m, 2 * m + 2) if isinstance(m, int) else bass.ds(m * 2, 2)
                        a.copy(gate_hi[:, two, :], gate_raw[:, two, :]).then_inc(ghi, 1)

                    def front(m, q):
                        QOF[0] = q
                        for g in range(3):
                            conv_in(m, g)
                        for i in range(2):
                            z_th(m, q, i)
                        dt_e(m)
                        xbc_th(m, q)

                    u_high(0)
                    front(0, 0)

                    def body(m, q, nxt):
                        QOF[0] = 1 - q
                        if nxt:
                            u_high(m + 1)
                        tok_major(m, 0)
                        exp_cs(m, 0)
                        decays(m, 0)
                        if nxt:
                            conv_in(m + 1, 0)
                            conv_in(m + 1, 1)
                            conv_in(m + 1, 2)
                        tok_major(m, 1)
                        exp_cs(m, 1)
                        if nxt:
                            z_th(m + 1, 1 - q, 0)
                        decays(m, 1)
                        if nxt:
                            gate_high(m)
                        square_sum(m, 0)
                        if nxt:
                            z_th(m + 1, 1 - q, 1)
                            dt_e(m + 1)
                            xbc_th(m + 1, 1 - q)
                        square_sum(m, 1)
                        h2t_copy(m)

                    with act.Fori(0, NA // 2 - 1) as b:
                        for q in range(2):
                            body(b * 2 + q, q, True)
                    body(NA - 2, 0, True)
                    body(NA - 1, 1, False)

                @block.vector
                def _(dve):
                    v = nc.vector
                    n = 0

                    def after(ins):
                        nonlocal n
                        n += 1
                        ins.then_inc(su_v, 1)
                        dve.wait_ge(su_v, n)


                    def ln_stats(m, q):
                        dve.wait_ge(x_in[q], (m - q) * 8 + 16)
                        for t in range(CA):
                            v.bn_stats(st6[:, t, :], x_t[:, q, t, :]).then_inc(stats, 1)
                        dve.wait_ge(stats, m * CA + CA)
                        v.memset(idle[:, :], 0.0)
                        for t in range(CA):
                            v.bn_aggr(mom[:, t, :], st6[:, t, :]).then_inc(moments, 1)

                    def normalize(m, q):
                        dve.wait_ge(scales, m * 7 + 7)
                        if not (isinstance(m, int) and m == 0):
                            dve.wait_ge(ut_done, m * 2)
                        for t in range(CA):
                            v.tensor_scalar(h0[:, q, t, :], x_t[:, q, t, :], mom[:, t, 0:1], rstd[:, t:t + 1],
                                            ALU.subtract, ALU.mult).then_inc(h0_ready, 1)
                        for t in range(CA):
                            v.tensor_scalar(u[:, t, :], x_t[:, q, t, :], mom[:, t, 0:1], rr[:, t:t + 1],
                                            ALU.subtract, ALU.mult).then_inc(u_ready, 1)

                    def u_low(m):
                        for i in range(2):
                            dve.wait_ge(uh_ready, m * 2 + i + 1)
                            v.tensor_tensor(u_lo[:, 2 * i:2 * i + 2, :],
                                            b_tp[i][:, :].rearrange("p (k q) -> p k q", k=2),
                                            u_hi[:, 2 * i:2 * i + 2, :].bitcast(F32), ALU.subtract)\
                                .then_inc(ul_ready, 1)

                    def conv(m, q, g):
                        dve.wait_ge(xraw_ready, m * 3 + g + 1)
                        dve.wait_ge(halo_ready, m + 1)
                        s = Steps(dve, conv_step, 24)
                        s.begin(m)
                        s.k = 8 * g
                        for tap in range(TAPS - 1, -1, -1):
                            for ch in (2 * g, 2 * g + 1):
                                src = xraw[:, ch, tap:tap + TA]
                                if tap == TAPS - 1:
                                    s.done(v.tensor_scalar(xbc[:, q, ch, :], src, convw_sb[:, ch, tap:tap + 1],
                                                           convb_sb[:, ch:ch + 1], ALU.mult, ALU.add))
                                else:
                                    s.wait(1)
                                    s.done(v.scalar_tensor_tensor(xbc[:, q, ch, :], src,
                                                                  convw_sb[:, ch, tap:tap + 1],
                                                                  xbc[:, q, ch, :], ALU.mult, ALU.add))

                    def xbc_silu(m, q):
                        dve.wait_ge(xtanh, m + 1)
                        flat = xbc[:, q, :, :].rearrange("p c q -> p (c q)")
                        v.scalar_tensor_tensor(flat, xbc_tanh[:, :], 1.0, flat, ALU.add, ALU.mult)\
                            .then_inc(xbc_ready, 1)

                    def z_silu(m, q, i):
                        dve.wait_ge(ztanh, m * 2 + i + 1)
                        v.scalar_tensor_tensor(zs[:, q, 2 * i:2 * i + 2, :].rearrange("p c q -> p (c q)"),
                                               z_tanh[:, i, :], 1.0, b_ip[(q + 3 + i) % 2][:, :],
                                               ALU.add, ALU.mult).then_inc(zs_ready, 1)

                    def dt_chain(m, q):
                        s = Steps(dve, dt_step, DT)
                        s.begin(m)
                        dve.wait_ge(dtp_done, m + 1)
                        b2 = rows_sb[:, H:3 * H]
                        s.done(v.tensor_tensor(pre[:, :], b_misc[:, DT0:DT0 + 2 * H], b2, ALU.add))
                        s.wait()
                        s.done(v.scalar_tensor_tensor(nabs[:, :], pre[:, :], -1.0, pre[:, :], ALU.mult, ALU.min))
                        dve.wait_ge(dt_exp, m + 1)
                        s.done(v.tensor_scalar(s1[:, :], e1[:, :], 2.0, None, ALU.add))
                        s.wait()
                        s.done(v.reciprocal(s1[:, :], s1[:, :]))
                        s.wait()
                        s.done(v.tensor_tensor(s1[:, :], s1[:, :], e1[:, :], ALU.mult))
                        s.wait()
                        s.done(v.tensor_tensor(s2[:, :], s1[:, :], s1[:, :], ALU.mult))
                        s.wait()
                        s.done(v.tensor_scalar(acc[:, :], s2[:, :], 1.0 / (2 * LN1P_TERMS + 1), None, ALU.mult))
                        for k in range(LN1P_TERMS - 1, 0, -1):
                            s.wait()
                            s.done(v.scalar_tensor_tensor(acc[:, :], acc[:, :], 1.0 / (2 * k + 1), s2[:, :],
                                                          ALU.add, ALU.mult))
                        s.wait()
                        s.done(v.scalar_tensor_tensor(acc[:, :], acc[:, :], 1.0, s1[:, :], ALU.add, ALU.mult))
                        s.done(v.tensor_scalar(relu[:, :], pre[:, :], 0.0, None, ALU.max))
                        s.wait()
                        s.done(v.scalar_tensor_tensor(dtv[:, q, :], acc[:, :], 2.0, relu[:, :], ALU.mult, ALU.add))
                        s.wait()
                        s.done(v.tensor_tensor(av[:, q, :], dtv[:, q, :], a_rate[:, :], ALU.mult))
                        s.end()

                    def differences(m, c):
                        dve.wait_ge(ecs_ready, m * CA + c + 1)
                        dve.wait_ge(xb_ready, m * CA + c + 1)
                        if not (isinstance(m, int) and m * CA + c == 0):
                            dve.wait_ge(y_done, m * CA + c)
                        for hh in range(H):
                            v.scalar_tensor_tensor(decay[:, hh * P:hh * P + P], b_cs[:, hh * P:hh * P + P],
                                                   xb_tok[:, 2 * P + hh:2 * P + hh + 1], negmask[:, :],
                                                   ALU.subtract, ALU.add)
                        v.tensor_tensor(wt[:, :], heads(b_cs[:, :])[:, :, P - 1], xb_tok[:, 2 * P:2 * P + H],
                                        ALU.subtract).then_inc(diff_done, 1)

                    def decay_scores(m, q, c):
                        dve.wait_ge(e_ready, (m * CA + c) * 2 + 1)
                        if not (isinstance(m, int) and m * CA + c == 0):
                            dve.wait_ge(xw_ready, m * CA + c)
                        v.tensor_tensor(wk[:, :], wt[:, :], dtv[:, q, c * H:c * H + H], ALU.mult)\
                            .then_inc(wk_ready, 1)
                        dve.wait_ge(e_ready, (m * CA + c) * 2 + 2)
                        dve.wait_ge(g_done, m * CA + c + 1)
                        for hh in range(H):
                            ins = v.scalar_tensor_tensor(decay[:, hh * P:hh * P + P], b_g[:, hh * P:hh * P + P],
                                                         dtv[:, q, c * H + hh:c * H + hh + 1],
                                                         decay[:, hh * P:hh * P + P], ALU.mult, ALU.mult)
                        ins.then_inc(m_ready, 1)

                    def y_gate(m, q, c):
                        dve.wait_ge(y_done, m * CA + c + 1)
                        if not (isinstance(m, int) and m * CA + c == 0):
                            dve.wait_ge(o_done, m * CA + c)
                        for hh in range(H):
                            ins = v.scalar_tensor_tensor(y[:, hh * P:hh * P + P], xbc[:, q, 0, c * P:c * P + P],
                                                         rows_sb[:, 3 * H + hh:3 * H + hh + 1],
                                                         b_y[:, hh * P:hh * P + P], ALU.mult, ALU.add)
                        ins.then_inc(yd_ready, 1)
                        dve.wait_ge(yd_ready, m * CA + c + 1)
                        v.tensor_tensor(heads(y[:, :]), heads(y[:, :]), zs[:, q, :, c * P:c * P + P], ALU.mult)\
                            .then_inc(yg_ready, 1)

                    def state_update(m, q, c):
                        dve.wait_ge(st_done, m * CA + c + 1)
                        dve.wait_ge(cd_ready, m * CA + c + 1)
                        last = q == 1 and c == CA - 1
                        for hh in range(H):
                            ins = v.scalar_tensor_tensor(state[:, hh * P:hh * P + P], state[:, hh * P:hh * P + P],
                                                         ecs[:, hh * P + P - 1:hh * P + P],
                                                         b_cs[:, hh * P:hh * P + P], ALU.mult, ALU.add)
                        if last:
                            ins.then_inc(state_raw, 1)
                            dve.wait_ge(state_raw, (m + 1) // 2 if isinstance(m, int) else QH[0] + 1)
                            ins = v.tensor_scalar(state[:, :], state[:, :], keep[:, bass.ds(m + 1, 1)], None,
                                                  ALU.mult)
                        ins.then_inc(s_upd, 1)

                    def residual(m, q, c):
                        dve.wait_ge(o_done, m * CA + c + 1)
                        if not (isinstance(m, int) and m == 0):
                            dve.wait_ge(a_out, m * 32)
                        v.tensor_tensor(h[:, c, :], b_g[:, :], h0[:, q, c, :], ALU.add).then_inc(h_ready, 1)

                    def h2_norm(m):
                        dve.wait_ge(rms_step, m * 2 + 2)
                        for t in range(CA):
                            v.tensor_scalar(h2[:, t, :], h[:, t, :], rh[:, t:t + 1], None, ALU.mult)\
                                .then_inc(h2_ready, 1)

                    QH = [0]
                    ln_stats(0, 0)
                    normalize(0, 0)
                    dve.wait_ge(ln_in, 16)
                    for k in range(KD):
                        dve.wait_ge(whi, k + 1)
                        v.scalar_tensor_tensor(win_lo[:, k, :], win_raw[:, k, :], ln_sb[:, k:k + 1],
                                               win_hi[:, k, :].bitcast(F32),
                                               ALU.mult, ALU.subtract).then_inc(wlo, 1)
                    u_low(0)
                    dve.wait_ge(su_a, 1)
                    for k in range(KD):
                        ins = v.scalar_tensor_tensor(wdt_lo[:, k, :], wdt_raw[:, k, :], ln_sb[:, k:k + 1],
                                                     wdt_hi[:, k, :].bitcast(F32), ALU.mult, ALU.subtract)
                    after(ins)
                    dve.wait_ge(c_in, 80)
                    dve.wait_ge(su_a, 3)
                    after(v.tensor_scalar(a_rate[:, :], a_rate[:, :], -1.0, None, ALU.mult))
                    after(v.tensor_scalar(convw_sb[:, :, :].rearrange("p c t -> p (c t)"),
                                          convw_sb[:, :, :].rearrange("p c t -> p (c t)"), 0.5, None, ALU.mult))
                    after(v.tensor_scalar(convb_sb[:, :], convb_sb[:, :], 0.5, None, ALU.mult))
                    after(v.tensor_scalar(wout_sb[:, :, :].rearrange("p h d -> p (h d)"),
                                          wout_sb[:, :, :].rearrange("p h d -> p (h d)"), 0.5, None, ALU.mult))
                    assert n == SU_V
                    ln_stats(1, 1)
                    normalize(1, 1)
                    for g in range(3):
                        conv(0, 0, g)
                    z_silu(0, 0, 0)
                    z_silu(0, 0, 1)
                    dt_chain(0, 0)
                    xbc_silu(0, 0)

                    def body(m, q, nxt, nxt2):
                        if nxt:
                            u_low(m + 1)
                        differences(m, 0)
                        decay_scores(m, q, 0)
                        if nxt:
                            conv(m + 1, 1 - q, 0)
                        y_gate(m, q, 0)
                        state_update(m, q, 0)
                        if nxt:
                            conv(m + 1, 1 - q, 1)
                        residual(m, q, 0)
                        differences(m, 1)
                        decay_scores(m, q, 1)
                        if nxt:
                            conv(m + 1, 1 - q, 2)
                            z_silu(m + 1, 1 - q, 0)
                        y_gate(m, q, 1)
                        state_update(m, q, 1)
                        if nxt:
                            z_silu(m + 1, 1 - q, 1)
                            dt_chain(m + 1, 1 - q)
                            xbc_silu(m + 1, 1 - q)
                        residual(m, q, 1)
                        if nxt2:
                            ln_stats(m + 2, q)
                        h2_norm(m)
                        if nxt2:
                            normalize(m + 2, q)

                    with dve.Fori(0, NA // 2 - 1) as b:
                        QH[0] = b
                        for q in range(2):
                            body(b * 2 + q, q, True, True)
                    body(NA - 2, 0, True, False)
                    body(NA - 1, 1, False, False)

                @block.tensor
                def _(pe):
                    t_ = nc.tensor

                    def u_transpose(m):
                        pe.wait_ge(u_ready, m * CA + CA)
                        if not (isinstance(m, int) and m == 0):
                            pe.wait_ge(ul_ready, m * 2)
                            if not (isinstance(m, int) and m == 1):
                                pe.wait_ge(h2t_ready, (m - 1) * 2)
                        for i in range(2):
                            for k in range(2):
                                for t in range(CA):
                                    ins = t_.transpose(b_tp[i][:, k * TA + t * P:k * TA + t * P + P],
                                                       u[:, t, (2 * i + k) * P:(2 * i + k + 1) * P], ident[:, :])
                            ins.then_inc(ut_done, 1)

                    def in_proj(m, q, g):
                        if g == 0:
                            pe.wait_ge(ul_ready, m * 2 + 2)
                        if g < 2:
                            if not (isinstance(m, int) and m == 0):
                                pe.wait_ge(zs_ready, m * 2 - 1 + g)
                        else:
                            pe.wait_ge(xraw_ready, m * 3 + g - 1)
                        bank = b_ip[(q + g) % 2]
                        for c in range(2):
                            col = (2 * g + c) * P
                            n = 0
                            for k in range(KD):
                                for wv, uv in ((win_hi, u_hi), (win_lo, u_hi), (win_hi, u_lo)):
                                    ins = t_.matmul(bank[:, c * TA:c * TA + TA], wv[:, k, col:col + P], uv[:, k, :],
                                                    start=(n == 0), stop=(n == 3 * KD - 1))
                                    n += 1
                        ins.then_inc(ip_done, 1)

                    def dt_proj(m):
                        if not (isinstance(m, int) and m == 0):
                            pe.wait_ge(xb_ready, m * CA)
                        for t in range(CA):
                            n = 0
                            for k in range(KD):
                                for wv, uv in ((wdt_hi, u_hi), (wdt_lo, u_hi), (wdt_hi, u_lo)):
                                    ins = t_.matmul(b_misc[:, DT0 + t * H:DT0 + t * H + H],
                                                    uv[:, k, t * P:t * P + P], wv[:, k, :],
                                                    start=(n == 0), stop=(n == 3 * KD - 1))
                                    n += 1
                        ins.then_inc(dtp_done, 1)

                    def scan_in(m, q, c):
                        pe.wait_ge(dt_step, m * DT + DT)
                        pe.wait_ge(xbc_ready, m + 1)
                        if not (isinstance(m, int) and m * CA + c == 0):
                            pe.wait_ge(xb_ready, m * CA + c)
                            pe.wait_ge(s_upd, m * CA + c)
                        tok = slice(c * P, c * P + P)
                        t_.transpose(b_misc[:, 0:P], xbc[:, q, 0, tok], ident[:, :])
                        t_.transpose(b_misc[:, P:2 * P], xbc[:, q, 1, tok], ident[:, :])
                        t_.matmul(b_misc[:, 2 * P:2 * P + H], tri[:, :], av[:, q, c * H:c * H + H],
                                  start=True, stop=True).then_inc(misc_done, 1)
                        pe.wait_ge(atri_ready, m * CA + c + 1)
                        t_.matmul(b_cs[:, :], ones[:, :], atri[:, :], start=True, stop=True).then_inc(csbc_done, 1)
                        if not (isinstance(m, int) and m * CA + c == 0):
                            pe.wait_ge(h_ready, m * CA + c)
                        t_.matmul(b_g[:, :], xbc[:, q, 1, tok], xbc[:, q, 2:6, tok],
                                  start=True, stop=True).then_inc(g_done, 1)

                    def scan_out(m, c):
                        pe.wait_ge(xw_ready, m * CA + c + 1)
                        pe.wait_ge(diff_done, m * CA + c + 1)
                        pe.wait_ge(m_ready, m * CA + c + 1)
                        pe.wait_ge(cd_ready, m * CA + c + 1)
                        if not (isinstance(m, int) and m * CA + c == 0):
                            pe.wait_ge(yd_ready, m * CA + c)
                            pe.wait_ge(s_upd, m * CA + c)
                        t_.matmul(b_y[:, :], xb_tok[:, 0:P], decay[:, :], start=True, stop=False)
                        for hh in range(H):
                            ins = t_.matmul(b_y[:, hh * P:hh * P + P], state[:, hh * P:hh * P + P],
                                            c_dec[:, hh * P:hh * P + P], start=False, stop=(hh == H - 1))
                        ins.then_inc(y_done, 1)
                        t_.matmul(b_cs[:, :], xb_tok[:, P:2 * P], xw[:, :], start=True, stop=True)\
                            .then_inc(st_done, 1)

                    def out_proj(m, c):
                        pe.wait_ge(yg_ready, m * CA + c + 1)
                        for hh in range(H):
                            ins = t_.matmul(b_g[:, :], y[:, hh * P:hh * P + P], wout_sb[:, hh, :],
                                            start=(hh == 0), stop=(hh == H - 1))
                        ins.then_inc(o_done, 1)

                    def h2_transpose(m):
                        pe.wait_ge(h2_ready, m * CA + CA)
                        for i in range(2):
                            for k in range(2):
                                for t in range(CA):
                                    ins = t_.transpose(b_tp[i][:, k * TA + t * P:k * TA + t * P + P],
                                                       h2[:, t, (2 * i + k) * P:(2 * i + k + 1) * P], ident[:, :])
                            ins.then_inc(h2t_done, 1)

                    pe.wait_ge(su_g, SU_G)
                    u_transpose(0)
                    pe.wait_ge(wlo, KD)
                    for g in range(NPAIR):
                        in_proj(0, 0, g)
                    pe.wait_ge(su_v, SU_V)
                    dt_proj(0)

                    def body(m, q, nxt):
                        if nxt:
                            u_transpose(m + 1)
                        scan_in(m, q, 0)
                        if nxt:
                            in_proj(m + 1, 1 - q, 0)
                            in_proj(m + 1, 1 - q, 1)
                        scan_out(m, 0)
                        if nxt:
                            in_proj(m + 1, 1 - q, 2)
                        out_proj(m, 0)
                        scan_in(m, q, 1)
                        if nxt:
                            in_proj(m + 1, 1 - q, 3)
                        scan_out(m, 1)
                        if nxt:
                            in_proj(m + 1, 1 - q, 4)
                            dt_proj(m + 1)
                        out_proj(m, 1)
                        h2_transpose(m)

                    with pe.Fori(0, NA // 2 - 1) as b:
                        for q in range(2):
                            body(b * 2 + q, q, True)
                    body(NA - 2, 0, True)
                    body(NA - 1, 1, False)

        with ExitStack() as st:
            up_hi = sb(st, "up_hi", [P, NJ, KD * P], F32R)
            up_lo, up_raw = over_raw(st, "up", [P, NJ, KD * P])
            down_sb = sb(st, "down_sb", [P, NJ, D])
            h2_raw = sb(st, "h2_raw", [P, KD, TB])
            h2_hi = sb(st, "h2_hi", [P, KD, TB], F32R)
            h2_lo = sb(st, "h2_lo", [P, KD, TB], F32R)
            hm = sb(st, "hm", [P, CB, D])
            x1 = sb(st, "x1", [P, CB, D])
            xn = sb(st, "xn", [P, CB, D])
            th = sb(st, "th", [P, TB])
            glu = sb(st, "glu", [P, 2, TB])
            tr = sb(st, "tr", [P, D])
            prod = tr
            mix = sb(st, "mix", [P, CB, D])
            wlog = sb(st, "wlog", [P, KD, NLOG])
            wbr = sb(st, "wbr", [P, P])
            sg = sb(st, "sg", [P, 4])
            eye = sb(st, "eye", [P, 4, 2, 4])
            b6 = sb(st, "b6", [P, CB, 6])
            bm = sb(st, "bm", [P, CB, 2])
            bv = sb(st, "bv", [P, CB])
            br = sb(st, "br", [P, CB])
            bq = sb(st, "bq", [P, CB])
            bx = sb(st, "bx", [P, CB])
            f6 = sb(st, "f6", [P, CB, 6])
            fm = sb(st, "fm", [P, CB, 2])
            fv = sb(st, "fv", [P, CB])
            fr = sb(st, "fr", [P, CB])
            fs = sb(st, "fs", [P, CB])
            lg = sb(st, "lg", [P, CB, NLOG])
            sm = sb(st, "sm", [P, CB, 8])
            smx = sb(st, "smx", [P, CB, 2])
            zl = sb(st, "zl", [P, 2, 4, 2, 4])
            ze = sb(st, "ze", [P, 2, 4, 2, 4])
            pm = sb(st, "pm", [P, 2, 4, 2, 4])
            rowv = sb(st, "rowv", [P, 2, 4, 2])
            colv = sb(st, "colv", [P, 2, 2, 4])

            b_gate, b_up = banks[0], banks[1]
            b_down = banks[2:6]
            b_tr, b_lg = banks[6], banks[7]

            k_in = sem("b_constants_loaded")
            UP_LOADS = [(0, 1), (1, 2), (2, 4), (4, 8), (8, NJ)]
            DOWN_LOADS = [(0, 2), (2, NJ)]
            ur_in = [sem(f"up_load{i}_done") for i in range(len(UP_LOADS))]
            dn_in = [sem(f"down_load{i}_done") for i in range(len(DOWN_LOADS))]
            up_h = sem("up_hi_ready")
            up_l = sem("up_lo_ready")
            b_su = sem("b_setup_steps")
            h2_in = sem("h2t_loaded")
            hm_in = sem("h_loaded")
            xb_in = sem("x_again_loaded")
            hh_ready = sem("h2_hi_ready")
            hl_ready = sem("h2_lo_ready")
            gate_done = sem("gate_product_done")
            up_done = sem("up_product_done")
            th_ready = sem("gate_silu_ready")
            glu_ready = sem("glu_ready")
            down_done = sem("down_product_done")
            mo_ready = sem("mlp_output_ready")
            c_step = sem("mhc_vector_steps")
            mom_b = sem("mlp_output_moments_ready")
            lnb = sem("mlp_output_scale_ready")
            nb_ready = sem("mlp_output_normalized")
            x1_ready = sem("x1_ready")
            mom_x = sem("x1_moments_ready")
            lnx = sem("x1_scale_steps")
            xn_ready = sem("streams_ready")
            xt_done = sem("streams_transposed")
            xt_ready = sem("streams_transpose_copied")
            lg_done = sem("logits_done")
            sm_in = sem("softmax_inputs_ready")
            sm_exp = sem("softmax_exps_ready")
            z_in = sem("sinkhorn_inputs_ready")
            z_exp = sem("sinkhorn_exps_ready")
            xp_ready = sem("x_pre_ready")
            xpt_done = sem("x_pre_transposed")
            xpt_ready = sem("x_pre_transpose_copied")
            br_done = sem("branch_product_done")
            mom_f = sem("mix_moments_ready")
            lnf = sem("mix_scale_ready")
            fin_n = sem("mix_normalized")
            fin = sem("tile_output_ready")
            hres_ready = sem("stream_mixers_ready")
            ym_ready = sem("branch_share_ready")
            pool_mix = sem("gpsimd_mixing_steps")
            b_out = sem("outputs_stored")

            with nc.Block() as block:

                @block.sync
                def _(sp):
                    def load_h2(m):
                        if not (isinstance(m, int) and m == 0):
                            sp.wait_ge(hl_ready, m * KD)
                        for uu in range(2):
                            sp.dma_start(h2_raw[:, :, uu * TA:uu * TA + TA],
                                         at_tile(h2t_scr_b[:, uu], m)).then_inc(h2_in, 16)

                    def load_hm(m):
                        if not (isinstance(m, int) and m == 0):
                            sp.wait_ge(x1_ready, m * CB)
                        for uu in range(2):
                            sp.dma_start(hm[:, 2 * uu:2 * uu + 2, :], at_tile(h_scr_b[:, uu], m))\
                                .then_inc(hm_in, 16)

                    def load_x(m):
                        if not (isinstance(m, int) and m == 0):
                            sp.wait_ge(fin, m * CB)
                        sp.dma_start(x1[:, :, :], at_tile(x_b, m)).then_inc(xb_in, 16)

                    def store(m):
                        for t in range(CB):
                            sp.wait_ge(fin, m * CB + t + 1)
                            sp.dma_start(at_tile(out_b[:, :, t], m), mix[:, t, :]).then_inc(b_out, 16)

                    def load_up(i):
                        j0, j1 = UP_LOADS[i]
                        sp.dma_start(up_raw[:, j0:j1, :], up_w[:, j0:j1, :]).then_inc(ur_in[i], 16)

                    def load_down(i):
                        j0, j1 = DOWN_LOADS[i]
                        sp.dma_start(down_sb[:, j0:j1, :], down_w[:, j0:j1, :]).then_inc(dn_in[i], 16)

                    load_h2(0)
                    for i in range(3):
                        load_up(i)
                    load_down(0)
                    load_up(3)
                    load_down(1)
                    load_up(4)
                    sp.dma_start(wlog[:, :, :], w_logit).then_inc(k_in, 16)
                    sp.dma_start(wbr[:, :], w_branch).then_inc(k_in, 16)
                    load_hm(0)
                    load_x(0)
                    load_h2(1)
                    with sp.Fori(1, NB - 1) as m:
                        load_hm(m)
                        load_h2(m + 1)
                        store(m - 1)
                        load_x(m)
                    load_hm(NB - 1)
                    store(NB - 2)
                    load_x(NB - 1)
                    store(NB - 1)
                    sp.wait_ge(b_out, 16 * TOK // P)

                @block.gpsimd
                def _(pool):
                    g = nc.gpsimd

                    def out_scale(m):
                        pool.wait_ge(mom_b, m * CB + CB)
                        g.tensor_tensor(bv[:, :], bm[:, :, 1], epsc[:, :], ALU.add).then_inc(lnb, 1)
                        pool.wait_ge(lnb, m * 2 + 1)
                        g.tensor_tensor(br[:, :], bv[:, :], halfc[:, :], ALU.pow).then_inc(lnb, 1)

                    def x1_add(m):
                        pool.wait_ge(xb_in, m * 16 + 16)
                        for t in range(CB):
                            pool.wait_ge(nb_ready, m * CB + t + 1)
                            g.tensor_tensor(x1[:, t, :], x1[:, t, :], hm[:, t, :], ALU.add).then_inc(x1_ready, 1)

                    def x1_scales(m):
                        s = Steps(pool, lnx, 6)
                        s.begin(m)
                        pool.wait_ge(mom_x, m * CB + CB)
                        s.done(g.tensor_tensor(bv[:, :], bm[:, :, 1], epsc[:, :], ALU.add))
                        s.wait()
                        s.done(g.tensor_tensor(br[:, :], bv[:, :], halfc[:, :], ALU.pow))
                        s.wait()
                        s.done(g.tensor_tensor(bq[:, :], br[:, :], br[:, :], ALU.mult))
                        s.wait()
                        s.done(g.tensor_tensor(bq[:, :], bq[:, :], bm[:, :, 1], ALU.mult))
                        s.wait()
                        s.done(g.tensor_tensor(bq[:, :], bq[:, :], epsm[:, :], ALU.add))
                        s.wait()
                        s.done(g.tensor_tensor(bx[:, :], bq[:, :], halfc[:, :], ALU.pow))
                        s.end()

                    def pool_mixing(m):
                        t = CB - 1
                        s = Steps(pool, pool_mix, 8)
                        s.begin(m)
                        pool.wait_ge(hres_ready, m * 2 + 2)
                        pool.wait_ge(ym_ready, m * CB + CB)
                        for jj in range(4):
                            hcol = pm[:, t // 2, :, t % 2, jj:jj + 1].broadcast_to([P, 4, P])
                            xj = xn[:, t, jj * P:jj * P + P].rearrange("p (o q) -> p o q", o=1).broadcast_to([P, 4, P])
                            if jj > 0:
                                s.wait()
                            s.done(g.tensor_tensor(heads(prod[:, :]), xj, hcol, ALU.mult))
                            s.wait()
                            s.done(g.tensor_tensor(mix[:, t, :], mix[:, t, :], prod[:, :], ALU.add))
                        s.end()

                    def mix_scale(m, t):
                        i = m * CB + t
                        pool.wait_ge(mom_f, i + 1)
                        g.tensor_tensor(fv[:, t:t + 1], fm[:, t, 1:2], epsc[:, 0:1], ALU.add)\
                            .then_inc(lnf, 1)
                        pool.wait_ge(lnf, i * 4 + 1)
                        g.tensor_tensor(fr[:, t:t + 1], fv[:, t:t + 1], halfc[:, 0:1], ALU.pow)\
                            .then_inc(lnf, 1)
                        pool.wait_ge(lnf, i * 4 + 2)
                        g.tensor_tensor(fs[:, t:t + 1], fm[:, t, 0:1], fr[:, t:t + 1], ALU.mult).then_inc(lnf, 1)
                        pool.wait_ge(lnf, i * 4 + 3)
                        g.tensor_tensor(fs[:, t:t + 1], zeroc[:, 0:1], fs[:, t:t + 1], ALU.subtract)\
                            .then_inc(lnf, 1)

                    def final_add(m, t):
                        pool.wait_ge(fin_n, m * CB + t + 1)
                        g.tensor_tensor(mix[:, t, :], mix[:, t, :], x1[:, t, :], ALU.add)\
                            .then_inc(fin, 1)

                    def mhc(m):
                        out_scale(m)
                        x1_add(m)
                        x1_scales(m)
                        pool_mixing(m)
                        for t in range(CB):
                            mix_scale(m, t)
                            if t > 0:
                                final_add(m, t - 1)
                        final_add(m, CB - 1)

                    with pool.Fori(0, NB) as m:
                        mhc(m)

                @block.scalar
                def _(act):
                    a = nc.scalar
                    def up_high(j):
                        for i, (j0, j1) in enumerate(UP_LOADS):
                            if j0 == j:
                                act.wait_ge(ur_in[i], 16)
                        a.copy(up_hi[:, j, :], up_raw[:, j, :]).then_inc(up_h, 1)

                    a.activation(sg[:, 0:1], rows_sb[:, 16:17], ACT.Exp, scale=-1.0).then_inc(b_su, 1)
                    act.wait_ge(h2_in, 32)
                    for k in range(KD):
                        a.copy(h2_hi[:, k, :], h2_raw[:, k, :]).then_inc(hh_ready, 1)
                    up_high(0)
                    up_high(1)

                    def h2_high(m):
                        act.wait_ge(h2_in, m * 32 + 32)
                        act.wait_ge(up_done, m * NJ)
                        for k in range(KD):
                            a.copy(h2_hi[:, k, :], h2_raw[:, k, :]).then_inc(hh_ready, 1)

                    def gate_silu(m, j):
                        act.wait_ge(gate_done, m * NJ + j + 1)
                        if not (isinstance(m, int) and m * NJ + j == 0):
                            act.wait_ge(glu_ready, m * NJ + j)
                        a.activation(th[:, :], b_gate[:, :], ACT.Silu).then_inc(th_ready, 1)

                    def tr_copy(m, t):
                        i = m * CB + t
                        act.wait_ge(xt_done, i + 1)
                        if not (isinstance(m, int) and i == 0):
                            act.wait_ge(lg_done, i)
                        a.copy(tr[:, :], b_tr[:, :]).then_inc(xt_ready, 1)

                    def softmax_exp(m):
                        act.wait_ge(sm_in, m + 1)
                        a.activation(sm[:, :, :], sm[:, :, :], ACT.Exp).then_inc(sm_exp, 1)

                    def sink_exp(m):
                        act.wait_ge(z_in, m * 2 + 2)
                        a.activation(ze[:, :, :, :], zl[:, :, :, :], ACT.Exp).then_inc(z_exp, 1)
                        act.wait_ge(z_in, m * 2 + 2)
                        a.activation(pm[:, :, :, :], pm[:, :, :, :], ACT.Exp).then_inc(z_exp, 1)

                    def xpre_copy(m, t):
                        i = m * CB + t
                        act.wait_ge(xpt_done, i + 1)
                        if t > 0:
                            act.wait_ge(br_done, i)
                        else:
                            act.wait_ge(lg_done, i + CB)
                        a.copy(tr[:, 0:P], b_lg[:, 0:P]).then_inc(xpt_ready, 1)

                    def branch_share(m, t):
                        i = m * CB + t
                        act.wait_ge(br_done, i + 1)
                        for ii in range(4):
                            ins = a.activation(mix[:, t, ii * P:ii * P + P], b_lg[:, P:2 * P], ACT.Copy,
                                               scale=sm[:, t, 4 + ii:5 + ii])
                        ins.then_inc(ym_ready, 1)

                    def mix_norm(m, t):
                        i = m * CB + t
                        act.wait_ge(lnf, i * 4 + 4)
                        a.activation(mix[:, t, :], mix[:, t, :], ACT.Identity, bias=fs[:, t:t + 1],
                                     scale=fr[:, t:t + 1]).then_inc(fin_n, 1)

                    def body(m, mlp, mhc, c):
                        for j in range(NJ):
                            if mhc and j == 2:
                                tr_copy(c, 0)
                                tr_copy(c, 1)
                            if mlp and not mhc and j + 2 < NJ:
                                up_high(j + 2)
                            if mlp:
                                gate_silu(m, j)
                            if mhc:
                                if j == 2:
                                    tr_copy(c, 2)
                                    tr_copy(c, 3)
                                    softmax_exp(c)
                                    sink_exp(c)
                                if 5 <= j < 5 + CB:
                                    xpre_copy(c, j - 5)
                                    branch_share(c, j - 5)
                        if mlp:
                            h2_high(m + 1) if not isinstance(m, int) or m < NB - 1 else None
                        if mhc:
                            for t in range(CB):
                                mix_norm(c, t)

                    body(0, True, False, 0)
                    with act.Fori(1, NB - 1) as m:
                        body(m, True, True, m - 1)
                    body(NB - 1, True, True, NB - 2)
                    body(0, False, True, NB - 1)

                @block.vector
                def _(dve):
                    v = nc.vector
                    PER = CSTEPS

                    def up_low(j):
                        dve.wait_ge(up_h, j + 1)
                        v.tensor_tensor(up_lo[:, j, :], up_raw[:, j, :],
                                        up_hi[:, j, :].bitcast(F32), ALU.subtract).then_inc(up_l, 1)

                    for k in range(KD):
                        dve.wait_ge(hh_ready, k + 1)
                        v.tensor_tensor(h2_lo[:, k, :], h2_raw[:, k, :], h2_hi[:, k, :].bitcast(F32),
                                        ALU.subtract).then_inc(hl_ready, 1)
                    up_low(0)
                    up_low(1)
                    n = 1

                    def after(ins):
                        nonlocal n
                        n += 1
                        ins.then_inc(b_su, 1)
                        dve.wait_ge(b_su, n)

                    dve.wait_ge(b_su, 1)
                    after(v.tensor_scalar(sg[:, 1:2], sg[:, 0:1], 1.0, None, ALU.add))
                    after(v.reciprocal(sg[:, 2:3], sg[:, 1:2]))
                    after(v.tensor_scalar(sg[:, 3:4], sg[:, 2:3], -1.0, 1.0, ALU.mult, ALU.add))
                    after(v.memset(eye[:, :, :, :], 0.0))
                    for i in range(4):
                        after(v.tensor_scalar(eye[:, i, :, i], eye[:, i, :, i], sg[:, 3:4], None, ALU.add))

                    def h2_low(m):
                        for k in range(KD):
                            dve.wait_ge(hh_ready, m * KD + k + 1)
                            v.tensor_tensor(h2_lo[:, k, :], h2_raw[:, k, :], h2_hi[:, k, :].bitcast(F32),
                                            ALU.subtract).then_inc(hl_ready, 1)

                    def gate_up(m, j):
                        i = m * NJ + j
                        dve.wait_ge(th_ready, i + 1)
                        dve.wait_ge(up_done, i + 1)
                        if not (isinstance(m, int) and i < 2):
                            dve.wait_ge(down_done, i - 1)
                        v.tensor_tensor(glu[:, j % 2, :], th[:, :], b_up[:, :], ALU.mult)\
                            .then_inc(glu_ready, 1)

                    def mlp_out(m):
                        dve.wait_ge(down_done, m * NJ + NJ)
                        dve.wait_ge(hm_in, m * 32 + 32)
                        for t in range(CB):
                            v.tensor_tensor(hm[:, t, :], b_down[t][:, :], hm[:, t, :], ALU.add)\
                                .then_inc(mo_ready, 1)

                    s = Steps(dve, c_step, PER)

                    def step(ins, wait=True):
                        s.done(ins)
                        if wait:
                            s.wait()

                    def norm_out(m):
                        for t in range(CB):
                            dve.wait_ge(mo_ready, m * CB + t + 1)
                            step(v.bn_stats(b6[:, t, :], hm[:, t, :]), wait=False)
                        s.wait()
                        v.memset(idle[:, :], 0.0)
                        for t in range(CB):
                            v.bn_aggr(bm[:, t, :], b6[:, t, :]).then_inc(mom_b, 1)
                        dve.wait_ge(lnb, m * 2 + 2)
                        for t in range(CB):
                            v.tensor_scalar(hm[:, t, :], hm[:, t, :], bm[:, t, 0:1], br[:, t:t + 1],
                                            ALU.subtract, ALU.mult).then_inc(nb_ready, 1)

                    def streams(m):
                        for t in range(CB):
                            dve.wait_ge(x1_ready, m * CB + t + 1)
                            step(v.bn_stats(b6[:, t, :], x1[:, t, :]), wait=False)
                        s.wait()
                        v.memset(idle[:, :], 0.0)
                        for t in range(CB):
                            v.bn_aggr(bm[:, t, :], b6[:, t, :]).then_inc(mom_x, 1)
                        dve.wait_ge(lnx, m * 6 + 2)
                        for t in range(CB):
                            v.tensor_scalar(xn[:, t, :], x1[:, t, :], bm[:, t, 0:1], br[:, t:t + 1],
                                            ALU.subtract, ALU.mult).then_inc(xn_ready, 1)

                    def logits(m):
                        dve.wait_ge(lnx, m * 6 + 6)
                        dve.wait_ge(lg_done, m * CB + CB)
                        for t in range(CB):
                            step(v.scalar_tensor_tensor(lg[:, t, :], b_lg[:, t * NLOG:(t + 1) * NLOG],
                                                        bx[:, t:t + 1], rows_sb[:, 17:17 + NLOG],
                                                        ALU.mult, ALU.add), wait=(t == CB - 1))
                        pp = lg[:, :, 16:24].rearrange("p t (s j) -> p t s j", s=2)
                        sm4 = sm[:, :, :].rearrange("p t (s j) -> p t s j", s=2)
                        mx = smx[:, :, :].rearrange("p t (s o) -> p t s o", o=1)
                        step(v.tensor_reduce(smx[:, :, :], pp, AX.X, ALU.max))
                        v.tensor_tensor(sm4, pp, mx.broadcast_to([P, CB, 2, 4]), ALU.subtract).then_inc(sm_in, 1)
                        for t in range(CB):
                            step(v.tensor_scalar(zl[:, t // 2, :, t % 2, :],
                                                 lg[:, t, 0:16].rearrange("p (i j) -> p i j", i=4),
                                                 10.0, None, ALU.mult), wait=(t == CB - 1))
                        both(lambda c: v.tensor_reduce(rowv[:, c, :, :], zl[:, c, :, :, :], AX.X, ALU.max))
                        both(lambda c: v.tensor_tensor(by_row(zl, c), by_row(zl, c), row_b(c), ALU.subtract))
                        both(lambda c: v.tensor_reduce(colv[:, c, :, :], by_col(zl, c), AX.X, ALU.max))
                        s.wait()
                        for c in range(2):
                            v.scalar_tensor_tensor(flat_i(pm, c), flat_i(zl, c), SHIFT, col_b(c),
                                                   ALU.add, ALU.subtract).then_inc(z_in, 1)

                    def flat_i(z, c):
                        return z[:, c, :, :, :].rearrange("p i t j -> p i (t j)")

                    def by_row(z, c):
                        return z[:, c, :, :, :].rearrange("p i t j -> p (i t) j")

                    def by_col(z, c):
                        return z[:, c, :, :, :].rearrange("p i t j -> p t j i")

                    def row_b(c):
                        return rowv[:, c, :, :].rearrange("p i (t o) -> p (i t) o", o=1).broadcast_to([P, 8, 4])

                    def col_b(c):
                        return colv[:, c, :, :].rearrange("p (o t) j -> p o (t j)", o=1).broadcast_to([P, 4, 8])

                    def both(op):
                        for c in range(2):
                            s.wait(1)
                            s.done(op(c))

                    def softmax_finish(m):
                        sm4 = sm[:, :, :].rearrange("p t (s j) -> p t s j", s=2)
                        mx = smx[:, :, :].rearrange("p t (s o) -> p t s o", o=1)
                        dve.wait_ge(sm_exp, m + 1)
                        step(v.tensor_reduce(smx[:, :, :], sm4, AX.X, ALU.add))
                        step(v.reciprocal(smx[:, :, :], smx[:, :, :]))
                        step(v.tensor_tensor(sm4, sm4, mx.broadcast_to([P, CB, 2, 4]), ALU.mult))

                    def sink_first(m):
                        dve.wait_ge(z_exp, m * 2 + 1)
                        both(lambda c: v.tensor_reduce(rowv[:, c, :, :], ze[:, c, :, :, :], AX.X, ALU.add))
                        both(lambda c: v.reciprocal(rowv[:, c, :, :], rowv[:, c, :, :]))
                        dve.wait_ge(z_exp, m * 2 + 2)
                        both(lambda c: v.tensor_tensor(by_row(pm, c), by_row(pm, c), row_b(c), ALU.mult))

                    def sink_row():
                        both(lambda c: v.tensor_reduce(rowv[:, c, :, :], pm[:, c, :, :, :], AX.X, ALU.add))
                        both(lambda c: v.reciprocal(rowv[:, c, :, :], rowv[:, c, :, :]))
                        both(lambda c: v.scalar_tensor_tensor(by_row(pm, c), row_b(c), SCALE_UP, by_row(pm, c),
                                                              ALU.mult, ALU.mult))

                    def sink_col(last=False):
                        both(lambda c: v.tensor_reduce(colv[:, c, :, :], by_col(pm, c), AX.X, ALU.add))
                        both(lambda c: v.reciprocal(colv[:, c, :, :], colv[:, c, :, :]))
                        both(lambda c: v.scalar_tensor_tensor(flat_i(pm, c), col_b(c), 1.0 if last else SCALE_UP,
                                                              flat_i(pm, c), ALU.mult, ALU.mult))

                    def sink_end(m):
                        s.wait()
                        for c in range(2):
                            flat = pm[:, c, :, :, :].rearrange("p i t j -> p (i t j)")
                            v.scalar_tensor_tensor(flat, flat, sg[:, 2:3],
                                                   eye[:, :, :, :].rearrange("p i t j -> p (i t j)"),
                                                   ALU.mult, ALU.add).then_inc(hres_ready, 1)
                        dve.wait_ge(hres_ready, m * 2 + 2)

                    def x_pre(m):
                        if not (isinstance(m, int) and m == 0):
                            dve.wait_ge(b_out, m * 16 * CB)
                        for t0 in range(0, CB, 2):
                            for n4 in range(4):
                                for t in (t0, t0 + 1):
                                    src, wgt = xn[:, t, n4 * P:n4 * P + P], sm[:, t, n4:n4 + 1]
                                    if n4 == 0:
                                        s.done(v.tensor_scalar(mix[:, t, 0:P], src, wgt, None, ALU.mult))
                                        continue
                                    s.wait(1 if n4 < 3 or t == t0 else 0)
                                    ins = v.scalar_tensor_tensor(mix[:, t, 0:P], src, wgt, mix[:, t, 0:P],
                                                                 ALU.mult, ALU.add)
                                    if n4 < 3:
                                        s.done(ins)
                                    else:
                                        ins.then_inc(xp_ready, 1)

                    def mix_stats(m, t):
                        step(v.bn_stats(f6[:, t, :], mix[:, t, :]), wait=False)
                        s.wait()
                        v.memset(idle[:, :], 0.0)
                        v.bn_aggr(fm[:, t, :], f6[:, t, :]).then_inc(mom_f, 1)

                    def mixing(m, t):
                        dve.wait_ge(ym_ready, m * CB + t + 1)
                        for jj in range(4):
                            for ii in range(4):
                                dst = mix[:, t, ii * P:ii * P + P]
                                if jj > 0:
                                    s.wait(3)
                                step(v.scalar_tensor_tensor(dst, xn[:, t, jj * P:jj * P + P],
                                                            pm[:, t // 2, ii, t % 2, jj:jj + 1], dst,
                                                            ALU.mult, ALU.add), wait=False)
                        s.wait()
                        mix_stats(m, t)

                    halves = [0]

                    def sinkhorn(upto):
                        while halves[0] < min(upto, 2 * SINK):
                            k = halves[0]
                            if k % 2 == 0:
                                sink_row()
                            else:
                                sink_col(last=(k == 2 * SINK - 1))
                            halves[0] += 1

                    PACE = {2: 6, 3: 18, 4: 26, **{j: 26 + 12 * (j - 4) for j in range(5, 11)}}

                    def body(m, mlp, mhc, c):
                        if mhc:
                            dve.sem_clear(c_step)
                            s.begin(0)
                        for j in range(NJ):
                            if mhc and j == 0:
                                norm_out(c)
                            if mlp and not mhc and j + 2 < NJ:
                                up_low(j + 2)
                            if mlp:
                                gate_up(m, j)
                            if mhc:
                                if j == 0:
                                    streams(c)
                                if j == 2:
                                    logits(c)
                                    softmax_finish(c)
                                    sink_first(c)
                                    halves[0] = 1
                                if j in PACE:
                                    sinkhorn(PACE[j])
                                if j == 4:
                                    x_pre(c)
                                if j == 11:
                                    sinkhorn(2 * SINK)
                                    sink_end(c)
                                if j >= 11:
                                    mixing(c, j - 11)
                            if mlp and j == 13:
                                if not isinstance(m, int) or m < NB - 1:
                                    h2_low(m + 1)
                            if mhc:
                                if j == 13:
                                    dve.wait_ge(pool_mix, c * 8 + 8)
                                    mix_stats(c, CB - 1)
                        if mhc:
                            s.end()
                            s.wait()
                        if mlp:
                            mlp_out(m)

                    body(0, True, False, 0)
                    with dve.Fori(1, NB - 1) as m:
                        body(m, True, True, m - 1)
                    body(NB - 1, True, True, NB - 2)
                    body(0, False, True, NB - 1)

                @block.tensor
                def _(pe):
                    t_ = nc.tensor

                    def product(m, j, bank, w_hi, w_lo, signal, fresh=False, midway=None):
                        n = 0
                        for k in range(KD):
                            if k == KD // 2 and midway:
                                midway()
                            if fresh:
                                pe.wait_ge(hl_ready, m * KD + k + 1)
                            for wv, hv in ((w_hi, h2_hi), (w_lo, h2_hi), (w_hi, h2_lo)):
                                ins = t_.matmul(bank[:, :], wv[:, j, k * P:k * P + P], hv[:, k, :],
                                                start=(n == 0), stop=(n == 3 * KD - 1))
                                n += 1
                        ins.then_inc(signal, 1)

                    def gate(m, j, midway=None):
                        i = m * NJ + j
                        if not (isinstance(m, int) and i == 0):
                            pe.wait_ge(th_ready, i)
                        product(m, j, b_gate, gate_hi, gate_lo, gate_done, j == 0, midway)

                    def up(m, j, first, midway=None):
                        i = m * NJ + j
                        if first:
                            pe.wait_ge(up_l, j + 1)
                        if not (isinstance(m, int) and i == 0):
                            pe.wait_ge(glu_ready, i)
                        product(m, j, b_up, up_hi, up_lo, up_done, midway=midway)

                    def down(m, j):
                        i = m * NJ + j
                        pe.wait_ge(glu_ready, i + 1)
                        if j == 0:
                            if not (isinstance(m, int) and m == 0):
                                pe.wait_ge(mo_ready, m * CB)
                        if isinstance(m, int) and m == 0:
                            for i, (j0, j1) in enumerate(DOWN_LOADS):
                                if j0 == j:
                                    pe.wait_ge(dn_in[i], 16)
                        for t in range(CB):
                            ins = t_.matmul(b_down[t][:, :], glu[:, j % 2, t * P:t * P + P], down_sb[:, j, :],
                                            start=(j == 0), stop=(j == NJ - 1))
                        ins.then_inc(down_done, 1)

                    def stream_transpose(c, t):
                        i = c * CB + t
                        pe.wait_ge(xn_ready, i + 1)
                        if not (isinstance(c, int) and i == 0):
                            pe.wait_ge(xt_ready, i)
                        for k in range(KD):
                            ins = t_.transpose(b_tr[:, k * P:k * P + P], xn[:, t, k * P:k * P + P], ident[:, :])
                        ins.then_inc(xt_done, 1)

                    def stream_logits(c, t):
                        i = c * CB + t
                        if t == 0 and not (isinstance(c, int) and c == 0):
                            pe.wait_ge(ym_ready, i)
                        if t == 0:
                            pe.wait_ge(k_in, 32)
                        pe.wait_ge(xt_ready, i + 1)
                        for k in range(KD):
                            ins = t_.matmul(b_lg[:, t * NLOG:(t + 1) * NLOG], tr[:, k * P:k * P + P],
                                            wlog[:, k, :], start=(k == 0), stop=(k == KD - 1))
                        ins.then_inc(lg_done, 1)

                    def branch_transpose(c, t):
                        i = c * CB + t
                        pe.wait_ge(xp_ready, i + 1)
                        if t > 0:
                            pe.wait_ge(ym_ready, i)
                        t_.transpose(b_lg[:, 0:P], mix[:, t, 0:P], ident[:, :]).then_inc(xpt_done, 1)

                    def branch(c, t):
                        pe.wait_ge(xpt_ready, c * CB + t + 1)
                        t_.matmul(b_lg[:, P:2 * P], tr[:, 0:P], wbr[:, :], start=True, stop=True)\
                            .then_inc(br_done, 1)

                    def body(m, mlp, mhc, c, first):
                        for j in range(NJ):
                            def streams(t):
                                if mhc and j == 2:
                                    if t > 0:
                                        stream_logits(c, t - 1)
                                    if t < CB:
                                        stream_transpose(c, t)

                            streams(0)
                            if mlp:
                                gate(m, j, lambda: streams(1))
                            else:
                                streams(1)
                            streams(2)
                            if mhc and 5 <= j < 5 + CB:
                                branch_transpose(c, j - 5)
                            if mlp:
                                up(m, j, first, lambda: streams(3))
                            else:
                                streams(3)
                            streams(4)
                            if mhc and 5 <= j < 5 + CB:
                                branch(c, j - 5)
                            if mlp and j > 0:
                                down(m, j - 1)
                        if mlp:
                            down(m, NJ - 1)

                    body(0, True, False, 0, True)
                    with pe.Fori(1, NB) as m:
                        body(m, True, True, m - 1, False)
                    body(0, False, True, NB - 1, False)


def kernel(**inputs):
    import numpy as _np
    import concourse.bacc as _bacc
    from concourse import mybir as _mybir
    from concourse.bass_utils import run_bass_kernel_spmd as _run

    i = {k: _np.asarray(a) for k, a in inputs.items()}

    def by_chunk(w):
        return w.reshape(-1, P, w.shape[1]).transpose(1, 0, 2)

    w_in = i["L0_attn_w_in"].T
    z, xb, dt = w_in[:, :D], w_in[:, D:D + 6 * P], w_in[:, D + 6 * P:]

    def by_hidden(w):
        return w.reshape(NJ, P, KD, P).transpose(3, 0, 2, 1).reshape(P, NJ, KD * P)

    feeds = {
        "x": i["L0_attn_hidden_states"].reshape(TOK, D),
        "w_in": by_chunk(_np.concatenate([xb, z], axis=1)),
        "w_dt": by_chunk(dt),
        "conv_w": i["L0_attn_conv_w"].reshape(NXBC, P, TAPS).transpose(1, 0, 2),
        "conv_b": i["L0_attn_conv_b"].reshape(NXBC, P).T,
        "w_out": by_chunk(i["L0_attn_w_out"].T),
        "gate_w": by_hidden(i["L0_attn_gate_w"]),
        "up_w": by_hidden(i["L0_attn_up_w"]),
        "down_w": by_chunk(i["L0_attn_down_w"].T),
        "ln_w": _np.concatenate([i["L0_attn_ln1_w"].reshape(KD, P).T, i["L0_attn_ln2_w"].reshape(KD, P).T], axis=1),
        "rows": _np.concatenate([i["L0_attn_A_log"], i["L0_attn_dt_bias"], i["L0_attn_dt_bias"], i["L0_attn_D"],
                                 i["L0_ffn_gate"], i["L0_ffn_H_res_base"].reshape(-1), i["L0_ffn_H_pre_base"],
                                 i["L0_ffn_H_post_base"]]).reshape(1, -1),
        "w_logit": by_chunk(_np.concatenate([i["L0_ffn_W_res"], i["L0_ffn_W_pre"], i["L0_ffn_W_post"]]).T),
        "w_branch": i["L0_ffn_W_branch"],
    }
    nc = _bacc.Bacc("TRN2", target_bir_lowering=False, num_devices=1)
    arrays, args = {}, []
    for name, a in feeds.items():
        a = _np.ascontiguousarray(a)
        arrays[f"in_{name}"] = a
        args.append(nc.dram_tensor(f"in_{name}", a.shape, _mybir.dt.from_np(a.dtype), kind="ExternalInput").ap())
    args.append(nc.dram_tensor("out_0", (TOK, D), F32, kind="ExternalOutput").ap())
    mamba_mlp_mhc(nc, *args)
    r = _run(nc, [arrays], core_ids=[0])
    return r.results[0]["out_0"].reshape(BATCHES, TOK // BATCHES, D)
```

```python
from contextlib import ExitStack

import concourse.bass as bass
from concourse import mybir

F32 = mybir.dt.float32
F32R = mybir.dt.float32r
ACT = mybir.ActivationFunctionType
ALU = mybir.AluOpType
AX = mybir.AxisListType

P = 128
D = 512
KD = D // P
H = 4
INTER = 1792
NJ = INTER // P
TOK = 2048
BATCHES = 2
TA = 256
CA = TA // P
NA = TOK // TA
TB = 512
CB = TB // P
NB = TOK // TB
NXBC = 6
TAPS = 4
HALO = TAPS - 1
NPAIR = 5
NLOG = 24
SINK = 50
EPS = 1e-5
EPS_MHC = 1.1920929e-07
MASKED = -1.0e30
SHIFT = 80.0
SCALE_UP = 5.5406223843935098e34
LN1P_TERMS = 8


SU_G = 15
SU_V = 5


def at_tile(ap, m):
    if isinstance(m, int):
        return ap[m]
    names = " ".join("bcde"[:len(ap.shape) - 2])
    return ap[bass.ds(m, 1)].rearrange(f"a p {names} -> (a p) {names}") if len(ap.shape) == 3 else \
        ap[bass.ds(m, 1)].squeeze(0)


class Steps:

    def __init__(self, eng, sem, per_tile):
        self.eng, self.sem, self.per_tile, self.k, self.m = eng, sem, per_tile, 0, 0

    def begin(self, m):
        self.m, self.k = m, 0

    def done(self, ins):
        ins.then_inc(self.sem, 1)
        self.k += 1

    def wait(self, back=0):
        self.eng.wait_ge(self.sem, self.m * self.per_tile + (self.k - back))

    def end(self):
        assert self.k == self.per_tile, (self.k, self.per_tile)


def heads(ap):
    return ap.rearrange("p (h q) -> p h q", h=H)


def mamba_mlp_mhc(nc, x, w_in, w_dt, conv_w, conv_b, w_out, gate_w, up_w, down_w, ln_w,
                  rows, w_logit, w_branch, out):
    DT = 18
    CONV = 2 * (TAPS - 1)
    h_scr = nc.dram_tensor("h_scr", (NA, P, CA, D), F32, kind="Internal").ap()
    h2t_scr = nc.dram_tensor("h2t_scr", (NA, P, KD, TA), F32, kind="Internal").ap()
    x_a = x.rearrange("(m t p) d -> m p t d", t=CA, p=P)
    x_b = x.rearrange("(m t p) d -> m p t d", t=CB, p=P)
    out_b = out.rearrange("(m t p) d -> m p t d", t=CB, p=P)
    h_scr_b = h_scr.rearrange("(m u) p t d -> m u p t d", u=2)
    h2t_scr_b = h2t_scr.rearrange("(m u) p k q -> m u p k q", u=2)

    with ExitStack() as whole:
        def sem(name):
            return whole.enter_context(nc.semaphore(name))

        def sb(stack, name, shape, dt=F32):
            return stack.enter_context(nc.sbuf_tensor(name, shape, dt))

        def over_raw(stack, name, shape):
            with nc.sbuf_tensor(f"{name}_raw", shape, F32) as raw:
                pass
            return sb(stack, f"{name}_lo", shape, F32R), raw

        ident = sb(whole, "ident", [P, P])
        rows_sb = sb(whole, "rows_sb", [P, 64])
        NR = rows.shape[1]
        ln_sb = sb(whole, "ln_sb", [P, 2 * KD])
        halfc = sb(whole, "halfc", [P, CB])
        idle = sb(whole, "idle", [P, 1])
        epsc = sb(whole, "epsc", [P, CB])
        epsm = sb(whole, "epsm", [P, CB])
        zeroc = sb(whole, "zeroc", [P, 1])
        gate_hi = sb(whole, "gate_hi", [P, NJ, KD * P], F32R)
        gate_lo, gate_raw = over_raw(whole, "gate", [P, NJ, KD * P])
        h2_in = sem("h2t_loaded")
        banks = [whole.enter_context(nc.psum_tensor(f"bank{i}", [P, 512], F32)) for i in range(8)]

        with ExitStack() as st:
            with nc.sbuf_tensor("h2_raw", [P, KD, TB], F32) as h2_raw:
                pass
            win_hi = sb(st, "win_hi", [P, KD, 2 * NPAIR * P], F32R)
            tri = sb(st, "tri", [P, P])
            negmask = sb(st, "negmask", [P, P])
            ones = sb(st, "ones", [P, P])
            keep = sb(st, "keep", [P, NA + 1])
            win_lo, win_raw = over_raw(st, "win", [P, KD, 2 * NPAIR * P])
            wdt_raw = sb(st, "wdt_raw", [P, KD, H])
            wdt_hi = sb(st, "wdt_hi", [P, KD, H], F32R)
            wdt_lo = sb(st, "wdt_lo", [P, KD, H], F32R)
            wout_hi = sb(st, "wout_hi", [P, H, D], F32R)
            wout_lo, wout_raw = over_raw(st, "wout", [P, H, D])
            y_hi = sb(st, "y_hi", [P, D], F32R)
            y_lo = sb(st, "y_lo", [P, D], F32R)
            convw_sb = sb(st, "convw_sb", [P, NXBC, TAPS])
            convb_sb = sb(st, "convb_sb", [P, NXBC])
            a_rate = sb(st, "a_rate", [P, 2 * H])
            x_t = sb(st, "x_t", [P, 2, CA, D])
            h0 = sb(st, "h0", [P, 2, CA, D])
            u = sb(st, "u", [P, CA, D])
            u_hi = sb(st, "u_hi", [P, KD, TA], F32R)
            u_lo = sb(st, "u_lo", [P, KD, TA], F32R)
            xraw = sb(st, "xraw", [P, NXBC, HALO + TA])
            xbc = sb(st, "xbc", [P, 2, NXBC, TA])
            xbc_tanh = sb(st, "xbc_tanh", [P, 3, 2 * TA])
            zs = sb(st, "zs", [P, 2, H, TA])
            decay = sb(st, "decay", [P, 512])
            ecs = sb(st, "ecs", [P, 512])
            c_dec = sb(st, "c_dec", [P, 512])
            xw = sb(st, "xw", [P, 512])
            xb_tok = sb(st, "xb_tok", [P, 2 * P + H])
            state = sb(st, "state", [P, 512])
            atri = sb(st, "atri", [P, 512])
            y = sb(st, "y", [P, 512])
            h = sb(st, "h", [P, CA, D])
            h2 = sb(st, "h2", [P, CA, D])
            h2t = sb(st, "h2t", [P, KD, TA])
            st6 = sb(st, "st6", [P, CA, 6])
            mom = sb(st, "mom", [P, CA, 2])
            ve = sb(st, "ve", [P, CA])
            rstd = sb(st, "rstd", [P, CA])
            qv = sb(st, "qv", [P, CA])
            rr = sb(st, "rr", [P, CA])
            ss = sb(st, "ss", [P, CA])
            msq = sb(st, "msq", [P, CA])
            rh = sb(st, "rh", [P, CA])
            dt_h = sb(st, "dt_h", [H, TA])
            pre = sb(st, "pre", [P, 2 * H])
            nabs = sb(st, "nabs", [P, 2 * H])
            e1 = sb(st, "e1", [P, 2 * H])
            s1 = sb(st, "s1", [P, 2 * H])
            s2 = sb(st, "s2", [P, 2 * H])
            acc = sb(st, "acc", [P, 2 * H])
            relu = sb(st, "relu", [P, 2 * H])
            dtv = sb(st, "dtv", [P, 2, 2 * H])
            av = sb(st, "av", [P, 2, 2 * H])
            wt = sb(st, "wt", [P, H])
            wk = sb(st, "wk", [P, H])

            b_tp, b_ip = banks[0:2], banks[2:4]
            b_cs, b_g, b_y, b_misc = banks[4], banks[5], banks[6], banks[7]
            DT0 = 264

            c_in = sem("constants_loaded")
            ln_in = sem("norm_weights_loaded")
            win_in = [sem(f"w_in_chunk{k}_loaded") for k in range(KD)]
            gate_in = sem("gate_weights_loaded")
            ghi = sem("gate_hi_ready")
            glo = sem("gate_lo_ready")
            whi = sem("weight_hi_ready")
            wlo = sem("weight_lo_ready")
            su_v = sem("setup_vector_steps")
            su_g = sem("setup_gpsimd_steps")
            su_a = sem("setup_scalar_steps")
            x_in = [sem("x_loaded_even"), sem("x_loaded_odd")]
            stats = sem("ln_stats_done")
            moments = sem("ln_moments_done")
            scales = sem("ln_scale_steps")
            h0_ready = sem("h0_ready")
            u_ready = sem("u_ready")
            ut_done = sem("u_transposed")
            uh_ready = sem("u_hi_ready")
            ul_ready = sem("u_lo_ready")
            ip_done = sem("in_projection_pair_done")
            xraw_ready = sem("conv_input_ready")
            halo_ready = sem("conv_halo_ready")
            conv_step = sem("conv_steps")
            tap_ready = sem("conv_current_tap_ready")
            xtanh = sem("xbc_tanh_ready")
            xbc_ready = sem("xbc_ready")
            ztanh = sem("z_tanh_ready")
            zs_ready = sem("z_silu_ready")
            dth_done = sem("dt_projected_by_head")
            dth_ready = sem("dt_by_head_copied")
            dtp_done = sem("dt_by_token")
            dt_step = sem("dt_steps")
            dt_exp = sem("dt_exp_ready")
            atri_ready = sem("atri_ready")
            misc_done = sem("token_major_done")
            xb_ready = sem("token_major_copied")
            csbc_done = sem("cumsum_done")
            ecs_ready = sem("exp_cumsum_ready")
            diff_done = sem("cumsum_differences_ready")
            e_ready = sem("decay_exps_ready")
            wk_ready = sem("state_weights_ready")
            g_done = sem("scores_done")
            m_ready = sem("decayed_scores_ready")
            cd_ready = sem("c_decayed_ready")
            xw_ready = sem("x_weighted_ready")
            y_done = sem("y_done")
            st_done = sem("chunk_state_done")
            yd_ready = sem("y_plus_dx_ready")
            yg_ready = sem("y_gated_ready")
            yh_ready = sem("y_hi_ready")
            yl_ready = sem("y_lo_ready")
            wo_hi = sem("w_out_hi_ready")
            wo_lo = sem("w_out_lo_ready")
            s_upd = sem("state_updated")
            state_raw = sem("state_before_reset")
            o_done = sem("out_projection_done")
            h_ready = sem("h_ready")
            ss_ready = sem("h_mean_square_ready")
            rms_step = sem("h_rms_steps")
            h2_ready = sem("h2_ready")
            h2t_done = sem("h2_transposed")
            h2t_ready = sem("h2t_copied")
            a_out = sem("block_a_stored")

            with nc.Block() as block:

                @block.sync
                def _(sp):
                    sp.dma_start(ln_sb[:, :], ln_w).then_inc(ln_in, 16)
                    sp.dma_start(x_t[:, 0, :, :], x_a[0]).then_inc(x_in[0], 16)
                    for k in range(KD):
                        sp.dma_start(win_raw[:, k, :], w_in[:, k, :]).then_inc(win_in[k], 16)
                    sp.dma_start(rows_sb[:, 0:NR], rows.broadcast_to([P, NR])).then_inc(c_in, 16)
                    sp.dma_start(convw_sb[:, :, :], conv_w).then_inc(c_in, 16)
                    sp.dma_start(convb_sb[:, :], conv_b).then_inc(c_in, 16)
                    sp.dma_start(wdt_raw[:, :, :], w_dt).then_inc(c_in, 16)
                    sp.dma_start(x_t[:, 1, :, :], x_a[1]).then_inc(x_in[1], 16)
                    sp.dma_start(wout_raw[:, :, :], w_out).then_inc(c_in, 16)
                    sp.dma_start(gate_raw[:, :, :], gate_w).then_inc(gate_in, 16)

                    def load_x(m, q):
                        sp.wait_ge(h0_ready, (m - 2) * CA + CA)
                        sp.dma_start(x_t[:, q, :, :], at_tile(x_a, m)).then_inc(x_in[q], 16)

                    def store(m):
                        sp.wait_ge(h2_ready, m * CA + CA)
                        sp.dma_start(at_tile(h_scr, m), h[:, :, :]).then_inc(a_out, 16)
                        sp.wait_ge(h2t_ready, m * 2 + 2)
                        sp.dma_start(at_tile(h2t_scr, m), h2t[:, :, :]).then_inc(a_out, 16)

                    load_x(2, 0)
                    load_x(3, 1)
                    with sp.Fori(0, NA // 2 - 2) as b:
                        store(b * 2)
                        load_x(b * 2 + 4, 0)
                        store(b * 2 + 1)
                        load_x(b * 2 + 5, 1)
                    for m in range(NA - 4, NA - 1):
                        store(m)
                    sp.wait_ge(a_out, 32 * (NA - 1))
                    sp.wait_ge(ip_done, NA * NPAIR)
                    for uu in range(2):
                        sp.dma_start(h2_raw[:, :, uu * TA:uu * TA + TA],
                                     h2t_scr_b[0, uu]).then_inc(h2_in, 16)
                    store(NA - 1)
                    sp.wait_ge(a_out, 32 * NA)

                @block.gpsimd
                def _(pool):
                    g = nc.gpsimd
                    n = 0

                    def after(ins):
                        nonlocal n
                        n += 1
                        ins.then_inc(su_g, 1)
                        pool.wait_ge(su_g, n)

                    after(g.memset(ident[:, :], 0.0))
                    after(g.affine_select(out=ident[:, :], in_=ident[:, :], compare_op=ALU.not_equal,
                                          fill=1.0, base=0, pattern=[[-1, P]], channel_multiplier=1))
                    after(g.memset(ones[:, :], 1.0))
                    after(g.memset(negmask[:, :], 0.0))
                    after(g.affine_select(out=tri[:, :], in_=ones[:, :], compare_op=ALU.is_ge,
                                          fill=0.0, base=0, pattern=[[1, P]], channel_multiplier=-1))
                    after(g.affine_select(out=negmask[:, :], in_=negmask[:, :], compare_op=ALU.is_ge,
                                          fill=MASKED, base=0, pattern=[[1, P]], channel_multiplier=-1))
                    after(g.memset(halfc[:, :], -0.5))
                    after(g.memset(epsc[:, :], EPS))
                    after(g.memset(epsm[:, :], EPS_MHC))
                    after(g.memset(zeroc[:, :], 0.0))
                    after(g.memset(keep[:, :], 1.0))
                    for b in range(0, BATCHES + 1):
                        i = b * NA // BATCHES
                        after(g.memset(keep[:, i:i + 1], 0.0))
                    after(g.memset(state[:, :], 0.0))
                    assert n == SU_G, n
                    g.memset(xraw[:, :, 0:HALO], 0.0).then_inc(halo_ready, 1)

                    def ln_scales(m):
                        s = Steps(pool, scales, 7)
                        s.begin(m)
                        pool.wait_ge(moments, m * CA + CA)
                        pool.wait_ge(h0_ready, m * CA)
                        pool.wait_ge(u_ready, m * CA)
                        s.done(g.tensor_tensor(ve[:, :], mom[:, :, 1], epsc[:, 0:CA], ALU.add))
                        s.wait()
                        s.done(g.tensor_tensor(rstd[:, :], ve[:, :], halfc[:, 0:CA], ALU.pow))
                        s.wait()
                        s.done(g.tensor_tensor(qv[:, :], rstd[:, :], rstd[:, :], ALU.mult))
                        s.wait()
                        s.done(g.tensor_tensor(qv[:, :], qv[:, :], mom[:, :, 1], ALU.mult))
                        s.wait()
                        s.done(g.tensor_tensor(qv[:, :], qv[:, :], epsc[:, 0:CA], ALU.add))
                        s.wait()
                        s.done(g.tensor_tensor(rr[:, :], qv[:, :], halfc[:, 0:CA], ALU.pow))
                        s.wait()
                        s.done(g.tensor_tensor(rr[:, :], rr[:, :], rstd[:, :], ALU.mult))
                        s.end()

                    def halo(m):
                        pool.wait_ge(conv_step, m * 3 * CONV)
                        kp = keep[:, bass.ds(m, 1)].rearrange("p (a o) -> p a o", o=1)
                        g.tensor_tensor(xraw[:, :, 0:HALO], xraw[:, :, TA:TA + HALO],
                                        kp.broadcast_to([P, NXBC, HALO]), ALU.mult)\
                            .then_inc(halo_ready, 1)

                    def a_tri(m, q, c):
                        pool.wait_ge(dt_step, m * DT + DT)
                        pool.wait_ge(csbc_done, m * CA + c)
                        a4 = av[:, q, c * H:c * H + H].rearrange("p (h o) -> p h o", o=1)
                        t4 = tri[:, :].rearrange("p (o q) -> p o q", o=1)
                        g.tensor_tensor(heads(atri[:, :]), t4.broadcast_to([P, H, P]),
                                        a4.broadcast_to([P, H, P]), ALU.mult).then_inc(atri_ready, 1)

                    def c_decayed(m, q, c):
                        pool.wait_ge(ecs_ready, m * CA + c + 1)
                        pool.wait_ge(xbc_ready, m * 3 + 3)
                        pool.wait_ge(y_done, m * CA + c)
                        g.tensor_tensor(heads(c_dec[:, :]), xbc[:, q, 2:6, c * P:c * P + P],
                                        heads(ecs[:, :]), ALU.mult).then_inc(cd_ready, 1)

                    def x_weighted(m, c):
                        pool.wait_ge(wk_ready, m * CA + c + 1)
                        pool.wait_ge(xb_ready, m * CA + c + 1)
                        pool.wait_ge(st_done, m * CA + c)
                        x4 = xb_tok[:, 0:P].rearrange("p (o q) -> p o q", o=1)
                        w4 = wk[:, :].rearrange("p (h o) -> p h o", o=1)
                        g.tensor_tensor(heads(xw[:, :]), x4.broadcast_to([P, H, P]),
                                        w4.broadcast_to([P, H, P]), ALU.mult).then_inc(xw_ready, 1)

                    def y_low(m, c):
                        pool.wait_ge(yh_ready, m * CA + c + 1)
                        g.tensor_tensor(y_lo[:, :], y[:, :], y_hi[:, :].bitcast(F32), ALU.subtract)\
                            .then_inc(yl_ready, 1)

                    def h_rms(m):
                        pool.wait_ge(ss_ready, m * CA + CA)
                        pool.wait_ge(h2_ready, m * CA)
                        g.tensor_tensor(msq[:, :], ss[:, :], epsc[:, 0:CA], ALU.add)\
                            .then_inc(rms_step, 1)
                        pool.wait_ge(rms_step, m * 2 + 1)
                        g.tensor_tensor(rh[:, :], msq[:, :], halfc[:, 0:CA], ALU.pow).then_inc(rms_step, 1)

                    def gate_low(m):
                        pool.wait_ge(ghi, m + 1)
                        two = slice(2 * m, 2 * m + 2) if isinstance(m, int) else bass.ds(m * 2, 2)
                        g.tensor_tensor(gate_lo[:, two, :], gate_raw[:, two, :],
                                        gate_hi[:, two, :].bitcast(F32), ALU.subtract).then_inc(glo, 1)

                    def body(m, q, before, nxt, nxt2):
                        if nxt:
                            halo(m + 1)
                        if before:
                            y_low(m - 1, 1)
                        c_decayed(m, q, 0)
                        x_weighted(m, 0)
                        if before:
                            h_rms(m - 1)
                        if nxt2:
                            ln_scales(m + 2)
                        a_tri(m, q, 1)
                        if isinstance(m, int) and m == 0:
                            pool.wait_ge(wo_hi, 1)
                            g.tensor_tensor(wout_lo[:, :, :], wout_raw[:, :, :], wout_hi[:, :, :].bitcast(F32),
                                            ALU.subtract).then_inc(wo_lo, 1)
                        y_low(m, 0)
                        c_decayed(m, q, 1)
                        x_weighted(m, 1)
                        if nxt:
                            a_tri(m + 1, 1 - q, 0)
                            gate_low(m)

                    ln_scales(0)
                    ln_scales(1)
                    a_tri(0, 0, 0)
                    body(0, 0, False, True, True)
                    with pool.Fori(0, NA // 2 - 2) as b:
                        body(b * 2 + 1, 1, True, True, True)
                        body(b * 2 + 2, 0, True, True, True)
                    body(NA - 3, 1, True, True, True)
                    body(NA - 2, 0, True, True, False)
                    body(NA - 1, 1, True, False, False)
                    y_low(NA - 1, 1)
                    h_rms(NA - 1)

                @block.scalar
                def _(act):
                    a = nc.scalar
                    act.wait_ge(ln_in, 16)
                    for k in range(KD):
                        act.wait_ge(win_in[k], 16)
                        a.activation(win_hi[:, k, :], win_raw[:, k, :], ACT.Copy,
                                     scale=ln_sb[:, k:k + 1]).then_inc(whi, 1)
                    act.wait_ge(c_in, 80)
                    for k in range(KD):
                        ins = a.activation(wdt_hi[:, k, :], wdt_raw[:, k, :], ACT.Copy,
                                           scale=ln_sb[:, k:k + 1])
                    ins.then_inc(su_a, 1)
                    a.activation(a_rate[:, 0:H], rows_sb[:, 0:H], ACT.Exp).then_inc(su_a, 1)
                    a.activation(a_rate[:, H:2 * H], rows_sb[:, 0:H], ACT.Exp).then_inc(su_a, 1)

                    def u_high(m):
                        for i in range(2):
                            act.wait_ge(ut_done, m * 2 + i + 1)
                            if not (isinstance(m, int) and m == 0):
                                act.wait_ge(ip_done, m * NPAIR)
                            a.copy(u_hi[:, 2 * i:2 * i + 2, :],
                                   b_tp[i][:, :].rearrange("p (k q) -> p k q", k=2)).then_inc(uh_ready, 1)

                    def conv_in(m, g):
                        act.wait_ge(ip_done, m * NPAIR + g + 1)
                        act.wait_ge(halo_ready, m + 1)
                        bank = b_ip[(QOF[0] + g) % 2]
                        a.copy(xraw[:, 2 * g:2 * g + 2, HALO:HALO + TA],
                               bank[:, :].rearrange("p (k q) -> p k q", k=2)).then_inc(xraw_ready, 1)
                        for k in range(2):
                            ch = 2 * g + k
                            ins = a.activation(xbc[:, QOF[0], ch, :], bank[:, k * TA:k * TA + TA], ACT.Identity,
                                               bias=convb_sb[:, ch:ch + 1], scale=convw_sb[:, ch, TAPS - 1:TAPS])
                        ins.then_inc(tap_ready, 1)

                    def z_th(m, q, i):
                        act.wait_ge(ip_done, m * NPAIR + 3 + i + 1)
                        a.activation(zs[:, q, 2 * i:2 * i + 2, :].rearrange("p c q -> p (c q)"),
                                     b_ip[(q + 3 + i) % 2][:, :], ACT.Tanh, scale=0.5)\
                            .then_inc(ztanh, 1)

                    def dt_copy(m):
                        act.wait_ge(dth_done, m + 1)
                        if not (isinstance(m, int) and m == 0):
                            act.wait_ge(dtp_done, m)
                        a.copy(dt_h[:, :], b_misc[0:H, 0:TA]).then_inc(dth_ready, 1)

                    def dt_e(m):
                        act.wait_ge(dt_step, m * DT + 2)
                        a.activation(e1[:, :], nabs[:, :], ACT.Exp).then_inc(dt_exp, 1)

                    def xbc_th(m, q, g):
                        act.wait_ge(conv_step, m * 3 * CONV + CONV * (g + 1))
                        if not (isinstance(m, int) and m == 0):
                            act.wait_ge(xbc_ready, m * 3 + g - 2)
                        a.activation(xbc_tanh[:, g, :], xbc[:, q, 2 * g:2 * g + 2, :].rearrange("p c q -> p (c q)"),
                                     ACT.Tanh).then_inc(xtanh, 1)

                    def tok_major(m, c):
                        act.wait_ge(misc_done, m * CA + c + 1)
                        if not (isinstance(m, int) and m * CA + c == 0):
                            act.wait_ge(st_done, m * CA + c)
                        a.copy(xb_tok[:, :], b_misc[:, 0:2 * P + H]).then_inc(xb_ready, 1)

                    def exp_cs(m, c):
                        act.wait_ge(csbc_done, m * CA + c + 1)
                        if not (isinstance(m, int) and m * CA + c == 0):
                            act.wait_ge(cd_ready, m * CA + c)
                            act.wait_ge(s_upd, m * CA + c)
                        a.activation(ecs[:, :], b_cs[:, :], ACT.Exp).then_inc(ecs_ready, 1)

                    def decays(m, c):
                        act.wait_ge(diff_done, m * CA + c + 1)
                        a.activation(wt[:, :], wt[:, :], ACT.Exp).then_inc(e_ready, 1)
                        a.activation(decay[:, :], decay[:, :], ACT.Exp).then_inc(e_ready, 1)

                    def y_high(m, c):
                        act.wait_ge(yg_ready, m * CA + c + 1)
                        if not (isinstance(m, int) and m * CA + c == 0):
                            act.wait_ge(o_done, m * CA + c)
                        a.copy(y_hi[:, :], y[:, :]).then_inc(yh_ready, 1)

                    def square_sum(m, c):
                        act.wait_ge(h_ready, m * CA + c + 1)
                        if not (isinstance(m, int) and m == 0):
                            act.wait_ge(h2t_done, m * 2)
                            act.wait_ge(rms_step, m * 2)
                        a.activation(h2[:, c, :], h[:, c, :], ACT.Square, scale=float(D) ** -0.5,
                                     accum_out=ss[:, c:c + 1])\
                            .then_inc(ss_ready, 1)

                    def h2t_copy(m):
                        for i in range(2):
                            act.wait_ge(h2t_done, m * 2 + i + 1)
                            if not (isinstance(m, int) and m == 0):
                                act.wait_ge(a_out, m * 32)
                            for k in range(2):
                                ins = a.activation(h2t[:, 2 * i + k, :], b_tp[i][:, k * TA:k * TA + TA],
                                                   ACT.Copy, scale=ln_sb[:, KD + 2 * i + k:KD + 2 * i + k + 1])
                            ins.then_inc(h2t_ready, 1)

                    QOF = [0]
                    def gate_high(m):
                        act.wait_ge(gate_in, 16)
                        two = slice(2 * m, 2 * m + 2) if isinstance(m, int) else bass.ds(m * 2, 2)
                        a.copy(gate_hi[:, two, :], gate_raw[:, two, :]).then_inc(ghi, 1)

                    QOF = [0]
                    u_high(0)
                    dt_copy(0)
                    dt_e(0)
                    act.wait_ge(su_v, SU_V)
                    for g in range(3):
                        conv_in(0, g)
                    for g in range(3):
                        xbc_th(0, 0, g)
                    for i in range(2):
                        z_th(0, 0, i)
                    a.copy(wout_hi[:, :, :], wout_raw[:, :, :]).then_inc(wo_hi, 1)

                    def body(m, q, before, nxt):
                        QOF[0] = 1 - q
                        if before:
                            y_high(m - 1, 1)
                        tok_major(m, 0)
                        exp_cs(m, 0)
                        if nxt:
                            u_high(m + 1)
                        decays(m, 0)
                        if before:
                            square_sum(m - 1, 1)
                        if nxt:
                            dt_copy(m + 1)
                            dt_e(m + 1)
                            conv_in(m + 1, 0)
                        if before:
                            h2t_copy(m - 1)
                        if nxt:
                            gate_high(m)
                            conv_in(m + 1, 1)
                        tok_major(m, 1)
                        exp_cs(m, 1)
                        y_high(m, 0)
                        if nxt:
                            xbc_th(m + 1, 1 - q, 0)
                            conv_in(m + 1, 2)
                        decays(m, 1)
                        if nxt:
                            xbc_th(m + 1, 1 - q, 1)
                        square_sum(m, 0)
                        if nxt:
                            xbc_th(m + 1, 1 - q, 2)
                            z_th(m + 1, 1 - q, 0)
                            z_th(m + 1, 1 - q, 1)

                    body(0, 0, False, True)
                    with act.Fori(0, NA // 2 - 1) as b:
                        body(b * 2 + 1, 1, True, True)
                        body(b * 2 + 2, 0, True, True)
                    body(NA - 1, 1, True, False)
                    y_high(NA - 1, 1)
                    square_sum(NA - 1, 1)
                    h2t_copy(NA - 1)

                @block.vector
                def _(dve):
                    v = nc.vector
                    n = 0

                    def after(ins):
                        nonlocal n
                        n += 1
                        ins.then_inc(su_v, 1)
                        dve.wait_ge(su_v, n)


                    def ln_stats(m, q):
                        dve.wait_ge(x_in[q], (m - q) * 8 + 16)
                        for t in range(CA):
                            v.bn_stats(st6[:, t, :], x_t[:, q, t, :]).then_inc(stats, 1)

                    def ln_moments(m):
                        if not (isinstance(m, int) and m == 0):
                            dve.wait_ge(h0_ready, m * CA)
                        dve.wait_ge(stats, m * CA + CA)
                        v.memset(idle[:, :], 0.0)
                        for t in range(CA):
                            v.bn_aggr(mom[:, t, :], st6[:, t, :]).then_inc(moments, 1)

                    def ln_out(m, q):
                        if not (isinstance(m, int) and m <= 1):
                            dve.wait_ge(h_ready, (m - 1) * CA)
                        dve.wait_ge(scales, m * 7 + 7)
                        for t in range(CA):
                            v.tensor_scalar(h0[:, q, t, :], x_t[:, q, t, :], mom[:, t, 0:1], rstd[:, t:t + 1],
                                            ALU.subtract, ALU.mult).then_inc(h0_ready, 1)

                    def rms_out(m, q):
                        dve.wait_ge(scales, m * 7 + 7)
                        if not (isinstance(m, int) and m == 0):
                            dve.wait_ge(ut_done, m * 2)
                        for t in range(CA):
                            v.tensor_scalar(u[:, t, :], x_t[:, q, t, :], mom[:, t, 0:1], rr[:, t:t + 1],
                                            ALU.subtract, ALU.mult).then_inc(u_ready, 1)

                    def u_low(m):
                        for i in range(2):
                            dve.wait_ge(uh_ready, m * 2 + i + 1)
                            v.tensor_tensor(u_lo[:, 2 * i:2 * i + 2, :],
                                            b_tp[i][:, :].rearrange("p (k q) -> p k q", k=2),
                                            u_hi[:, 2 * i:2 * i + 2, :].bitcast(F32), ALU.subtract)\
                                .then_inc(ul_ready, 1)

                    def conv(m, q, g):
                        dve.wait_ge(xraw_ready, m * 3 + g + 1)
                        dve.wait_ge(tap_ready, m * 3 + g + 1)
                        dve.wait_ge(halo_ready, m + 1)
                        s = Steps(dve, conv_step, 3 * CONV)
                        s.begin(m)
                        s.k = CONV * g
                        for tap in range(TAPS - 2, -1, -1):
                            for ch in (2 * g, 2 * g + 1):
                                if tap < TAPS - 2:
                                    s.wait(1)
                                s.done(v.scalar_tensor_tensor(xbc[:, q, ch, :], xraw[:, ch, tap:tap + TA],
                                                              convw_sb[:, ch, tap:tap + 1],
                                                              xbc[:, q, ch, :], ALU.mult, ALU.add))

                    def xbc_silu(m, q, g):
                        dve.wait_ge(xtanh, m * 3 + g + 1)
                        flat = xbc[:, q, 2 * g:2 * g + 2, :].rearrange("p c q -> p (c q)")
                        v.scalar_tensor_tensor(flat, xbc_tanh[:, g, :], 1.0, flat, ALU.add, ALU.mult)\
                            .then_inc(xbc_ready, 1)

                    def z_silu(m, q, i):
                        dve.wait_ge(ztanh, m * 2 + i + 1)
                        flat = zs[:, q, 2 * i:2 * i + 2, :].rearrange("p c q -> p (c q)")
                        v.scalar_tensor_tensor(flat, flat, 1.0, b_ip[(q + 3 + i) % 2][:, :],
                                               ALU.add, ALU.mult).then_inc(zs_ready, 1)

                    def dt_chain(m, q):
                        s = Steps(dve, dt_step, DT)
                        s.begin(m)
                        dve.wait_ge(dtp_done, m + 1)
                        b2 = rows_sb[:, H:3 * H]
                        s.done(v.tensor_tensor(pre[:, :], b_misc[:, DT0:DT0 + 2 * H], b2, ALU.add))
                        s.wait()
                        s.done(v.scalar_tensor_tensor(nabs[:, :], pre[:, :], -1.0, pre[:, :], ALU.mult, ALU.min))
                        dve.wait_ge(dt_exp, m + 1)
                        s.done(v.tensor_scalar(s1[:, :], e1[:, :], 2.0, None, ALU.add))
                        s.wait()
                        s.done(v.reciprocal(s1[:, :], s1[:, :]))
                        s.wait()
                        s.done(v.tensor_tensor(s1[:, :], s1[:, :], e1[:, :], ALU.mult))
                        s.wait()
                        s.done(v.tensor_tensor(s2[:, :], s1[:, :], s1[:, :], ALU.mult))
                        s.wait()
                        s.done(v.tensor_scalar(acc[:, :], s2[:, :], 1.0 / (2 * LN1P_TERMS + 1), None, ALU.mult))
                        for k in range(LN1P_TERMS - 1, 0, -1):
                            s.wait()
                            s.done(v.scalar_tensor_tensor(acc[:, :], acc[:, :], 1.0 / (2 * k + 1), s2[:, :],
                                                          ALU.add, ALU.mult))
                        s.wait()
                        s.done(v.scalar_tensor_tensor(acc[:, :], acc[:, :], 1.0, s1[:, :], ALU.add, ALU.mult))
                        s.done(v.tensor_scalar(relu[:, :], pre[:, :], 0.0, None, ALU.max))
                        s.wait()
                        s.done(v.scalar_tensor_tensor(dtv[:, q, :], acc[:, :], 2.0, relu[:, :], ALU.mult, ALU.add))
                        s.wait()
                        s.done(v.tensor_tensor(av[:, q, :], dtv[:, q, :], a_rate[:, :], ALU.mult))
                        s.end()

                    def differences(m, c):
                        dve.wait_ge(ecs_ready, m * CA + c + 1)
                        dve.wait_ge(xb_ready, m * CA + c + 1)
                        if not (isinstance(m, int) and m * CA + c == 0):
                            dve.wait_ge(y_done, m * CA + c)
                        for hh in range(H):
                            v.scalar_tensor_tensor(decay[:, hh * P:hh * P + P], b_cs[:, hh * P:hh * P + P],
                                                   xb_tok[:, 2 * P + hh:2 * P + hh + 1], negmask[:, :],
                                                   ALU.subtract, ALU.add)
                        v.tensor_tensor(wt[:, :], heads(b_cs[:, :])[:, :, P - 1], xb_tok[:, 2 * P:2 * P + H],
                                        ALU.subtract).then_inc(diff_done, 1)

                    def decay_scores(m, q, c):
                        dve.wait_ge(e_ready, (m * CA + c) * 2 + 1)
                        if not (isinstance(m, int) and m * CA + c == 0):
                            dve.wait_ge(xw_ready, m * CA + c)
                        v.tensor_tensor(wk[:, :], wt[:, :], dtv[:, q, c * H:c * H + H], ALU.mult)\
                            .then_inc(wk_ready, 1)
                        dve.wait_ge(e_ready, (m * CA + c) * 2 + 2)
                        dve.wait_ge(g_done, m * CA + c + 1)
                        for hh in range(H):
                            ins = v.scalar_tensor_tensor(decay[:, hh * P:hh * P + P], b_g[:, hh * P:hh * P + P],
                                                         dtv[:, q, c * H + hh:c * H + hh + 1],
                                                         decay[:, hh * P:hh * P + P], ALU.mult, ALU.mult)
                        ins.then_inc(m_ready, 1)

                    def y_gate(m, q, c):
                        dve.wait_ge(y_done, m * CA + c + 1)
                        if not (isinstance(m, int) and m * CA + c == 0):
                            dve.wait_ge(o_done, m * CA + c)
                        for hh in range(H):
                            ins = v.scalar_tensor_tensor(y[:, hh * P:hh * P + P], xbc[:, q, 0, c * P:c * P + P],
                                                         rows_sb[:, 3 * H + hh:3 * H + hh + 1],
                                                         b_y[:, hh * P:hh * P + P], ALU.mult, ALU.add)
                        ins.then_inc(yd_ready, 1)
                        dve.wait_ge(yd_ready, m * CA + c + 1)
                        v.tensor_tensor(heads(y[:, :]), heads(y[:, :]), zs[:, q, :, c * P:c * P + P], ALU.mult)\
                            .then_inc(yg_ready, 1)

                    def state_update(m, q, c):
                        dve.wait_ge(st_done, m * CA + c + 1)
                        dve.wait_ge(cd_ready, m * CA + c + 1)
                        last = q == 1 and c == CA - 1
                        for hh in range(H):
                            ins = v.scalar_tensor_tensor(state[:, hh * P:hh * P + P], state[:, hh * P:hh * P + P],
                                                         ecs[:, hh * P + P - 1:hh * P + P],
                                                         b_cs[:, hh * P:hh * P + P], ALU.mult, ALU.add)
                        if last:
                            ins.then_inc(state_raw, 1)
                            dve.wait_ge(state_raw, (m + 1) // 2 if isinstance(m, int) else QH[0] + 1)
                            ins = v.tensor_scalar(state[:, :], state[:, :], keep[:, bass.ds(m + 1, 1)], None,
                                                  ALU.mult)
                        ins.then_inc(s_upd, 1)

                    def residual(m, q, c):
                        dve.wait_ge(o_done, m * CA + c + 1)
                        if not (isinstance(m, int) and m == 0):
                            dve.wait_ge(a_out, m * 32)
                        v.tensor_tensor(h[:, c, :], b_y[:, :], h0[:, q, c, :], ALU.add).then_inc(h_ready, 1)

                    def h2_norm(m):
                        dve.wait_ge(rms_step, m * 2 + 2)
                        for t in range(CA):
                            v.tensor_scalar(h2[:, t, :], h[:, t, :], rh[:, t:t + 1], None, ALU.mult)\
                                .then_inc(h2_ready, 1)

                    QH = [0]
                    ln_stats(0, 0)
                    ln_moments(0)
                    rms_out(0, 0)
                    ln_out(0, 0)
                    dve.wait_ge(ln_in, 16)
                    for k in range(KD):
                        dve.wait_ge(whi, k + 1)
                        v.scalar_tensor_tensor(win_lo[:, k, :], win_raw[:, k, :], ln_sb[:, k:k + 1],
                                               win_hi[:, k, :].bitcast(F32),
                                               ALU.mult, ALU.subtract).then_inc(wlo, 1)
                    u_low(0)
                    dve.wait_ge(su_a, 1)
                    for k in range(KD):
                        ins = v.scalar_tensor_tensor(wdt_lo[:, k, :], wdt_raw[:, k, :], ln_sb[:, k:k + 1],
                                                     wdt_hi[:, k, :].bitcast(F32), ALU.mult, ALU.subtract)
                    after(ins)
                    dve.wait_ge(c_in, 80)
                    dve.wait_ge(su_a, 3)
                    after(v.tensor_scalar(a_rate[:, :], a_rate[:, :], -1.0, None, ALU.mult))
                    after(v.tensor_scalar(convw_sb[:, :, :].rearrange("p c t -> p (c t)"),
                                          convw_sb[:, :, :].rearrange("p c t -> p (c t)"), 0.5, None, ALU.mult))
                    after(v.tensor_scalar(convb_sb[:, :], convb_sb[:, :], 0.5, None, ALU.mult))
                    after(v.tensor_scalar(wout_raw[:, :, :].rearrange("p h d -> p (h d)"),
                                          wout_raw[:, :, :].rearrange("p h d -> p (h d)"), 0.5, None, ALU.mult))
                    assert n == SU_V
                    ln_stats(1, 1)
                    ln_moments(1)
                    dt_chain(0, 0)
                    for g in range(3):
                        conv(0, 0, g)
                    rms_out(1, 1)
                    for g in range(3):
                        xbc_silu(0, 0, g)
                    for i in range(2):
                        z_silu(0, 0, i)

                    def body(m, q, before, nxt, nxt2):
                        differences(m, 0)
                        if nxt:
                            u_low(m + 1)
                        decay_scores(m, q, 0)
                        if nxt2:
                            ln_stats(m + 2, q)
                        if before:
                            residual(m - 1, 1 - q, 1)
                        if nxt:
                            ln_out(m + 1, 1 - q)
                        if nxt2:
                            ln_moments(m + 2)
                        if before:
                            h2_norm(m - 1)
                        if nxt:
                            dt_chain(m + 1, 1 - q)
                        state_update(m, q, 0)
                        y_gate(m, q, 0)
                        if nxt:
                            conv(m + 1, 1 - q, 0)
                            conv(m + 1, 1 - q, 1)
                            xbc_silu(m + 1, 1 - q, 0)
                        differences(m, 1)
                        if nxt2:
                            rms_out(m + 2, q)
                        decay_scores(m, q, 1)
                        residual(m, q, 0)
                        if nxt:
                            xbc_silu(m + 1, 1 - q, 1)
                            conv(m + 1, 1 - q, 2)
                        state_update(m, q, 1)
                        if nxt:
                            xbc_silu(m + 1, 1 - q, 2)
                        y_gate(m, q, 1)
                        if nxt:
                            z_silu(m + 1, 1 - q, 0)
                            z_silu(m + 1, 1 - q, 1)

                    body(0, 0, False, True, True)
                    with dve.Fori(0, NA // 2 - 2) as b:
                        QH[0] = b
                        body(b * 2 + 1, 1, True, True, True)
                        body(b * 2 + 2, 0, True, True, True)
                    body(NA - 3, 1, True, True, True)
                    body(NA - 2, 0, True, True, False)
                    body(NA - 1, 1, True, False, False)
                    residual(NA - 1, 1, 1)
                    h2_norm(NA - 1)

                @block.tensor
                def _(pe):
                    t_ = nc.tensor

                    def u_transpose(m):
                        pe.wait_ge(u_ready, m * CA + CA)
                        if not (isinstance(m, int) and m == 0):
                            pe.wait_ge(ul_ready, m * 2)
                            if not (isinstance(m, int) and m <= 2):
                                pe.wait_ge(h2t_ready, (m - 2) * 2)
                        for i in range(2):
                            for k in range(2):
                                for t in range(CA):
                                    ins = t_.transpose(b_tp[i][:, k * TA + t * P:k * TA + t * P + P],
                                                       u[:, t, (2 * i + k) * P:(2 * i + k + 1) * P], ident[:, :])
                            ins.then_inc(ut_done, 1)

                    def in_proj(m, q, g):
                        if g < 2:
                            if not (isinstance(m, int) and m == 0):
                                pe.wait_ge(zs_ready, m * 2 - 1 + g)
                        else:
                            pe.wait_ge(tap_ready, m * 3 + g - 1)
                        bank = b_ip[(q + g) % 2]
                        for c in range(2):
                            if g == 0 and c == 1:
                                pe.wait_ge(dth_ready, m + 1)
                            col = (2 * g + c) * P
                            n = 0
                            for k in range(KD):
                                for wv, uv in ((win_hi, u_hi), (win_lo, u_hi), (win_hi, u_lo)):
                                    ins = t_.matmul(bank[:, c * TA:c * TA + TA], wv[:, k, col:col + P], uv[:, k, :],
                                                    start=(n == 0), stop=(n == 3 * KD - 1))
                                    n += 1
                        ins.then_inc(ip_done, 1)

                    def dt_proj(m):
                        pe.wait_ge(ul_ready, m * 2 + 2)
                        if not (isinstance(m, int) and m == 0):
                            pe.wait_ge(xb_ready, m * CA - 1)
                        n = 0
                        for k in range(KD):
                            for wv, uv in ((wdt_hi, u_hi), (wdt_lo, u_hi), (wdt_hi, u_lo)):
                                ins = t_.matmul(b_misc[0:H, 0:TA], wv[:, k, :], uv[:, k, :],
                                                start=(n == 0), stop=(n == 3 * KD - 1))
                                n += 1
                        ins.then_inc(dth_done, 1)

                    def dt_transpose(m):
                        for t in range(CA):
                            ins = t_.transpose(b_misc[:, DT0 + t * H:DT0 + t * H + H], dt_h[:, t * P:t * P + P],
                                               ident[0:H, 0:H])
                        ins.then_inc(dtp_done, 1)

                    def scan_in(m, q, c, nxt):
                        pe.wait_ge(dt_step, m * DT + DT)
                        if c == 1 and nxt:
                            pe.wait_ge(dt_step, m * DT + DT + 1)
                        pe.wait_ge(xbc_ready, m * 3 + 3)
                        if not (isinstance(m, int) and m * CA + c == 0):
                            pe.wait_ge(xb_ready, m * CA + c)
                            pe.wait_ge(s_upd, m * CA + c)
                        tok = slice(c * P, c * P + P)
                        t_.transpose(b_misc[:, 0:P], xbc[:, q, 0, tok], ident[:, :])
                        t_.transpose(b_misc[:, P:2 * P], xbc[:, q, 1, tok], ident[:, :])
                        t_.matmul(b_misc[:, 2 * P:2 * P + H], tri[:, :], av[:, q, c * H:c * H + H],
                                  start=True, stop=True).then_inc(misc_done, 1)
                        pe.wait_ge(atri_ready, m * CA + c + 1)
                        t_.matmul(b_cs[:, :], ones[:, :], atri[:, :], start=True, stop=True).then_inc(csbc_done, 1)
                        if not (isinstance(m, int) and m * CA + c == 0):
                            pe.wait_ge(m_ready, m * CA + c)
                        t_.matmul(b_g[:, :], xbc[:, q, 1, tok], xbc[:, q, 2:6, tok],
                                  start=True, stop=True).then_inc(g_done, 1)

                    def scan_out(m, c):
                        pe.wait_ge(xw_ready, m * CA + c + 1)
                        pe.wait_ge(diff_done, m * CA + c + 1)
                        pe.wait_ge(m_ready, m * CA + c + 1)
                        pe.wait_ge(cd_ready, m * CA + c + 1)
                        if not (isinstance(m, int) and m * CA + c == 0):
                            pe.wait_ge(h_ready, m * CA + c)
                            pe.wait_ge(s_upd, m * CA + c)
                        t_.matmul(b_y[:, :], xb_tok[:, 0:P], decay[:, :], start=True, stop=False)
                        for hh in range(H):
                            ins = t_.matmul(b_y[:, hh * P:hh * P + P], state[:, hh * P:hh * P + P],
                                            c_dec[:, hh * P:hh * P + P], start=False, stop=(hh == H - 1))
                        ins.then_inc(y_done, 1)
                        t_.matmul(b_cs[:, :], xb_tok[:, P:2 * P], xw[:, :], start=True, stop=True)\
                            .then_inc(st_done, 1)

                    def out_proj(m, c):
                        if isinstance(m, int) and m * CA + c == 0:
                            pe.wait_ge(wo_lo, 1)
                        pe.wait_ge(yl_ready, m * CA + c + 1)
                        n = 0
                        for hh in range(H):
                            for yv, wv in ((y_hi, wout_hi), (y_hi, wout_lo), (y_lo, wout_hi)):
                                ins = t_.matmul(b_y[:, :], yv[:, hh * P:hh * P + P], wv[:, hh, :],
                                                start=(n == 0), stop=(n == 3 * H - 1))
                                n += 1
                        ins.then_inc(o_done, 1)

                    def h2_transpose(m):
                        pe.wait_ge(h2_ready, m * CA + CA)
                        if isinstance(m, int) and m == NA - 1:
                            pe.wait_ge(h2t_ready, m * 2)
                        elif isinstance(m, int) and m == NA - 2:
                            pe.wait_ge(ul_ready, NA * 2)
                        else:
                            pe.wait_ge(ul_ready, m * 2 + 4)
                        for i in range(2):
                            for k in range(2):
                                for t in range(CA):
                                    ins = t_.transpose(b_tp[i][:, k * TA + t * P:k * TA + t * P + P],
                                                       h2[:, t, (2 * i + k) * P:(2 * i + k + 1) * P], ident[:, :])
                            ins.then_inc(h2t_done, 1)

                    pe.wait_ge(su_g, SU_G)
                    u_transpose(0)
                    pe.wait_ge(su_v, SU_V)
                    dt_proj(0)
                    pe.wait_ge(wlo, KD)
                    for g in range(NPAIR):
                        in_proj(0, 0, g)
                        if g == 0:
                            dt_transpose(0)

                    def body(m, q, before, nxt):
                        scan_in(m, q, 0, nxt)
                        if nxt:
                            u_transpose(m + 1)
                        if before:
                            out_proj(m - 1, 1)
                        if nxt:
                            dt_proj(m + 1)
                            in_proj(m + 1, 1 - q, 0)
                            dt_transpose(m + 1)
                        scan_out(m, 0)
                        if before:
                            h2_transpose(m - 1)
                        if nxt:
                            in_proj(m + 1, 1 - q, 1)
                        scan_in(m, q, 1, nxt)
                        if nxt:
                            in_proj(m + 1, 1 - q, 2)
                        out_proj(m, 0)
                        if nxt:
                            in_proj(m + 1, 1 - q, 3)
                        scan_out(m, 1)
                        if nxt:
                            in_proj(m + 1, 1 - q, 4)

                    body(0, 0, False, True)
                    with pe.Fori(0, NA // 2 - 1) as b:
                        body(b * 2 + 1, 1, True, True)
                        body(b * 2 + 2, 0, True, True)
                    body(NA - 1, 1, True, False)
                    out_proj(NA - 1, 1)
                    h2_transpose(NA - 1)

        with ExitStack() as st:
            sb(st, "h2_raw_place", [P, KD, TB])
            up_hi = sb(st, "up_hi", [P, NJ, KD * P], F32R)
            up_lo, up_raw = over_raw(st, "up", [P, NJ, KD * P])
            down_sb = sb(st, "down_sb", [P, NJ, D])
            h2_hi = sb(st, "h2_hi", [P, KD, TB], F32R)
            h2_lo = sb(st, "h2_lo", [P, KD, TB], F32R)
            hm = sb(st, "hm", [P, CB, D])
            x1 = sb(st, "x1", [P, CB, D])
            xn = sb(st, "xn", [P, CB, D])
            th = sb(st, "th", [P, TB])
            glu = sb(st, "glu", [P, 2, TB])
            tr = sb(st, "tr", [P, D])
            prod = tr
            mix = sb(st, "mix", [P, CB, D])
            wlog = sb(st, "wlog", [P, KD, NLOG])
            wbr = sb(st, "wbr", [P, P])
            sg = sb(st, "sg", [P, 4])
            eye = sb(st, "eye", [P, 4, 2, 4])
            b6 = sb(st, "b6", [P, CB, 6])
            bm = sb(st, "bm", [P, CB, 2])
            bv = sb(st, "bv", [P, CB])
            br = sb(st, "br", [P, CB])
            bq = sb(st, "bq", [P, CB])
            bx = sb(st, "bx", [P, CB])
            f6 = sb(st, "f6", [P, CB, 6])
            fm = sb(st, "fm", [P, CB, 2])
            fv = sb(st, "fv", [P, CB])
            fr = sb(st, "fr", [P, CB])
            fs = sb(st, "fs", [P, CB])
            lg = sb(st, "lg", [P, CB, NLOG])
            sm = sb(st, "sm", [P, CB, 8])
            smx = sb(st, "smx", [P, CB, 2])
            zl = sb(st, "zl", [P, 2, 4, 2, 4])
            ze = sb(st, "ze", [P, 2, 4, 2, 4])
            pm = sb(st, "pm", [P, 2, 4, 2, 4])
            rowv = sb(st, "rowv", [P, 2, 4, 2])
            colv = sb(st, "colv", [P, 2, 2, 4])

            b_gate, b_up = banks[0], banks[1]
            b_down = banks[2:6]
            b_tr, b_lg = banks[6], banks[7]

            k_in = sem("b_constants_loaded")
            UP_LOADS = [(0, 1), (1, 2), (2, 4), (4, 8), (8, NJ)]
            DOWN_LOADS = [(0, 2), (2, NJ)]
            ur_in = [sem(f"up_load{i}_done") for i in range(len(UP_LOADS))]
            dn_in = [sem(f"down_load{i}_done") for i in range(len(DOWN_LOADS))]
            up_h = sem("up_hi_ready")
            up_l = sem("up_lo_ready")
            b_su = sem("b_setup_steps")
            hm_in = sem("h_loaded")
            xb_in = [sem(f"x_part{t}_loaded") for t in range(CB)]
            hh_ready = sem("h2_hi_ready")
            hl_ready = sem("h2_lo_ready")
            gate_done = sem("gate_product_done")
            up_done = sem("up_product_done")
            th_ready = sem("gate_silu_ready")
            glu_ready = sem("glu_ready")
            down_done = sem("down_product_done")
            mo_ready = sem("mlp_output_ready")
            c_step = sem("mhc_vector_steps")
            mom_b = sem("mlp_output_moments_ready")
            lnb = sem("mlp_output_scale_ready")
            nb_ready = sem("mlp_output_normalized")
            x1_ready = sem("x1_ready")
            mom_x = sem("x1_moments_ready")
            lnx = sem("x1_scale_steps")
            xn_ready = sem("streams_ready")
            xt_done = sem("streams_transposed")
            xt_ready = sem("streams_transpose_copied")
            lg_done = sem("logits_done")
            sm_in = sem("softmax_inputs_ready")
            sm_exp = sem("softmax_exps_ready")
            z_in = sem("sinkhorn_inputs_ready")
            z_exp = sem("sinkhorn_exps_ready")
            xp_ready = sem("x_pre_ready")
            xpt_done = sem("x_pre_transposed")
            xpt_ready = sem("x_pre_transpose_copied")
            br_done = sem("branch_product_done")
            mom_f = sem("mix_moments_ready")
            lnf = sem("mix_scale_ready")
            fin_n = sem("mix_normalized")
            fin = sem("tile_output_ready")
            hres_ready = sem("stream_mixers_ready")
            ym_ready = sem("branch_share_ready")
            pool_mix = sem("gpsimd_mixing_steps")
            prod_ready = sem("mixing_products_ready")
            b_out = sem("outputs_stored")

            with nc.Block() as block:

                @block.sync
                def _(sp):
                    def load_h2(m):
                        sp.wait_ge(hl_ready, m * KD)
                        for uu in range(2):
                            sp.dma_start(h2_raw[:, :, uu * TA:uu * TA + TA],
                                         at_tile(h2t_scr_b[:, uu], m)).then_inc(h2_in, 16)

                    def load_hm(m):
                        if not (isinstance(m, int) and m == 0):
                            sp.wait_ge(x1_ready, m * CB)
                        for uu in range(2):
                            sp.dma_start(hm[:, 2 * uu:2 * uu + 2, :], at_tile(h_scr_b[:, uu], m))\
                                .then_inc(hm_in, 16)

                    def load_x(m, t):
                        sp.dma_start(x1[:, t, :], at_tile(x_b[:, :, t], m)).then_inc(xb_in[t], 16)

                    def store(m, nxt):
                        for t in range(CB):
                            sp.wait_ge(fin, m * CB + t + 1)
                            sp.dma_start(at_tile(out_b[:, :, t], m), mix[:, t, :]).then_inc(b_out, 16)
                            if nxt:
                                load_x(m + 1, t)

                    def load_up(i):
                        j0, j1 = UP_LOADS[i]
                        sp.dma_start(up_raw[:, j0:j1, :], up_w[:, j0:j1, :]).then_inc(ur_in[i], 16)

                    def load_down(i):
                        j0, j1 = DOWN_LOADS[i]
                        sp.dma_start(down_sb[:, j0:j1, :], down_w[:, j0:j1, :]).then_inc(dn_in[i], 16)

                    for i in range(3):
                        load_up(i)
                    load_down(0)
                    load_up(3)
                    load_down(1)
                    load_up(4)
                    sp.dma_start(wlog[:, :, :], w_logit).then_inc(k_in, 16)
                    sp.dma_start(wbr[:, :], w_branch).then_inc(k_in, 16)
                    load_hm(0)
                    for t in range(CB):
                        load_x(0, t)
                    load_h2(1)
                    with sp.Fori(1, NB - 1) as m:
                        load_hm(m)
                        load_h2(m + 1)
                        store(m - 1, True)
                    load_hm(NB - 1)
                    store(NB - 2, True)
                    store(NB - 1, False)
                    sp.wait_ge(b_out, 16 * TOK // P)

                @block.gpsimd
                def _(pool):
                    g = nc.gpsimd

                    def out_scale(m):
                        pool.wait_ge(mom_b, m * CB + CB)
                        g.tensor_tensor(bv[:, :], bm[:, :, 1], epsc[:, :], ALU.add).then_inc(lnb, 1)
                        pool.wait_ge(lnb, m * 2 + 1)
                        g.tensor_tensor(br[:, :], bv[:, :], halfc[:, :], ALU.pow).then_inc(lnb, 1)

                    def x1_add(m):
                        for t in range(CB):
                            pool.wait_ge(xb_in[t], m * 16 + 16)
                            pool.wait_ge(nb_ready, m * CB + t + 1)
                            g.tensor_tensor(x1[:, t, :], x1[:, t, :], hm[:, t, :], ALU.add).then_inc(x1_ready, 1)

                    def x1_scales(m):
                        s = Steps(pool, lnx, 6)
                        s.begin(m)
                        pool.wait_ge(mom_x, m * CB + CB)
                        s.done(g.tensor_tensor(bv[:, :], bm[:, :, 1], epsc[:, :], ALU.add))
                        s.wait()
                        s.done(g.tensor_tensor(br[:, :], bv[:, :], halfc[:, :], ALU.pow))
                        s.wait()
                        s.done(g.tensor_tensor(bq[:, :], br[:, :], br[:, :], ALU.mult))
                        s.wait()
                        s.done(g.tensor_tensor(bq[:, :], bq[:, :], bm[:, :, 1], ALU.mult))
                        s.wait()
                        s.done(g.tensor_tensor(bq[:, :], bq[:, :], epsm[:, :], ALU.add))
                        s.wait()
                        s.done(g.tensor_tensor(bx[:, :], bq[:, :], halfc[:, :], ALU.pow))
                        s.end()

                    def pool_mixing(m):
                        t = CB - 1
                        s = Steps(pool, pool_mix, 8)
                        s.begin(m)
                        pool.wait_ge(hres_ready, m * 2 + 2)
                        pool.wait_ge(ym_ready, m * CB + CB)
                        for jj in range(4):
                            hcol = pm[:, t // 2, :, t % 2, jj:jj + 1].broadcast_to([P, 4, P])
                            xj = xn[:, t, jj * P:jj * P + P].rearrange("p (o q) -> p o q", o=1).broadcast_to([P, 4, P])
                            if jj > 0:
                                s.wait()
                            s.done(g.tensor_tensor(heads(prod[:, :]), xj, hcol, ALU.mult))
                            s.wait()
                            s.done(g.tensor_tensor(mix[:, t, :], mix[:, t, :], prod[:, :], ALU.add))
                        s.end()

                    def pool_mixing_last(m):
                        s = Steps(pool, pool_mix, 8)
                        s.begin(m)
                        pool.wait_ge(ym_ready, m * CB + CB)
                        for n in range(8):
                            pool.wait_ge(prod_ready, n + 1)
                            if n > 0:
                                s.wait()
                            mt = mix[:, CB - 2 + n // 4, :]
                            s.done(g.tensor_tensor(mt, mt, (tr, th)[n % 2][:, :], ALU.add))
                            if n == 4:
                                mix_scale(m, 0)
                        s.end()

                    def mix_scale(m, t):
                        i = m * CB + t
                        pool.wait_ge(mom_f, i + 1)
                        g.tensor_tensor(fv[:, t:t + 1], fm[:, t, 1:2], epsc[:, 0:1], ALU.add)\
                            .then_inc(lnf, 1)
                        pool.wait_ge(lnf, i * 4 + 1)
                        g.tensor_tensor(fr[:, t:t + 1], fv[:, t:t + 1], halfc[:, 0:1], ALU.pow)\
                            .then_inc(lnf, 1)
                        pool.wait_ge(lnf, i * 4 + 2)
                        g.tensor_tensor(fs[:, t:t + 1], fm[:, t, 0:1], fr[:, t:t + 1], ALU.mult).then_inc(lnf, 1)
                        pool.wait_ge(lnf, i * 4 + 3)
                        g.tensor_tensor(fs[:, t:t + 1], zeroc[:, 0:1], fs[:, t:t + 1], ALU.subtract)\
                            .then_inc(lnf, 1)

                    def final_add(m, t):
                        pool.wait_ge(fin_n, m * CB + t + 1)
                        g.tensor_tensor(mix[:, t, :], mix[:, t, :], x1[:, t, :], ALU.add)\
                            .then_inc(fin, 1)

                    def mhc(m):
                        out_scale(m)
                        x1_add(m)
                        x1_scales(m)
                        if isinstance(m, int):
                            pool_mixing_last(m)
                            for t in range(1, CB):
                                mix_scale(m, t)
                            return
                        pool_mixing(m)
                        for t in range(CB):
                            mix_scale(m, t)
                            if t > 0:
                                final_add(m, t - 1)
                        final_add(m, CB - 1)

                    with pool.Fori(0, NB - 1) as m:
                        mhc(m)
                    mhc(NB - 1)

                @block.scalar
                def _(act):
                    a = nc.scalar
                    def up_high(j):
                        for i, (j0, j1) in enumerate(UP_LOADS):
                            if j0 == j:
                                act.wait_ge(ur_in[i], 16)
                        a.copy(up_hi[:, j, :], up_raw[:, j, :]).then_inc(up_h, 1)

                    act.wait_ge(h2_in, 32)
                    for k in range(KD):
                        a.copy(h2_hi[:, k, :], h2_raw[:, k, :]).then_inc(hh_ready, 1)
                    a.activation(sg[:, 0:1], rows_sb[:, 16:17], ACT.Exp, scale=-1.0).then_inc(b_su, 1)
                    up_high(0)
                    up_high(1)

                    def h2_high(m):
                        act.wait_ge(h2_in, m * 32 + 32)
                        act.wait_ge(up_done, m * NJ)
                        for k in range(KD):
                            a.copy(h2_hi[:, k, :], h2_raw[:, k, :]).then_inc(hh_ready, 1)

                    def gate_silu(m, j):
                        act.wait_ge(gate_done, m * NJ + j + 1)
                        if not (isinstance(m, int) and m * NJ + j == 0):
                            act.wait_ge(glu_ready, m * NJ + j)
                        a.activation(th[:, :], b_gate[:, :], ACT.Silu).then_inc(th_ready, 1)

                    def tr_copy(m, t):
                        i = m * CB + t
                        last = isinstance(m, int) and m == NB - 1
                        act.wait_ge(xt_done, i + 1)
                        if last and t >= 2:
                            act.wait_ge(lg_done, i - 1)
                        elif last and t == 1:
                            act.wait_ge(glu_ready, NB * NJ)
                        elif not (isinstance(m, int) and i == 0):
                            act.wait_ge(lg_done, i)
                        if last and t % 2:
                            a.copy(th[:, :], b_up[:, :]).then_inc(xt_ready, 1)
                        else:
                            a.copy(tr[:, :], b_tr[:, :]).then_inc(xt_ready, 1)

                    def softmax_exp(m):
                        act.wait_ge(sm_in, m + 1)
                        a.activation(sm[:, :, :], sm[:, :, :], ACT.Exp).then_inc(sm_exp, 1)

                    def sink_exp(m):
                        act.wait_ge(z_in, m * 2 + 2)
                        a.activation(ze[:, :, :, :], zl[:, :, :, :], ACT.Exp).then_inc(z_exp, 1)
                        act.wait_ge(z_in, m * 2 + 2)
                        a.activation(pm[:, :, :, :], pm[:, :, :, :], ACT.Exp).then_inc(z_exp, 1)

                    def xpre_copy(m, t):
                        i = m * CB + t
                        act.wait_ge(xpt_done, i + 1)
                        if t > 0:
                            act.wait_ge(br_done, i)
                        else:
                            act.wait_ge(lg_done, i + CB)
                        a.copy(tr[:, 0:P], b_lg[:, 0:P]).then_inc(xpt_ready, 1)

                    def branch_share(m, t):
                        i = m * CB + t
                        act.wait_ge(br_done, i + 1)
                        for ii in range(4):
                            ins = a.activation(mix[:, t, ii * P:ii * P + P], b_lg[:, P:2 * P], ACT.Copy,
                                               scale=sm[:, t, 4 + ii:5 + ii])
                        ins.then_inc(ym_ready, 1)

                    def products(m):
                        act.wait_ge(hres_ready, m * 2 + 2)
                        for n in range(8):
                            t, jj = CB - 2 + n // 4, n % 4
                            if n >= 2:
                                act.wait_ge(pool_mix, m * 8 + n - 1)
                            for ii in range(4):
                                ins = a.activation((tr, th)[n % 2][:, ii * P:ii * P + P],
                                                   xn[:, t, jj * P:jj * P + P], ACT.Copy,
                                                   scale=pm[:, t // 2, ii, t % 2, jj:jj + 1])
                            ins.then_inc(prod_ready, 1)

                    def mix_norm(m, t):
                        i = m * CB + t
                        act.wait_ge(lnf, i * 4 + 4)
                        a.activation(mix[:, t, :], mix[:, t, :], ACT.Identity, bias=fs[:, t:t + 1],
                                     scale=fr[:, t:t + 1]).then_inc(fin_n, 1)

                    def body(m, mlp, mhc, c):
                        for j in range(NJ):
                            if mlp and not mhc and j + 2 < NJ:
                                up_high(j + 2)
                            if mhc and j == 2:
                                tr_copy(c, 0)
                            if mlp:
                                gate_silu(m, j)
                            if mhc:
                                if j == 2:
                                    for t in range(1, CB):
                                        tr_copy(c, t)
                                    softmax_exp(c)
                                    sink_exp(c)
                                if 5 <= j < 5 + CB:
                                    xpre_copy(c, j - 5)
                                    branch_share(c, j - 5)
                        if mlp:
                            h2_high(m + 1) if not isinstance(m, int) or m < NB - 1 else None
                        if mhc:
                            if not mlp:
                                products(c)
                            for t in range(CB):
                                mix_norm(c, t)

                    body(0, True, False, 0)
                    with act.Fori(1, NB - 1) as m:
                        body(m, True, True, m - 1)
                    body(NB - 1, True, True, NB - 2)
                    body(0, False, True, NB - 1)

                @block.vector
                def _(dve):
                    v = nc.vector

                    def up_low(j):
                        dve.wait_ge(up_h, j + 1)
                        v.tensor_tensor(up_lo[:, j, :], up_raw[:, j, :],
                                        up_hi[:, j, :].bitcast(F32), ALU.subtract).then_inc(up_l, 1)

                    for k in range(KD):
                        dve.wait_ge(hh_ready, k + 1)
                        v.tensor_tensor(h2_lo[:, k, :], h2_raw[:, k, :], h2_hi[:, k, :].bitcast(F32),
                                        ALU.subtract).then_inc(hl_ready, 1)
                    up_low(0)
                    up_low(1)
                    n = 1

                    def after(ins):
                        nonlocal n
                        n += 1
                        ins.then_inc(b_su, 1)
                        dve.wait_ge(b_su, n)

                    dve.wait_ge(b_su, 1)
                    after(v.tensor_scalar(sg[:, 1:2], sg[:, 0:1], 1.0, None, ALU.add))
                    after(v.reciprocal(sg[:, 2:3], sg[:, 1:2]))
                    after(v.tensor_scalar(sg[:, 3:4], sg[:, 2:3], -1.0, 1.0, ALU.mult, ALU.add))
                    after(v.memset(eye[:, :, :, :], 0.0))
                    for i in range(4):
                        after(v.tensor_scalar(eye[:, i, :, i], eye[:, i, :, i], sg[:, 3:4], None, ALU.add))

                    def h2_low(m):
                        for k in range(KD):
                            dve.wait_ge(hh_ready, m * KD + k + 1)
                            v.tensor_tensor(h2_lo[:, k, :], h2_raw[:, k, :], h2_hi[:, k, :].bitcast(F32),
                                            ALU.subtract).then_inc(hl_ready, 1)

                    def gate_up(m, j):
                        i = m * NJ + j
                        dve.wait_ge(th_ready, i + 1)
                        dve.wait_ge(up_done, i + 1)
                        if not (isinstance(m, int) and i < 2):
                            dve.wait_ge(down_done, i - 1)
                        v.tensor_tensor(glu[:, j % 2, :], th[:, :], b_up[:, :], ALU.mult)\
                            .then_inc(glu_ready, 1)

                    def mlp_out(m):
                        dve.wait_ge(down_done, m * NJ + NJ)
                        dve.wait_ge(hm_in, m * 32 + 32)
                        for t in range(CB):
                            v.tensor_tensor(hm[:, t, :], b_down[t][:, :], hm[:, t, :], ALU.add)\
                                .then_inc(mo_ready, 1)

                    s = Steps(dve, c_step, 0)

                    def step(ins, wait=True):
                        s.done(ins)
                        if wait:
                            s.wait()

                    def norm_stats(m):
                        for t in range(CB):
                            dve.wait_ge(mo_ready, m * CB + t + 1)
                            step(v.bn_stats(b6[:, t, :], hm[:, t, :]), wait=False)
                        s.wait()
                        v.memset(idle[:, :], 0.0)
                        for t in range(CB):
                            v.bn_aggr(bm[:, t, :], b6[:, t, :]).then_inc(mom_b, 1)

                    def norm_apply(m):
                        dve.wait_ge(lnb, m * 2 + 2)
                        for t in range(CB):
                            v.tensor_scalar(hm[:, t, :], hm[:, t, :], bm[:, t, 0:1], br[:, t:t + 1],
                                            ALU.subtract, ALU.mult).then_inc(nb_ready, 1)

                    def streams_stats(m):
                        for t in range(CB):
                            dve.wait_ge(x1_ready, m * CB + t + 1)
                            step(v.bn_stats(b6[:, t, :], x1[:, t, :]), wait=False)
                        s.wait()
                        v.memset(idle[:, :], 0.0)
                        for t in range(CB):
                            v.bn_aggr(bm[:, t, :], b6[:, t, :]).then_inc(mom_x, 1)

                    def streams_apply(m):
                        dve.wait_ge(lnx, m * 6 + 2)
                        for t in range(CB):
                            v.tensor_scalar(xn[:, t, :], x1[:, t, :], bm[:, t, 0:1], br[:, t:t + 1],
                                            ALU.subtract, ALU.mult).then_inc(xn_ready, 1)

                    def logits(m):
                        dve.wait_ge(lnx, m * 6 + 6)
                        dve.wait_ge(lg_done, m * CB + CB)
                        for t in range(CB):
                            step(v.scalar_tensor_tensor(lg[:, t, :], b_lg[:, t * NLOG:(t + 1) * NLOG],
                                                        bx[:, t:t + 1], rows_sb[:, 17:17 + NLOG],
                                                        ALU.mult, ALU.add), wait=(t == CB - 1))
                        pp = lg[:, :, 16:24].rearrange("p t (s j) -> p t s j", s=2)
                        sm4 = sm[:, :, :].rearrange("p t (s j) -> p t s j", s=2)
                        mx = smx[:, :, :].rearrange("p t (s o) -> p t s o", o=1)
                        step(v.tensor_reduce(smx[:, :, :], pp, AX.X, ALU.max))
                        v.tensor_tensor(sm4, pp, mx.broadcast_to([P, CB, 2, 4]), ALU.subtract).then_inc(sm_in, 1)
                        for t in range(CB):
                            step(v.tensor_scalar(zl[:, t // 2, :, t % 2, :],
                                                 lg[:, t, 0:16].rearrange("p (i j) -> p i j", i=4),
                                                 10.0, None, ALU.mult), wait=(t == CB - 1))
                        both(lambda c: v.tensor_reduce(rowv[:, c, :, :], zl[:, c, :, :, :], AX.X, ALU.max))
                        both(lambda c: v.tensor_tensor(by_row(zl, c), by_row(zl, c), row_b(c), ALU.subtract))
                        both(lambda c: v.tensor_reduce(colv[:, c, :, :], by_col(zl, c), AX.X, ALU.max))
                        s.wait()
                        for c in range(2):
                            v.scalar_tensor_tensor(flat_i(pm, c), flat_i(zl, c), SHIFT, col_b(c),
                                                   ALU.add, ALU.subtract).then_inc(z_in, 1)

                    def flat_i(z, c):
                        return z[:, c, :, :, :].rearrange("p i t j -> p i (t j)")

                    def by_row(z, c):
                        return z[:, c, :, :, :].rearrange("p i t j -> p (i t) j")

                    def by_col(z, c):
                        return z[:, c, :, :, :].rearrange("p i t j -> p t j i")

                    def row_b(c):
                        return rowv[:, c, :, :].rearrange("p i (t o) -> p (i t) o", o=1).broadcast_to([P, 8, 4])

                    def col_b(c):
                        return colv[:, c, :, :].rearrange("p (o t) j -> p o (t j)", o=1).broadcast_to([P, 4, 8])

                    def both(op):
                        for c in range(2):
                            s.wait(1)
                            s.done(op(c))

                    def softmax_finish(m):
                        sm4 = sm[:, :, :].rearrange("p t (s j) -> p t s j", s=2)
                        mx = smx[:, :, :].rearrange("p t (s o) -> p t s o", o=1)
                        dve.wait_ge(sm_exp, m + 1)
                        step(v.tensor_reduce(smx[:, :, :], sm4, AX.X, ALU.add))
                        step(v.reciprocal(smx[:, :, :], smx[:, :, :]))
                        step(v.tensor_tensor(sm4, sm4, mx.broadcast_to([P, CB, 2, 4]), ALU.mult))

                    def sink_first(m):
                        dve.wait_ge(z_exp, m * 2 + 1)
                        both(lambda c: v.tensor_reduce(rowv[:, c, :, :], ze[:, c, :, :, :], AX.X, ALU.add))
                        both(lambda c: v.reciprocal(rowv[:, c, :, :], rowv[:, c, :, :]))
                        dve.wait_ge(z_exp, m * 2 + 2)
                        both(lambda c: v.tensor_tensor(by_row(pm, c), by_row(pm, c), row_b(c), ALU.mult))

                    def sink_row():
                        both(lambda c: v.tensor_reduce(rowv[:, c, :, :], pm[:, c, :, :, :], AX.X, ALU.add))
                        both(lambda c: v.reciprocal(rowv[:, c, :, :], rowv[:, c, :, :]))
                        both(lambda c: v.scalar_tensor_tensor(by_row(pm, c), row_b(c), SCALE_UP, by_row(pm, c),
                                                              ALU.mult, ALU.mult))

                    def sink_col(last=False):
                        both(lambda c: v.tensor_reduce(colv[:, c, :, :], by_col(pm, c), AX.X, ALU.add))
                        both(lambda c: v.reciprocal(colv[:, c, :, :], colv[:, c, :, :]))
                        both(lambda c: v.scalar_tensor_tensor(flat_i(pm, c), col_b(c), 1.0 if last else SCALE_UP,
                                                              flat_i(pm, c), ALU.mult, ALU.mult))

                    def sink_end(m):
                        s.wait()
                        for c in range(2):
                            flat = pm[:, c, :, :, :].rearrange("p i t j -> p (i t j)")
                            v.scalar_tensor_tensor(flat, flat, sg[:, 2:3],
                                                   eye[:, :, :, :].rearrange("p i t j -> p (i t j)"),
                                                   ALU.mult, ALU.add).then_inc(hres_ready, 1)
                        dve.wait_ge(hres_ready, m * 2 + 2)

                    def x_pre(m):
                        if not (isinstance(m, int) and m == 0):
                            dve.wait_ge(b_out, m * 16 * CB)
                        for t0 in range(0, CB, 2):
                            for n4 in range(4):
                                for t in (t0, t0 + 1):
                                    src, wgt = xn[:, t, n4 * P:n4 * P + P], sm[:, t, n4:n4 + 1]
                                    if n4 == 0:
                                        s.done(v.tensor_scalar(mix[:, t, 0:P], src, wgt, None, ALU.mult))
                                        continue
                                    s.wait(1 if n4 < 3 or t == t0 else 0)
                                    ins = v.scalar_tensor_tensor(mix[:, t, 0:P], src, wgt, mix[:, t, 0:P],
                                                                 ALU.mult, ALU.add)
                                    if n4 < 3:
                                        s.done(ins)
                                    else:
                                        ins.then_inc(xp_ready, 1)

                    def mix_stats(m, t):
                        step(v.bn_stats(f6[:, t, :], mix[:, t, :]), wait=False)
                        s.wait()
                        v.memset(idle[:, :], 0.0)
                        v.bn_aggr(fm[:, t, :], f6[:, t, :]).then_inc(mom_f, 1)

                    def mixing(m, t):
                        dve.wait_ge(ym_ready, m * CB + t + 1)
                        for jj in range(4):
                            for ii in range(4):
                                dst = mix[:, t, ii * P:ii * P + P]
                                if jj > 0:
                                    s.wait(3)
                                step(v.scalar_tensor_tensor(dst, xn[:, t, jj * P:jj * P + P],
                                                            pm[:, t // 2, ii, t % 2, jj:jj + 1], dst,
                                                            ALU.mult, ALU.add), wait=False)
                        s.wait()
                        mix_stats(m, t)

                    def final_add(m, t):
                        dve.wait_ge(fin_n, m * CB + t + 1)
                        v.tensor_tensor(mix[:, t, :], mix[:, t, :], x1[:, t, :], ALU.add).then_inc(fin, 1)

                    halves = [0]

                    def sinkhorn(upto):
                        while halves[0] < min(upto, 2 * SINK):
                            k = halves[0]
                            if k % 2 == 0:
                                sink_row()
                            else:
                                sink_col(last=(k == 2 * SINK - 1))
                            halves[0] += 1

                    PACE = {2: 6, 3: 18, 4: 26, **{j: 26 + 12 * (j - 4) for j in range(5, 11)}}

                    def body(m, mlp, mhc, c):
                        if mhc:
                            dve.sem_clear(c_step)
                            s.begin(0)
                        for j in range(NJ):
                            if mhc and j == 0:
                                norm_stats(c)
                            if mlp and not mhc and j + 2 < NJ:
                                up_low(j + 2)
                            if mlp:
                                gate_up(m, j)
                            if mhc:
                                if j == 0:
                                    norm_apply(c)
                                    streams_stats(c)
                                if j == 1:
                                    streams_apply(c)
                                if j == 2:
                                    logits(c)
                                    softmax_finish(c)
                                    sink_first(c)
                                    halves[0] = 1
                                if j == 4:
                                    x_pre(c)
                                if j in PACE:
                                    sinkhorn(PACE[j])
                                if j == 11:
                                    sinkhorn(2 * SINK)
                                    sink_end(c)
                                if 11 <= j < (14 if mlp else 13):
                                    mixing(c, j - 11)
                            if mlp and j == 13:
                                if not isinstance(m, int) or m < NB - 1:
                                    h2_low(m + 1)
                            if mhc:
                                if j == 13:
                                    if not mlp:
                                        dve.wait_ge(pool_mix, c * 8 + 4)
                                        mix_stats(c, CB - 2)
                                    dve.wait_ge(pool_mix, c * 8 + 8)
                                    mix_stats(c, CB - 1)
                                    if not mlp:
                                        for t in range(CB):
                                            final_add(c, t)
                        if mhc:
                            s.wait()
                        if mlp:
                            mlp_out(m)

                    body(0, True, False, 0)
                    with dve.Fori(1, NB - 1) as m:
                        body(m, True, True, m - 1)
                    body(NB - 1, True, True, NB - 2)
                    body(0, False, True, NB - 1)

                @block.tensor
                def _(pe):
                    t_ = nc.tensor

                    def product(m, j, bank, w_hi, w_lo, signal, fresh=False, midway=None):
                        n = 0
                        for k in range(KD):
                            if k == KD // 2 and midway:
                                midway()
                            if fresh:
                                pe.wait_ge(hl_ready, m * KD + k + 1)
                            for wv, hv in ((w_hi, h2_hi), (w_lo, h2_hi), (w_hi, h2_lo)):
                                ins = t_.matmul(bank[:, :], wv[:, j, k * P:k * P + P], hv[:, k, :],
                                                start=(n == 0), stop=(n == 3 * KD - 1))
                                n += 1
                        ins.then_inc(signal, 1)

                    def gate(m, j, midway=None):
                        i = m * NJ + j
                        if not (isinstance(m, int) and i == 0):
                            pe.wait_ge(th_ready, i)
                        product(m, j, b_gate, gate_hi, gate_lo, gate_done, j == 0, midway)

                    def up(m, j, first, midway=None):
                        i = m * NJ + j
                        if first:
                            pe.wait_ge(up_l, j + 1)
                        if not (isinstance(m, int) and i == 0):
                            pe.wait_ge(glu_ready, i)
                        product(m, j, b_up, up_hi, up_lo, up_done, midway=midway)

                    def down(m, j):
                        i = m * NJ + j
                        pe.wait_ge(glu_ready, i + 1)
                        if j == 0:
                            if not (isinstance(m, int) and m == 0):
                                pe.wait_ge(mo_ready, m * CB)
                        if isinstance(m, int) and m == 0:
                            for i, (j0, j1) in enumerate(DOWN_LOADS):
                                if j0 == j:
                                    pe.wait_ge(dn_in[i], 16)
                        for t in range(CB):
                            ins = t_.matmul(b_down[t][:, :], glu[:, j % 2, t * P:t * P + P], down_sb[:, j, :],
                                            start=(j == 0), stop=(j == NJ - 1))
                        ins.then_inc(down_done, 1)

                    def stream_transpose(c, t):
                        i = c * CB + t
                        last = isinstance(c, int) and c == NB - 1
                        pe.wait_ge(xn_ready, i + 1)
                        if last and t == 1:
                            pe.wait_ge(glu_ready, NB * NJ)
                        elif last and t >= 2:
                            pe.wait_ge(xt_ready, i - 1)
                        elif not (isinstance(c, int) and i == 0):
                            pe.wait_ge(xt_ready, i)
                        bank = b_up if last and t % 2 else b_tr
                        for k in range(KD):
                            ins = t_.transpose(bank[:, k * P:k * P + P], xn[:, t, k * P:k * P + P], ident[:, :])
                        ins.then_inc(xt_done, 1)

                    def stream_logits(c, t):
                        i = c * CB + t
                        if t == 0 and not (isinstance(c, int) and c == 0):
                            pe.wait_ge(ym_ready, i)
                        if t == 0:
                            pe.wait_ge(k_in, 32)
                        pe.wait_ge(xt_ready, i + 1)
                        src = th if isinstance(c, int) and c == NB - 1 and t % 2 else tr
                        for k in range(KD):
                            ins = t_.matmul(b_lg[:, t * NLOG:(t + 1) * NLOG], src[:, k * P:k * P + P],
                                            wlog[:, k, :], start=(k == 0), stop=(k == KD - 1))
                        ins.then_inc(lg_done, 1)

                    def branch_transpose(c, t):
                        i = c * CB + t
                        pe.wait_ge(xp_ready, i + 1)
                        if t > 0:
                            pe.wait_ge(ym_ready, i)
                        t_.transpose(b_lg[:, 0:P], mix[:, t, 0:P], ident[:, :]).then_inc(xpt_done, 1)

                    def branch(c, t):
                        pe.wait_ge(xpt_ready, c * CB + t + 1)
                        t_.matmul(b_lg[:, P:2 * P], tr[:, 0:P], wbr[:, :], start=True, stop=True)\
                            .then_inc(br_done, 1)

                    def body(m, mlp, mhc, c, first):
                        for j in range(NJ):
                            def streams(t):
                                if not mlp and t < CB:
                                    stream_transpose(c, t)
                                if t > 0:
                                    stream_logits(c, t - 1)
                                if mlp and t < CB:
                                    stream_transpose(c, t)

                            if mhc and j == 3:
                                streams(4)
                            if mlp:
                                gate(m, j, lambda: streams(0) if mhc and j == 2 else None)
                            elif mhc and j == 2:
                                streams(0)
                            if mhc and j == 2:
                                streams(1)
                            if mhc and 5 <= j < 5 + CB:
                                branch_transpose(c, j - 5)
                            if mlp:
                                up(m, j, first, lambda: streams(2) if mhc and j == 2 else None)
                            elif mhc and j == 2:
                                streams(2)
                            if mhc and j == 2:
                                streams(3)
                            if mhc and 5 <= j < 5 + CB:
                                branch(c, j - 5)
                            if mlp and j > 0:
                                down(m, j - 1)
                        if mlp:
                            down(m, NJ - 1)

                    body(0, True, False, 0, True)
                    with pe.Fori(1, NB) as m:
                        body(m, True, True, m - 1, False)
                    body(0, False, True, NB - 1, False)


def kernel(**inputs):
    import numpy as _np
    import concourse.bacc as _bacc
    from concourse import mybir as _mybir
    from concourse.bass_utils import run_bass_kernel_spmd as _run

    i = {k: _np.asarray(a) for k, a in inputs.items()}

    def by_chunk(w):
        return w.reshape(-1, P, w.shape[1]).transpose(1, 0, 2)

    w_in = i["L0_attn_w_in"].T
    z, xb, dt = w_in[:, :D], w_in[:, D:D + 6 * P], w_in[:, D + 6 * P:]

    def by_hidden(w):
        return w.reshape(NJ, P, KD, P).transpose(3, 0, 2, 1).reshape(P, NJ, KD * P)

    feeds = {
        "x": i["L0_attn_hidden_states"].reshape(TOK, D),
        "w_in": by_chunk(_np.concatenate([xb, z], axis=1)),
        "w_dt": by_chunk(dt),
        "conv_w": i["L0_attn_conv_w"].reshape(NXBC, P, TAPS).transpose(1, 0, 2),
        "conv_b": i["L0_attn_conv_b"].reshape(NXBC, P).T,
        "w_out": by_chunk(i["L0_attn_w_out"].T),
        "gate_w": by_hidden(i["L0_attn_gate_w"]),
        "up_w": by_hidden(i["L0_attn_up_w"]),
        "down_w": by_chunk(i["L0_attn_down_w"].T),
        "ln_w": _np.concatenate([i["L0_attn_ln1_w"].reshape(KD, P).T, i["L0_attn_ln2_w"].reshape(KD, P).T], axis=1),
        "rows": _np.concatenate([i["L0_attn_A_log"], i["L0_attn_dt_bias"], i["L0_attn_dt_bias"], i["L0_attn_D"],
                                 i["L0_ffn_gate"], i["L0_ffn_H_res_base"].reshape(-1), i["L0_ffn_H_pre_base"],
                                 i["L0_ffn_H_post_base"]]).reshape(1, -1),
        "w_logit": by_chunk(_np.concatenate([i["L0_ffn_W_res"], i["L0_ffn_W_pre"], i["L0_ffn_W_post"]]).T),
        "w_branch": i["L0_ffn_W_branch"],
    }
    nc = _bacc.Bacc("TRN2", target_bir_lowering=False, num_devices=1)
    arrays, args = {}, []
    for name, a in feeds.items():
        a = _np.ascontiguousarray(a)
        arrays[f"in_{name}"] = a
        args.append(nc.dram_tensor(f"in_{name}", a.shape, _mybir.dt.from_np(a.dtype), kind="ExternalInput").ap())
    args.append(nc.dram_tensor("out_0", (TOK, D), F32, kind="ExternalOutput").ap())
    mamba_mlp_mhc(nc, *args)
    r = _run(nc, [arrays], core_ids=[0])
    return r.results[0]["out_0"].reshape(BATCHES, TOK // BATCHES, D)
```
